# Optimizing a Trainium2 kernel written in Bass

```python
import numpy as np
import jax
import jax.numpy as jnp

def _softmax(x, axis=-1):
    return jax.nn.softmax(x, axis=axis)

def _gelu(x):
    return jax.nn.gelu(x, approximate=True)

def _silu(x):
    return jax.nn.silu(x)

def _sigmoid(x):
    return jax.nn.sigmoid(x)

def _layernorm(x, axis=-1, eps=1e-05):
    m = jnp.mean(x, axis=axis, keepdims=True)
    v = jnp.var(x, axis=axis, keepdims=True)
    return (x - m) / jnp.sqrt(v + eps)

def _scatter_add(tgt, idx, src, axis=0):
    return tgt.at[idx].add(src)

def _segment_sum(src, seg, n):
    return jax.ops.segment_sum(src, seg, n)
kernel_name = 'mk_flamingo_gated_d2_seqx_r8_ea58e5'

def setup_inputs(seed: int=0):
    np.random.seed(seed)
    _w = jnp.asarray

    def _rec_inputs():
        import jax
        import jax.numpy as jnp
        _rk = jax.random.key(seed)
        x = 7.22e-05 + 1 * jax.random.normal(jax.random.fold_in(_rk, 1), (64, 64, 256), jnp.float32)
        _lenS = 64 - jax.random.randint(jax.random.fold_in(_rk, 7), (64,), 0, max(1, 64 // 4) + 1, jnp.int32)
        _lenS2 = 64 - jax.random.randint(jax.random.fold_in(_rk, 8), (64,), 0, max(1, 64 // 4) + 1, jnp.int32)
        _ctx_2048P = jax.random.normal(jax.random.fold_in(_rk, 11), (64, 16, 256), jnp.float32)
        _ctx_2048c = jax.random.dirichlet(jax.random.fold_in(_rk, 511), 0.3 * jnp.ones((16,), jnp.float32), (64, 64))
        _ctx_2048t = jnp.einsum('bsk,bkd->bsd', _ctx_2048c, _ctx_2048P)
        _ctx_2048t = _ctx_2048t * jax.lax.rsqrt(jnp.mean(jnp.square(_ctx_2048t)) + 1e-12) * 0.953939
        ctx_2048 = 4.13588e-05 + 0.999923 * (_ctx_2048t + 0.3 * jax.random.normal(jax.random.fold_in(_rk, 611), (64, 64, 256), jnp.float32))
        _g = jax.random.normal(jax.random.fold_in(_rk, 9001), (2, 2), jnp.float32)
        _g = jnp.sign(_g) * jnp.maximum(jnp.abs(_g), 1.0) + (_g == 0) * 1.0
        g_xattn = _g[0]
        g_ffn = _g[1]
        return (x, ctx_2048, g_xattn, g_ffn)
    x, ctx_2048, g_xattn, g_ffn = _rec_inputs()

    def _L0_xattn_setup():
        import jax, jax.numpy as jnp
        import numpy as np
        N_HEAD = 8
        key = jax.random.key(seed)
        k1, k2, k3 = jax.random.split(key, 3)
        B, D, L = (4, 128, 256)
        q = jax.random.normal(k1, (B, D, L), dtype=jnp.float32)
        k = jax.random.normal(k2, (B, D, L), dtype=jnp.float32)
        v = jax.random.normal(k3, (B, D, L), dtype=jnp.float32)
        gamma = jnp.ones((), dtype=jnp.float32)
        return {'q': q, 'k': k, 'v': v, 'gamma': gamma}
    _L0_xattn_all = _L0_xattn_setup()
    _L0_xattn_in = {k: v for k, v in _L0_xattn_all.items() if k in ('gamma',)}
    del _L0_xattn_all

    def _L0_ffn_setup():
        import jax, jax.numpy as jnp
        import numpy as np
        EPS_NORM = 1e-12
        EPS_Q = 1e-05

        def simple_rmsnorm(x):
            d = x.shape[-1]
            n = jnp.maximum(jnp.linalg.norm(x, axis=-1, keepdims=True), EPS_NORM)
            return x / n * jnp.sqrt(jnp.asarray(d, x.dtype))

        def activation_quant(x):
            scale = 127.0 / jnp.clip(jnp.max(jnp.abs(x), axis=-1, keepdims=True), EPS_Q, None)
            return jnp.clip(jnp.round(x * scale), -128.0, 127.0) / scale

        def weight_quant(w):
            scale = 1.0 / jnp.clip(jnp.mean(jnp.abs(w)), EPS_Q, None)
            return jnp.clip(jnp.round(w * scale), -1.0, 1.0) / scale

        def bitlinear158(x, w):
            xn = simple_rmsnorm(x)
            xq = xn + jax.lax.stop_gradient(activation_quant(xn) - xn)
            wq = w + jax.lax.stop_gradient(weight_quant(w) - w)
            return jnp.einsum('bsd,od->bso', xq, wq)
        key = jax.random.key(seed)
        k1, k2, k3 = jax.random.split(key, 3)
        dim, inner = (256, 1024)
        x = jax.random.normal(k1, (4, 256, dim), dtype=jnp.float32)
        w1 = jax.random.normal(k2, (inner, dim), dtype=jnp.float32) * 0.02
        w2 = jax.random.normal(k3, (dim, inner), dtype=jnp.float32) * 0.02
        return {'x': x, 'w1': w1, 'w2': w2}
    _L0_ffn_all = _L0_ffn_setup()
    _L0_ffn_in = {k: v for k, v in _L0_ffn_all.items() if k in ('w1', 'w2')}
    del _L0_ffn_all

    def _L1_xattn_setup():
        import jax, jax.numpy as jnp
        import numpy as np
        from jax import lax
        LN_EPS = 1e-05
        key = jax.random.key(seed)
        ks = jax.random.split(key, 8)
        B, S, T, D = (4, 128, 256, 256)
        scale = 0.02
        return {'Z': jax.random.normal(ks[0], (B, S, D), dtype=jnp.float32), 'kv': jax.random.normal(ks[1], (B, T, D), dtype=jnp.float32), 'decay': jnp.float32(0.9), 'W_in': jax.random.normal(ks[2], (D, D), dtype=jnp.float32) * scale, 'b_in': jnp.zeros((D,), dtype=jnp.float32), 'W_out': jax.random.normal(ks[3], (D, D), dtype=jnp.float32) * scale, 'b_out': jnp.zeros((D,), dtype=jnp.float32), 'gamma': jnp.ones((D,), dtype=jnp.float32), 'beta': jnp.zeros((D,), dtype=jnp.float32)}
    _L1_xattn_all = _L1_xattn_setup()
    _L1_xattn_in = {k: v for k, v in _L1_xattn_all.items() if k in ('decay', 'W_in', 'b_in', 'W_out', 'b_out', 'gamma', 'beta')}
    del _L1_xattn_all

    def _L1_ffn_setup():
        import jax, jax.numpy as jnp
        import numpy as np
        B, S, H, F, E, R, K = (2, 128, 256, 896, 8, 32, 2)

        def _gather_slot(a_all, e):
            return jnp.take_along_axis(a_all, e[:, None, None], axis=1)[:, 0]
        key = jax.random.key(seed)
        ks = jax.random.split(key, 12)
        sc = 0.02
        n = lambda k, shape, s: jax.random.normal(k, shape, dtype=jnp.float32) * s
        return {'hidden_states': n(ks[0], (B, S, H), 1.0), 'Wg': n(ks[1], (E, H), sc), 'W1': n(ks[2], (F, H), sc), 'W2': n(ks[3], (H, F), sc), 'W3': n(ks[4], (F, H), sc), 'A1': n(ks[5], (E, R, H), sc), 'B1': n(ks[6], (E, F, R), sc), 'A2': n(ks[7], (E, R, F), sc), 'B2': n(ks[8], (E, H, R), sc), 'A3': n(ks[9], (E, R, H), sc), 'B3': n(ks[10], (E, F, R), sc)}
    _L1_ffn_all = _L1_ffn_setup()
    _L1_ffn_in = {k: v for k, v in _L1_ffn_all.items() if k in ('Wg', 'W1', 'W2', 'W3', 'A1', 'B1', 'A2', 'B2', 'A3', 'B3')}
    del _L1_ffn_all
    return {'x': x, 'ctx_2048': ctx_2048, 'g_xattn': g_xattn, 'g_ffn': g_ffn, 'L0_xattn_gamma': _L0_xattn_in['gamma'], 'L0_ffn_w1': _L0_ffn_in['w1'], 'L0_ffn_w2': _L0_ffn_in['w2'], 'L1_xattn_decay': _L1_xattn_in['decay'], 'L1_xattn_W_in': _L1_xattn_in['W_in'], 'L1_xattn_b_in': _L1_xattn_in['b_in'], 'L1_xattn_W_out': _L1_xattn_in['W_out'], 'L1_xattn_b_out': _L1_xattn_in['b_out'], 'L1_xattn_gamma': _L1_xattn_in['gamma'], 'L1_xattn_beta': _L1_xattn_in['beta'], 'L1_ffn_Wg': _L1_ffn_in['Wg'], 'L1_ffn_W1': _L1_ffn_in['W1'], 'L1_ffn_W2': _L1_ffn_in['W2'], 'L1_ffn_W3': _L1_ffn_in['W3'], 'L1_ffn_A1': _L1_ffn_in['A1'], 'L1_ffn_B1': _L1_ffn_in['B1'], 'L1_ffn_A2': _L1_ffn_in['A2'], 'L1_ffn_B2': _L1_ffn_in['B2'], 'L1_ffn_A3': _L1_ffn_in['A3'], 'L1_ffn_B3': _L1_ffn_in['B3']}

def reference(x, ctx_2048, g_xattn, g_ffn, L0_xattn_gamma, L0_ffn_w1, L0_ffn_w2, L1_xattn_decay, L1_xattn_W_in, L1_xattn_b_in, L1_xattn_W_out, L1_xattn_b_out, L1_xattn_gamma, L1_xattn_beta, L1_ffn_Wg, L1_ffn_W1, L1_ffn_W2, L1_ffn_W3, L1_ffn_A1, L1_ffn_B1, L1_ffn_A2, L1_ffn_B2, L1_ffn_A3, L1_ffn_B3):
    import jax
    import jax.numpy as jnp

    def _L0_xattn_ref(q, k, v, gamma):
        import jax, jax.numpy as jnp
        import numpy as np
        N_HEAD = 8
        B, Dq, Lq = q.shape
        Dv, Lk = (v.shape[-2], v.shape[-1])
        h = N_HEAD
        dq = Dq // h
        dv = Dv // h
        qh = q.reshape(B, h, dq, Lq)
        kh = k.reshape(B, h, dq, Lk)
        vh = v.reshape(B, h, dv, Lk)
        scale = 1.0 / jnp.sqrt(jnp.asarray(dq, dtype=q.dtype))
        qk = jnp.einsum('bhdq,bhdl->bhql', qh, kh) * scale
        sm = jax.nn.softmax(qk, axis=-1)
        ret = jnp.einsum('bhql,bhdl->bhdq', sm, vh)
        ret = ret.reshape(B, Dv, Lq)
        return gamma * ret

    def _L0_ffn_ref(x, w1, w2):
        import jax, jax.numpy as jnp
        import numpy as np
        EPS_NORM = 1e-12
        EPS_Q = 1e-05

        def simple_rmsnorm(x):
            d = x.shape[-1]
            n = jnp.maximum(jnp.linalg.norm(x, axis=-1, keepdims=True), EPS_NORM)
            return x / n * jnp.sqrt(jnp.asarray(d, x.dtype))

        def activation_quant(x):
            scale = 127.0 / jnp.clip(jnp.max(jnp.abs(x), axis=-1, keepdims=True), EPS_Q, None)
            return jnp.clip(jnp.round(x * scale), -128.0, 127.0) / scale

        def weight_quant(w):
            scale = 1.0 / jnp.clip(jnp.mean(jnp.abs(w)), EPS_Q, None)
            return jnp.clip(jnp.round(w * scale), -1.0, 1.0) / scale

        def bitlinear158(x, w):
            xn = simple_rmsnorm(x)
            xq = xn + jax.lax.stop_gradient(activation_quant(xn) - xn)
            wq = w + jax.lax.stop_gradient(weight_quant(w) - w)
            return jnp.einsum('bsd,od->bso', xq, wq)
        h = bitlinear158(x, w1)
        h = jax.nn.gelu(h, approximate=False)
        return bitlinear158(h, w2)

    def _L1_xattn_ref(Z, kv, decay, W_in, b_in, W_out, b_out, gamma, beta):
        import jax, jax.numpy as jnp
        import numpy as np
        from jax import lax
        LN_EPS = 1e-05
        B, T, D = kv.shape
        K = jax.nn.sigmoid(decay)
        x = jnp.einsum('btd,ed->bte', kv, W_in) + b_in

        def scan_fn(s, xt):
            s = K * s + xt
            return (s, s)
        s0 = jnp.zeros((B, D), dtype=kv.dtype)
        _, states = lax.scan(scan_fn, s0, jnp.swapaxes(x, 0, 1))
        states = jnp.swapaxes(states, 0, 1)
        proj = jnp.einsum('btd,ed->bte', states, W_out) + b_out
        summary = jnp.mean(proj, axis=1, keepdims=True)
        y = Z + summary
        mu = jnp.mean(y, axis=-1, keepdims=True)
        var = jnp.mean((y - mu) ** 2, axis=-1, keepdims=True)
        return (y - mu) / jnp.sqrt(var + LN_EPS) * gamma + beta

    def _L1_ffn_ref(hidden_states, Wg, W1, W2, W3, A1, B1, A2, B2, A3, B3):
        import jax, jax.numpy as jnp
        import numpy as np
        B, S, H, F, E, R, K = (2, 128, 256, 896, 8, 32, 2)

        def _gather_slot(a_all, e):
            return jnp.take_along_axis(a_all, e[:, None, None], axis=1)[:, 0]
        b, s, h = hidden_states.shape
        x = hidden_states.reshape(-1, h)
        nE = Wg.shape[0]
        logits = x @ Wg.T
        probs = jax.nn.softmax(logits.astype(jnp.float32), axis=-1)
        rw, sel = jax.lax.top_k(probs, K)
        rw = (rw / rw.sum(axis=-1, keepdims=True)).astype(x.dtype)
        base1 = x @ W1.T
        base3 = x @ W3.T
        a1_all = jnp.einsum('th,erh->ter', x, A1)
        a3_all = jnp.einsum('th,erh->ter', x, A3)
        out = jnp.zeros_like(x)
        for k in range(K):
            e = sel[:, k]
            mask = jax.nn.one_hot(e, nE, dtype=x.dtype)
            a1 = _gather_slot(a1_all, e)
            a3 = _gather_slot(a3_all, e)
            lora1 = jnp.einsum('ter,efr->tf', mask[:, :, None] * a1[:, None, :], B1)
            lora3 = jnp.einsum('ter,efr->tf', mask[:, :, None] * a3[:, None, :], B3)
            x1 = base1 + lora1
            x3 = base3 + lora3
            x2 = jax.nn.silu(x1) * x3
            down = x2 @ W2.T
            a2_all = jnp.einsum('tf,erf->ter', x2, A2)
            a2 = _gather_slot(a2_all, e)
            lora2 = jnp.einsum('ter,ehr->th', mask[:, :, None] * a2[:, None, :], B2)
            out = out + (down + lora2) * rw[:, k:k + 1]
        return out.reshape(b, s, h)
    x = x + jnp.tanh(g_xattn[0]) * _L0_xattn_ref(_layernorm(x, axis=-1), ctx_2048, ctx_2048, L0_xattn_gamma)
    x = x + jnp.tanh(g_ffn[0]) * _L0_ffn_ref(_layernorm(x, axis=-1), L0_ffn_w1, L0_ffn_w2)
    x = x + jnp.tanh(g_xattn[1]) * _L1_xattn_ref(_layernorm(x, axis=-1), ctx_2048, L1_xattn_decay, L1_xattn_W_in, L1_xattn_b_in, L1_xattn_W_out, L1_xattn_b_out, L1_xattn_gamma, L1_xattn_beta)
    x = x + jnp.tanh(g_ffn[1]) * _L1_ffn_ref(_layernorm(x, axis=-1), L1_ffn_Wg, L1_ffn_W1, L1_ffn_W2, L1_ffn_W3, L1_ffn_A1, L1_ffn_B1, L1_ffn_A2, L1_ffn_B2, L1_ffn_A3, L1_ffn_B3)
    return x

_drawn_inputs = setup_inputs


def setup_inputs(seed=0):
    import zlib

    import numpy as np

    out = dict(_drawn_inputs(seed))
    spreads = {'g_ffn': (-1.0, 0.6),
     'L1_xattn_b_in': (0.0, 0.1),
     'L1_xattn_b_out': (0.0, 0.1),
     'L1_xattn_gamma': (1.0, 0.2),
     'L1_xattn_beta': (0.0, 0.1)}
    factors = {'L1_ffn_Wg': 8.0,
     'L1_ffn_A1': 8.0,
     'L1_ffn_B1': 8.0,
     'L1_ffn_A2': 8.0,
     'L1_ffn_B2': 8.0,
     'L1_ffn_A3': 8.0,
     'L1_ffn_B3': 8.0}
    for name, (base, spread) in spreads.items():
        noise = np.random.default_rng([zlib.crc32(name.encode()), seed]).standard_normal(out[name].shape)
        drawn = base * np.exp(spread * noise) if base else spread * noise
        out[name] = jnp.asarray(drawn.astype(out[name].dtype))
    for name, factor in factors.items():
        out[name] = (out[name] * factor).astype(out[name].dtype)
    return out
```

```python
from contextlib import ExitStack

import concourse.bass as bass
from concourse import mybir

ALU = mybir.AluOpType
ACT = mybir.ActivationFunctionType
AX = mybir.AxisListType
BF16 = mybir.dt.bfloat16
F32 = mybir.dt.float32
U32 = mybir.dt.uint32

P = 128
NB, S, D = 64, 64, 256
TILES = NB * S // P
HEADS, DH = 8, 8
HALVES = 2 * TILES
F1 = 1024
F, E, R = 896, 8, 32
FT = F // P
ER = E * R
ROUND = 1.5 * 2.0**23
EPS = 1e-5


class Sems:

    def __init__(self, nc, ctx, prefix):
        self.nc, self.ctx, self.prefix, self.made = nc, ctx, prefix, {}

    def __call__(self, name):
        if name not in self.made:
            self.made[name] = self.ctx.enter_context(self.nc.semaphore(f"{self.prefix}_{name}"))
        return self.made[name]


def at_least(eng, sem, value, passed=None):
    if not isinstance(value, int) or value > 0:
        eng.wait_ge(sem, value)
        if passed is not None and not isinstance(value, int):
            eng.sem_inc(passed, 1)


def prepare(nc, t, sb_out):
    with ExitStack() as ctx:
        sem = Sems(nc, ctx, "prep")

        def sb(name, shape, dt=F32):
            return ctx.enter_context(nc.sbuf_tensor(name, shape, dt))

        nat = {n: sb(f"nat_{n}", [P, FT, D]) for n in ("W1", "W3", "B1", "B3")}
        nat |= {n: sb(f"nat_{n}", [P, 2, D]) for n in ("A1", "A3", "B2", "Win", "Wout")}
        nat |= {n: sb(f"nat_{n}", [P, 2, F]) for n in ("W2", "A2")}
        nat["w1"] = sb("nat_w1", [P, 8, D])
        nat["w2"] = sb("nat_w2", [P, 2, F1])
        nat_Wg = sb("nat_Wg", [E, D])
        tern = sb("tern", [P, 8 * D], BF16)
        tern1 = tern[:, :].rearrange("p (a b) -> p a b", b=D)
        tern2 = tern[:, :].rearrange("p (a b) -> p a b", b=F1)
        ones = sb("ones", [P, P])
        part = sb("part", [P, 8])
        powers = sb("powers", [P, 2, S])
        decays = sb("decays", [P, S])
        unit = sb("unit", [P, 2, S])
        wide = sb("wide", [P, 126])
        kvs = sb("kvs", [NB, D])
        kvsT = sb("kvsT", [P, 2, NB])
        uT = sb("uT", [P, 2, NB])
        bcol = sb("bcol", [P, 2])
        brow = sb("brow", [1, D])
        summ = sb("summ", [NB, D])
        tmp = sb("tmp", [P, 16])

        def psum(name, shape, dt=F32):
            return ctx.enter_context(nc.psum_tensor(name, shape, dt))

        turn = psum("turn", [P, 4, 512])
        turnb = psum("turnb", [P, 2, 1024], BF16)
        small = psum("small", [P, 512])
        acc = psum("acc", [P, 512])
        ident, identb = t["ident"], t["identb"]

        groups = []
        for n in ("W1", "W3", "B1", "B3"):
            hi, lo = t[n + "_hi"], t[n + "_lo"]
            for k in range(2):
                for f0, f1 in ((0, 4), (4, 7)):
                    groups.append((n, [nat[n][:, f, k * P:(k + 1) * P] for f in range(f0, f1)],
                                   hi[:, k, f0 * P:f1 * P], lo[:, k, f0 * P:f1 * P]))
        for n in ("A1", "A3", "B2"):
            groups.append((n, [nat[n][:, m, k * P:(k + 1) * P] for k in range(2) for m in range(2)],
                           t[n + "_hi"][:, :, :].rearrange("p a b -> p (a b)"),
                           t[n + "_lo"][:, :, :].rearrange("p a b -> p (a b)")))
        for n in ("W2", "A2"):
            for f0, f1 in ((0, 2), (2, 4), (4, 6), (6, 7)):
                groups.append((n, [nat[n][:, m, f * P:(f + 1) * P] for f in range(f0, f1) for m in range(2)],
                               t[n + "_hi"][:, f0:f1, :].rearrange("p a b -> p (a b)"),
                               t[n + "_lo"][:, f0:f1, :].rearrange("p a b -> p (a b)")))
        for n in ("Win", "Wout"):
            groups.append((n, [nat[n][:, m, k * P:(k + 1) * P] for k in range(2) for m in range(2)],
                           sb_out[n][:, :, :].rearrange("p a b -> p (a b)"), None))
        NG = len(groups)

        block = ctx.enter_context(nc.Block())

        @block.sync
        def _(sp):
            def load(dst, src, name):
                sp.dma_start(dst, src).then_inc(sem("in_" + name), 16)

            load(t["ctx"][:, :, :], t["ctx_dram"], "ctx")
            load(t["g"][:, 0:2], t["g_xattn_dram"], "gains")
            load(t["g"][:, 2:4], t["g_ffn_dram"], "gains")
            load(t["g"][:, 4:5], t["gamma0_dram"], "gains")
            load(t["g"][:, 5:6], t["decay_dram"], "gains")
            load(nat["w1"][:, :, :], t["w1_dram"], "w1")
            load(nat["w2"][:, :, :], t["w2_dram"], "w2")
            for n in ("W1", "W3", "W2", "A1", "A3", "A2", "Win", "Wout"):
                load(nat[n][:, :, :], t[n + "_dram"], n)
            for n in ("B1", "B3"):
                for f in range(FT):
                    load(nat[n][:, f, :].rearrange("p (e r) -> p e r", e=E), t[n + "_dram"][f], n)
            for m in range(2):
                load(nat["B2"][:, m, :].rearrange("p (e r) -> p e r", e=E), t["B2_dram"][m], "B2")
            sp.dma_start(bcol[:, :], t["b_in_dram"], allow_slow_non_contiguous=True).then_inc(sem("in_rest"), 16)
            load(brow[:, :], t["b_out_dram"], "rest")
            load(nat_Wg[:, :], t["Wg_dram"], "rest")
            load(t["gamma"][:, :], t["gamma_dram"], "rest")
            load(t["beta"][:, :], t["beta_dram"], "rest")
            sp.wait_ge(sem("summ"), 1)
            sp.dma_start(t["summ_dram"], summ[:, :]).then_inc(sem("summ_out"), 16)
            sp.wait_ge(sem("summ_out"), 16)
            sp.wait_ge(sem("in_rest"), 80)

        @block.gpsimd
        def _(pool):
            nc.gpsimd.memset(ones[:, :], 1.0).then_inc(sem("ones"), 1)
            nc.gpsimd.memset(unit[:, :, :], 1.0).then_inc(sem("pm"), 1)
            nc.gpsimd.memset(wide[:, :], 0.0).then_inc(sem("wide0"), 1)
            pool.wait_ge(sem("ones"), 1)
            nc.gpsimd.affine_select(out=ident[:, :], in_=ones[:, :], compare_op=ALU.is_equal, fill=0.0,
                                    base=0, pattern=[[-1, P]], channel_multiplier=1).then_inc(sem("ident"), 1)
            pool.wait_ge(sem("ident"), 1)
            nc.gpsimd.tensor_copy(identb[:, :], ident[:, :]).then_inc(sem("ident"), 1)
            pool.wait_ge(sem("pm"), 1)
            nc.gpsimd.affine_select(out=powers[:, :, :], in_=unit[:, :, :], compare_op=ALU.is_equal, fill=0.0,
                                    base=-(S - 1), pattern=[[-S, 2], [1, S]],
                                    channel_multiplier=1).then_inc(sem("pm"), 1)

        @block.scalar
        def _(act):
            act.wait_ge(sem("in_gains"), 64)
            nc.scalar.activation(t["tanh"][:, 0:4], t["g"][:, 0:4], ACT.Tanh).then_inc(sem("tanh"), 1)
            nc.scalar.activation(tmp[:, 0:1], t["g"][:, 5:6], ACT.Exp, scale=-1.0).then_inc(sem("expd"), 1)
            for i, (n, tiles, hi, lo) in enumerate(groups):
                act.wait_ge(sem("turned"), i + 1)
                nc.scalar.copy(hi, turn[:, i % 4, 0:len(tiles) * P]).then_inc(sem("hi"), 1)

        @block.vector
        def _(dve):
            count = [0]

            def link(ins):
                count[0] += 1
                ins.then_inc(sem("dve"), 1)
                dve.wait_ge(sem("dve"), count[0])

            dve.wait_ge(sem("tanh"), 1)
            nc.vector.tensor_tensor(t["gain0"][:, :], t["tanh"][:, 0:1], t["g"][:, 4:5], ALU.mult).then_inc(sem("gain0"), 1)
            dve.wait_ge(sem("expd"), 1)
            link(nc.vector.tensor_scalar(tmp[:, 1:2], tmp[:, 0:1], 1.0, None, ALU.add))
            link(nc.vector.reciprocal(tmp[:, 2:3], tmp[:, 1:2]))
            dve.wait_ge(sem("pm"), 2)
            link(nc.vector.tensor_scalar(decays[:, :], unit[:, 0, :], tmp[:, 2:3], None, ALU.mult))
            link(nc.vector.tensor_tensor_scan(decays[:, :], decays[:, :], unit[:, 0, :], 0.0, ALU.mult, ALU.add))
            link(nc.vector.tensor_reduce(tmp[:, 3:4], decays[:, :], AX.X, ALU.add))
            link(nc.vector.tensor_scalar(tmp[:, 4:5], tmp[:, 3:4], 1.0 / S, None, ALU.mult))
            for b in range(2):
                link(nc.vector.tensor_tensor(powers[:, b, :], powers[:, b, :], decays[:, :], ALU.mult))
            link(nc.vector.tensor_reduce(tmp[:, 5:7], powers[:, :, :], AX.X, ALU.add))
            dve.wait_ge(sem("wide0"), 1)
            nc.vector.tensor_scalar(wide[:, 62:64], tmp[:, 5:7], 1.0 / S, None, ALU.mult).then_inc(sem("wide"), 1)
            for j, (n, dst, out) in enumerate((("w1", t["mean1"], tern1), ("w2", t["mean2"], tern2))):
                dve.wait_ge(sem("in_" + n), 16)
                link(nc.vector.tensor_reduce(part[:, j:j + 1], nat[n][:, :, :], AX.XY, ALU.add,
                                             apply_absolute_value=True))
                count[0] += 1
                nc.vector.tensor_copy(part[:, 2 + j:3 + j], part[:, j:j + 1]).then_inc(sem("dve"), 1)
                dve.wait_ge(sem("dve"), count[0])
                nc.vector.tensor_copy(part[:, 4 + j:5 + j], part[:, j:j + 1]).then_inc(sem("wsum"), 1)
                dve.wait_ge(sem("total"), j + 1)
                link(nc.vector.tensor_scalar(dst[:, :], small[:, j:j + 1], 1.0 / (F1 * D), EPS, ALU.mult, ALU.max))
                link(nc.vector.reciprocal(tmp[:, 8 + j:9 + j], dst[:, :]))
                link(nc.vector.tensor_scalar(nat[n][:, :, :], nat[n][:, :, :], tmp[:, 8 + j:9 + j], ROUND, ALU.mult, ALU.add))
                link(nc.vector.tensor_scalar(nat[n][:, :, :], nat[n][:, :, :], -ROUND, 1.0, ALU.add, ALU.min))
                if j == 1:
                    dve.wait_ge(sem("turnedb"), 2)
                nc.vector.tensor_scalar(out[:, :, :], nat[n][:, :, :], -1.0, None, ALU.max).then_inc(sem("tern"), 1)
            for i in range(4):
                dve.wait_ge(sem("turnedb"), i + 1)
                dst = t["w1T"] if i < 2 else t["w2T"]
                flat = dst[:, :, :].rearrange("p a b -> p (a b)")[:, (i % 2) * 1024:(i % 2 + 1) * 1024]
                nc.vector.tensor_copy(flat, turnb[:, i % 2, :]).then_inc(sem("ternT"), 1)
            for i, (n, tiles, hi, lo) in enumerate(groups):
                dve.wait_ge(sem("hi"), i + 1)
                if lo is not None:
                    nc.vector.tensor_tensor(lo, turn[:, i % 4, 0:len(tiles) * P], hi, ALU.subtract).then_inc(sem("lo"), 1)
                else:
                    nc.vector.tensor_copy(tmp[:, 10:11], tmp[:, 8:9]).then_inc(sem("lo"), 1)
                    dve.wait_ge(sem("lo"), i + 1)
            dve.wait_ge(sem("WgT"), 1)
            nc.vector.tensor_copy(t["WgT"][:, :, :], small[:, 400:416].rearrange("p (a b) -> p a b", a=2)).then_inc(sem("WgT_sb"), 1)
            dve.wait_ge(sem("kvs"), 1)
            nc.vector.tensor_copy(kvs[:, :], acc[0:NB, 0:D]).then_inc(sem("kvs_sb"), 1)
            dve.wait_ge(sem("kvsT"), 1)
            nc.vector.tensor_copy(kvsT[:, :, :], small[:, 128:256].rearrange("p (a b) -> p a b", a=2)).then_inc(sem("kvsT_sb"), 1)
            dve.wait_ge(sem("in_rest"), 80)
            link(nc.vector.tensor_scalar(bcol[:, :], bcol[:, :], tmp[:, 4:5], None, ALU.mult))
            dve.wait_ge(sem("u"), 1)
            for m in range(2):
                nc.vector.tensor_scalar(uT[:, m, :], small[:, 256 + 64 * m:320 + 64 * m], bcol[:, m:m + 1], None,
                                        ALU.add).then_inc(sem("u_sb"), 1)
            dve.wait_ge(sem("s"), 1)
            nc.vector.tensor_copy(summ[:, :], acc[0:NB, D:2 * D]).then_inc(sem("summ"), 1)

        @block.tensor
        def _(pe):
            pe.wait_ge(sem("ident"), 2)
            pe.wait_ge(sem("wide"), 1)
            pe.wait_ge(sem("in_ctx"), 16)
            for i in range(TILES):
                last = nc.tensor.matmul(acc[0:NB, 0:D], wide[:, 62 - 2 * i:126 - 2 * i], t["ctx"][:, i, :],
                                        start=(i == 0), stop=(i == TILES - 1))
            last.then_inc(sem("kvs"), 1)
            for j in range(2):
                pe.wait_ge(sem("wsum"), j + 1)
                nc.tensor.matmul(small[:, j:j + 1], ones[:, :], part[:, 4 + j:5 + j], start=True, stop=True
                                 ).then_inc(sem("total"), 1)
            for i in range(4):
                pe.wait_ge(sem("tern"), 1 + i // 2)
                if i >= 2:
                    pe.wait_ge(sem("ternT"), i - 1)
                for c in range(8):
                    if i < 2:
                        src = tern1[:, c, i * P:(i + 1) * P]
                    else:
                        f, m = divmod(8 * (i - 2) + c, 2)
                        src = tern2[:, m, f * P:(f + 1) * P]
                    last = nc.tensor.transpose(turnb[:, i % 2, c * P:(c + 1) * P], src, identb[:, :])
                last.then_inc(sem("turnedb"), 1)
            for i, (n, tiles, hi, lo) in enumerate(groups):
                pe.wait_ge(sem("in_" + n), {"B1": 16 * FT, "B3": 16 * FT, "B2": 32}.get(n, 16))
                if i >= 4:
                    pe.wait_ge(sem("lo"), i - 3)
                for c, src in enumerate(tiles):
                    last = nc.tensor.transpose(turn[:, i % 4, c * P:(c + 1) * P], src, ident[:, :])
                last.then_inc(sem("turned"), 1)
            pe.wait_ge(sem("in_rest"), 80)
            for m in range(2):
                last = nc.tensor.transpose(small[:, 400 + 8 * m:408 + 8 * m], nat_Wg[:, m * P:(m + 1) * P], ident[0:E, 0:E])
            last.then_inc(sem("WgT"), 1)
            pe.wait_ge(sem("kvs_sb"), 1)
            for m in range(2):
                last = nc.tensor.transpose(small[:, 128 + 64 * m:192 + 64 * m], kvs[:, m * P:(m + 1) * P], ident[0:NB, 0:NB])
            last.then_inc(sem("kvsT"), 1)
            pe.wait_ge(sem("kvsT_sb"), 1)
            pe.wait_ge(sem("hi"), NG)
            for m in range(2):
                for k in range(2):
                    last = nc.tensor.matmul(small[:, 256 + 64 * m:320 + 64 * m], sb_out["Win"][:, k, m * P:(m + 1) * P],
                                            kvsT[:, k, :], start=(k == 0), stop=(k == 1))
            last.then_inc(sem("u"), 1)
            pe.wait_ge(sem("u_sb"), 2)
            for k in range(2):
                nc.tensor.matmul(acc[0:NB, D:2 * D], uT[:, k, :], sb_out["Wout"][:, k, :], start=(k == 0), stop=False)
            nc.tensor.matmul(acc[0:NB, D:2 * D], ones[0:1, 0:NB], brow[:, :], start=False, stop=True).then_inc(sem("s"), 1)


class Step:

    def __init__(self, i, s):
        self.i, self.s = i, s
        self.static = isinstance(i, int)

    def half(self, k=0):
        return self.i * 4 + (self.s + k)

    def quarter(self, k=0):
        return self.i + (self.s + k) // 4

    def tile(self, k=0):
        return self.i * 2 + (self.s + k) // 2

    def slot(self, k=0, m=4):
        return (self.s + k) % m

    def in_range(self, k, n=HALVES):
        return not self.static or 0 <= 4 * self.i + self.s + k < n


def attention(nc, t):
    with ExitStack() as ctx:
        sem = Sems(nc, ctx, "att")

        def sb(name, shape, dt=F32):
            return ctx.enter_context(nc.sbuf_tensor(name, shape, dt))

        def psum(name, shape, dt=F32):
            return ctx.enter_context(nc.psum_tensor(name, shape, dt))

        q_pack = sb("q_pack", [P, 4, HEADS, D], BF16)
        k_pack = sb("k_pack", [P, 4, HEADS, D], BF16)
        q_parts = sb("q_parts", [P, 2, 3, D], BF16)
        k_parts = sb("k_parts", [P, 2, 3, D], BF16)
        z = sb("z", [P, 2, D])
        q_rest = sb("q_rest", [P, D])
        k_rest = sb("k_rest", [P, D])
        probs = sb("probs", [P, HEADS, 2, D])
        vT = sb("vT", [P, 2, 2, 2 * HEADS, 32])
        pv_sb = sb("pv_sb", [P, 2, 2, D])
        nd = sb("nd", [P, 2, 2, D])
        stat6 = sb("stat6", [P, 6])
        mean_var = sb("mean_var", [P, 2, 2])
        rstd = sb("rstd", [P, 2, 2])
        half_neg = sb("half_neg", [P, 1])
        neg_max = sb("neg_max", [P, 2, HEADS, 2])
        neg_rest = sb("neg_rest", [P, 2 * HEADS])
        neg_parts = sb("neg_parts", [P, 2, 3, 2 * HEADS], BF16)
        neg_rows = sb("neg_rows", [3 * 2 * HEADS, 2, P], BF16)

        s1 = psum("s1", [P, 4, 512])
        s2 = psum("s2", [P, 2, 512])
        pv = psum("pv", [P, 2, D])
        misc = psum("misc", [P, 512])
        negT = misc[0:48, 256:320].bitcast(BF16)

        xres, ctx_sb, identb = t["x"], t["ctx"], t["identb"]
        q_dram, k_dram, pv_dram = t["q_parts_dram"], t["k_parts_dram"], t["pv_dram"]
        SCALE = float(DH) ** -0.5

        first, last_step = -6, HALVES + 2
        LOOP = (1, (HALVES - 8) // 4)

        def run(eng, step):
            for n in range(first, 4 * LOOP[0]):
                step(Step(n // 4, n % 4))
            with eng.Fori(*LOOP) as i:
                for s in range(4):
                    step(Step(i, s))
            for n in range(4 * LOOP[1], last_step + 1):
                step(Step(n // 4, n % 4))

        block = ctx.enter_context(nc.Block())

        @block.sync
        def _(sp):
            def step(n):
                if n.in_range(1):
                    at_least(sp, sem("neg_rows"), n.half(2), passed=t["passed"])
                    sp.dma_start(q_pack[96:99, n.slot(1), :, :], neg_rows[:, n.slot(1, 2), :]
                                 ).then_inc(sem(f"neg_in{n.slot(1, 2)}"), 16)
                if n.in_range(3):
                    h, slot, u = n.slot(3, 2), n.slot(3), n.slot(3) // 2
                    at_least(sp, sem(f"parts_out{u}"), n.quarter(3) * 128 + 128, passed=t["passed"])
                    at_least(sp, sem("s2_done"), n.half(0) * 8, passed=t["passed"])
                    rows = q_dram[u, :, :, h * 8:h * 8 + 8, :].rearrange("a d h l -> (a d) (h l)")
                    sp.dma_start(q_pack[0:72, slot, :, :].rearrange("p h l -> p (h l)"),
                                 rows.unsqueeze(0).to_broadcast([3, 24, HEADS * D])).then_inc(sem(f"pack_in{slot}"), 16)
                    sp.dma_start(k_pack[0:72, slot, :, :].rearrange("p h l -> p (h l)"),
                                 t["k_windows"](u, h)).then_inc(sem(f"pack_in{slot}"), 16)
                if n.in_range(-1):
                    b, u = n.slot(-1, 2), n.slot(-1) // 2
                    at_least(sp, sem("pv_sb"), n.half(0), passed=t["passed"])
                    if b == 0:
                        at_least(sp, sem(f"nd_in{u}"), n.quarter(-1) * 32, passed=t["passed"])
                    sp.dma_start(pv_dram[u, b].rearrange("g p l -> p g l"), pv_sb[:, b, :, :]
                                 ).then_inc(sem(f"pv_out{b}"), 16)
                if n.s % 2 == 0 and n.in_range(4):
                    u = n.slot(4) // 2
                    at_least(sp, sem("q_parts"), n.tile(4) + 1, passed=t["passed"])
                    at_least(sp, sem("k_parts"), n.tile(4) + 1, passed=t["passed"])
                    for b in range(2):
                        at_least(sp, sem(f"pack_in{2 * u + b}"), n.quarter(4) * 32, passed=t["passed"])
                    for a in range(3):
                        sp.dma_start(q_dram[u, a].rearrange("d h l -> h d l"), q_parts[:, u, a, :]
                                     ).then_inc(sem(f"parts_out{u}"), 16)
                    for a in range(5):
                        sp.dma_start(k_dram[u, a].rearrange("d h l -> h d l"), k_parts[:, u, a % 3, :]
                                     ).then_inc(sem(f"parts_out{u}"), 16)
                if n.s % 2 == 1 and n.in_range(-3):
                    u = n.slot(-3) // 2
                    for b in range(2):
                        at_least(sp, sem(f"pv_out{b}"), n.tile(-3) * 16 + 16, passed=t["passed"])
                    at_least(sp, sem("x_done"), n.tile(-3), passed=t["passed"])
                    for k in range(2):
                        src = pv_dram[u].rearrange("b g (j r) l -> (b g j) r l", r=32)[:, 8 * k:8 * k + 8, :]
                        sp.dma_start(nd[:, u, k, :], src).then_inc(sem(f"nd_in{u}"), 16)

            run(sp, step)

        @block.gpsimd
        def _(pool):
            for tile_ in (q_pack, k_pack):
                nc.gpsimd.memset(tile_[:, :, :, :], 0.0).then_inc(sem("zeroed"), 1)
            nc.gpsimd.memset(vT[:, :, :, :, :], 0.0).then_inc(sem("zeroed"), 1)
            nc.gpsimd.memset(half_neg[:, :], -0.5).then_inc(sem("zeroed"), 1)
            pool.wait_ge(sem("zeroed"), 4)
            nc.gpsimd.memset(k_pack[96:99, :, :, :], 1.0).then_inc(sem("constants"), 1)
            pool.wait_ge(sem("constants"), 1)
            nc.gpsimd.memset(vT[:, :, :, :, 8:16], 1.0).then_inc(sem("constants"), 1)

            def step(n):
                if n.s % 2 == 0 and n.in_range(6):
                    T, u = n.tile(6), n.slot(6) // 2
                    at_least(pool, sem("mean_var"), T + 1, passed=t["passed"])
                    nc.gpsimd.tensor_scalar(rstd[:, u, 0:1], mean_var[:, u, 1:2], EPS, 1.0, ALU.add, ALU.mult
                                            ).then_inc(sem("var_eps"), 1)
                    at_least(pool, sem("var_eps"), T + 1, passed=t["passed"])
                    nc.gpsimd.tensor_tensor(rstd[:, u, 1:2], rstd[:, u, 0:1], half_neg[:, :], ALU.pow
                                            ).then_inc(sem("rstd"), 1)
                    at_least(pool, sem("z"), T + 1, passed=t["passed"])
                    at_least(pool, sem(f"parts_out{u}"), n.quarter(6) * 128, passed=t["passed"])
                    split(z[:, u, :], q_parts, q_rest, u, T, "q")
                if n.s % 2 == 1 and n.in_range(5):
                    T, u = n.tile(5), n.slot(5) // 2
                    at_least(pool, sem("vT_psum"), T - 1, passed=t["passed"])
                    at_least(pool, sem(f"parts_out{u}"), n.quarter(5) * 128, passed=t["passed"])
                    split(ctx_sb[:, bass.ds(T, 1), :].rearrange("p a l -> p (a l)"), k_parts, k_rest, u, T, "k")
                if n.s % 2 == 0 and n.in_range(-4):
                    T, u = n.tile(-4), n.slot(-4) // 2
                    row = xres[:, bass.ds(T, 1), :].rearrange("p a l -> p (a l)")
                    at_least(pool, sem("recip"), T + 1, passed=t["passed"])
                    nc.gpsimd.tensor_tensor(nd[:, u, 0, :], nd[:, u, 0, :], nd[:, u, 1, :], ALU.mult
                                            ).then_inc(sem("ratio"), 1)
                    at_least(pool, sem("ratio"), T + 1, passed=t["passed"])
                    nc.gpsimd.tensor_scalar(nd[:, u, 1, :], nd[:, u, 0, :], t["gain0"][:, :], 1.0, ALU.mult, ALU.mult
                                            ).then_inc(sem("gained"), 1)
                    at_least(pool, sem("gained"), T + 1, passed=t["passed"])
                    nc.gpsimd.tensor_tensor(row, row, nd[:, u, 1, :], ALU.add).then_inc(sem("x_done"), 1)

            def split(src, parts, rest, u, T, name):
                done = sem(name + "_split")
                nc.gpsimd.tensor_copy(parts[:, u, 0, :], src).then_inc(done, 1)
                at_least(pool, done, T * 3 + 1, passed=t["passed"])
                nc.gpsimd.tensor_tensor(rest[:, :], src, parts[:, u, 0, :], ALU.subtract).then_inc(done, 1)
                at_least(pool, done, T * 3 + 2, passed=t["passed"])
                nc.gpsimd.tensor_copy(parts[:, u, 1, :], rest[:, :]).then_inc(done, 1)
                at_least(pool, done, T * 3 + 3, passed=t["passed"])
                nc.gpsimd.tensor_tensor(parts[:, u, 2, :], rest[:, :], parts[:, u, 1, :], ALU.subtract
                                        ).then_inc(sem(name + "_parts"), 1)
                at_least(pool, sem(name + "_parts"), T + 1, passed=t["passed"])

            run(pool, step)
            pool.wait_ge(sem("x_done"), TILES)

        @block.scalar
        def _(act):
            def step(n):
                for hd in range(HEADS):
                    if n.in_range(0):
                        at_least(act, sem("s2_done"), n.half(0) * 8 + (hd + 1))
                        at_least(act, sem("pv_group"), n.half(0) * 2 + (hd // 4 - 1))
                        nc.scalar.activation(probs[:, hd, :, :].rearrange("p a q -> p (a q)"), s2[:, hd % 2, :],
                                             ACT.Exp, scale=SCALE).then_inc(sem("exp_done"), 1)
                    if hd == 1 and n.in_range(-1):
                        at_least(act, sem("pv_group"), n.half(0) * 2)
                        at_least(act, sem(f"pv_out{n.slot(-1, 2)}"), n.tile(-1) * 16)
                        nc.scalar.copy(pv_sb[:, n.slot(-1, 2), :, :], pv[:, :, :]).then_inc(sem("pv_sb"), 1)
                    if hd == 7 and n.s % 2 == 1 and n.in_range(1):
                        T, u = n.tile(1), n.slot(1) // 2
                        at_least(act, sem("vT_psum"), T + 1)
                        at_least(act, sem("pv_group"), n.half(0) * 2 - 2)
                        if n.static:
                            at_least(act, sem("constants"), 2)
                        nc.scalar.copy(vT[:, u, :, :, 0:8], misc[:, 0:256].rearrange("p (a h d) -> p a h d", a=2, d=8)
                                       ).then_inc(sem("vT"), 1)

            run(act, step)

        @block.vector
        def _(dve):
            def step(n):
                if n.s % 2 == 0 and n.in_range(6):
                    T, u = n.tile(6), n.slot(6) // 2
                    row = xres[:, bass.ds(T, 1), :].rearrange("p a l -> p (a l)")
                    at_least(dve, sem("mean_var"), T, passed=t["passed"])
                    nc.vector.bn_stats(stat6[:, :], row).then_inc(sem("stats"), 1)
                    at_least(dve, sem("stats"), T + 1, passed=t["passed"])
                    at_least(dve, sem("z"), T - 1, passed=t["passed"])
                    nc.vector.bn_aggr(mean_var[:, u, :], stat6[:, :]).then_inc(sem("mean_var"), 1)
                for p in range(4):
                    if n.in_range(2):
                        at_least(dve, sem("s1_done"), n.half(2) * 4 + (p + 1))
                        if p == 0:
                            at_least(dve, sem("neg_parts"), n.half(1))
                        nc.vector.tensor_reduce(
                            neg_max[:, n.slot(0, 2), 2 * p:2 * p + 2, :],
                            s1[:, 2 * (p % 2):2 * (p % 2) + 2, :].rearrange("p a (b l) -> p a b l", b=2),
                            AX.X, ALU.max, negate=True).then_inc(sem("max_done"), 1)
                    if p == 0 and n.in_range(1):
                        at_least(dve, sem("negT"), n.half(2))
                        at_least(dve, sem(f"neg_in{n.slot(1, 2)}"), n.tile(1) * 16)
                        nc.vector.tensor_copy(neg_rows[:, n.slot(1, 2), :], negT).then_inc(sem("neg_rows"), 1)
                    if p == 1 and n.s % 2 == 0 and n.in_range(6):
                        T, u = n.tile(6), n.slot(6) // 2
                        row = xres[:, bass.ds(T, 1), :].rearrange("p a l -> p (a l)")
                        at_least(dve, sem("rstd"), T + 1)
                        at_least(dve, sem("q_parts"), T - 1)
                        nc.vector.tensor_scalar(z[:, u, :], row, mean_var[:, u, 0:1], rstd[:, u, 1:2],
                                                ALU.subtract, ALU.mult).then_inc(sem("z"), 1)
                    if p == 2 and n.s % 2 == 0 and n.in_range(-4):
                        T, u = n.tile(-4), n.slot(-4) // 2
                        at_least(dve, sem(f"nd_in{u}"), n.quarter(-4) * 32 + 32)
                        nc.vector.reciprocal(nd[:, u, 1, :], nd[:, u, 1, :]).then_inc(sem("recip"), 1)
                if n.in_range(2):
                    b = n.slot(0, 2)
                    flat = neg_max[:, b, :, :].rearrange("p a b -> p (a b)")
                    h = n.half(2)
                    at_least(dve, sem("max_done"), h * 4 + 4)
                    at_least(dve, sem("negT"), h - 1)
                    nc.vector.tensor_copy(neg_parts[:, b, 0, :], flat).then_inc(sem("neg_split"), 1)
                    dve.wait_ge(sem("neg_split"), h * 3 + 1)
                    nc.vector.tensor_tensor(neg_rest[:, :], flat, neg_parts[:, b, 0, :], ALU.subtract
                                            ).then_inc(sem("neg_split"), 1)
                    dve.wait_ge(sem("neg_split"), h * 3 + 2)
                    nc.vector.tensor_copy(neg_parts[:, b, 1, :], neg_rest[:, :]).then_inc(sem("neg_split"), 1)
                    dve.wait_ge(sem("neg_split"), h * 3 + 3)
                    nc.vector.tensor_tensor(neg_parts[:, b, 2, :], neg_rest[:, :], neg_parts[:, b, 1, :], ALU.subtract
                                            ).then_inc(sem("neg_parts"), 1)

            run(dve, step)

        @block.tensor
        def _(pe):
            pe.wait_ge(sem("constants"), 2)

            def pv_group(n, k, g):
                if not n.in_range(k):
                    return
                b, u = n.slot(k, 2), n.slot(k) // 2
                at_least(pe, sem("exp_done"), n.half(k) * 8 + (4 * g + 4))
                if g == 0:
                    at_least(pe, sem("vT"), n.tile(k) + 1)
                    at_least(pe, sem("pv_sb"), n.half(k))
                for a in range(2):
                    for j in range(4):
                        last = nc.tensor.matmul(pv[32 * j:32 * j + 32, g, :], vT[:, u, a, 8 * b + 4 * g + j, :],
                                                probs[:, 4 * g + j, a, :], start=(a == 0), stop=(a == 1),
                                                skip_group_check=True)
                last.then_inc(sem("pv_group"), 1)

            def step(n):
                for p in range(4):
                    if n.in_range(2):
                        slot = n.slot(2)
                        if p == 0:
                            at_least(pe, sem(f"pack_in{slot}"), n.quarter(2) * 32 + 32)
                        at_least(pe, sem("max_done"), n.half(2) * 4 + (p - 1))
                        for hd in (2 * p, 2 * p + 1):
                            for m in range(2):
                                last = nc.tensor.matmul(s1[:, 2 * (p % 2) + hd % 2, m * D:(m + 1) * D],
                                                        q_pack[0:96, slot, hd, m * P:(m + 1) * P],
                                                        k_pack[0:96, slot, hd, :], start=True, stop=True)
                        last.then_inc(sem("s1_done"), 1)
                    for hd in (2 * p, 2 * p + 1) if n.in_range(0) else ():
                        slot = n.slot(0)
                        if hd == 0:
                            at_least(pe, sem(f"neg_in{n.slot(0, 2)}"), n.tile(0) * 16 + 16)
                            at_least(pe, sem(f"pack_in{slot}"), n.quarter(0) * 32 + 32)
                        at_least(pe, sem("exp_done"), n.half(0) * 8 + (hd - 1))
                        for m in range(2):
                            last = nc.tensor.matmul(s2[:, hd % 2, m * D:(m + 1) * D],
                                                    k_pack[0:99, slot, hd, m * P:(m + 1) * P],
                                                    q_pack[0:99, slot, hd, :], start=True, stop=True)
                        last.then_inc(sem("s2_done"), 1)
                    if p == 0:
                        if n.in_range(1):
                            at_least(pe, sem("neg_parts"), n.half(2), passed=t["passed"])
                            at_least(pe, sem("neg_rows"), n.half(1), passed=t["passed"])
                            at_least(pe, sem("vT"), n.tile(2), passed=t["passed"])
                            nc.tensor.transpose(negT, neg_parts[:, n.slot(1, 2), :, :].rearrange("p a b -> p (a b)"),
                                                identb[:, :]).then_inc(sem("negT"), 1)
                        pv_group(n, -1, 1)
                    if p == 2 and n.s % 2 == 1 and n.in_range(1):
                        T, u = n.tile(1), n.slot(1) // 2
                        at_least(pe, sem("k_parts"), T + 1)
                        at_least(pe, sem("vT"), T)
                        at_least(pe, sem("neg_rows"), n.half(2))
                        for m in range(2):
                            for a in range(3):
                                last = nc.tensor.matmul(misc[:, m * P:(m + 1) * P], k_parts[:, u, a, m * P:(m + 1) * P],
                                                        identb[:, :], start=(a == 0), stop=(a == 2))
                        last.then_inc(sem("vT_psum"), 1)
                    if p == 2:
                        pv_group(n, 0, 0)

            run(pe, step)


CT = 4
CHUNKS = TILES // CT
N = CT * P
TINY = EPS * 1e-12 / 32.0

PER = {
    "dve_pre": 47, "mv1": 1, "pow1": 1, "q_in": 1, "xq": 1, "xqT_ps": 1, "xqT": 1, "hp": 4, "gelu": 4, "ssq": 4,
    "absmax": 4, "hr": 4, "hq": 4, "hqT_ps": 4, "hqT": 4, "y": 4, "y2": 4, "norm2": 1, "pool_pre": 6, "mv2": 1,
    "rstd2": 1, "yn": 1, "ys": 1, "mv3": 1, "rstd3": 1, "yn2": 1, "yb": 1, "x3": 1, "mv4": 1, "rstd4": 1, "z": 1,
    "zT": 1, "xTf": 1, "x_hi": 1, "x_lo": 1, "logits_ps": 1, "logits": 1, "gap": 1, "exp_gap": 1, "routing": 1,
    "gT_ps": 1, "gT": 1, "spread_ps": 6, "spread": 6, "summ_in": 16 * CT,
    "a_ps": 4, "a_hi": 4, "a_lo": 4, "a_masked": 4, "f0": 7, "fd": 7, "silu": 14, "gated": 14, "weighted": 14,
    "mixed": 7, "g1_hi": 7, "gc_hi": 7, "g1_lo": 7, "gc_lo": 7, "p_ps": 4, "p_read": 4, "m_hi": 2, "m_lo": 2,
    "dve_main": 2, "down": 4, "out_sb": 4, "stored": 16,
}


def tokens(nc, t):
    with ExitStack() as ctx:
        sem = Sems(nc, ctx, "tok")

        def sb(name, shape, dt=F32):
            return ctx.enter_context(nc.sbuf_tensor(name, shape, dt))

        def psum(name, shape, dt=F32):
            return ctx.enter_context(nc.psum_tensor(name, shape, dt))

        def need(eng, name, c, k, apart=False):
            apart = apart or eng.engine in (nc.gpsimd.engine, nc.sync.engine)
            at_least(eng, sem(name), c * PER[name] + (PER[name] + k), passed=t["passed"] if apart else None)

        xres, identb, ident = t["x"], t["identb"], t["ident"]

        st6 = sb("st6", [P, CT, 6])
        mv = sb("mv", [P, CT, 2])
        sm = sb("sm", [P, 16, CT])
        powers = sb("exponents", [P, 3, CT])
        d4 = sb("d4", [P, CT, D])
        xq = sb("xq", [P, CT, D], BF16)
        xqT = sb("xqT", [P, 2, N], BF16)
        h = sb("h", [P, 2, F1])
        junk = sb("junk", [P, F1], BF16)
        hq = sb("hq", [P, 2, F1], BF16)
        hqT = sb("hqT", [P, 8, P], BF16)
        y2 = sb("y2", [P, CT, D])
        xTf = h[:, 0, :].rearrange("p (a b) -> p a b", b=N)
        summ = h[:, 1, :].rearrange("p (a b) -> p a b", b=D)
        y4 = d4
        xT_hi = sb("xT_hi", [P, 2, N], BF16)
        xT_lo = sb("xT_lo", [P, 2, N], BF16)
        logits = sb("logits", [P, CT, E])
        top = sb("top", [P, CT, 8])
        top_i = sb("top_i", [P, CT, 8], U32)
        top_f = sb("top_f", [P, CT, 2])
        experts = sb("experts", [P, CT, E])
        onehot = sb("onehot", [P, CT, E])
        rw = sb("rw", [P, CT, 2])
        rw_rest = sb("rw_rest", [P, CT, 2])
        gpack = sb("gpack", [P, CT, 32], BF16)
        gT = sb("gT", [32, N], BF16)
        sel = sb("sel", [32, 6, P], BF16)
        sel_ones = sb("sel_ones", [32, 4, P], BF16)
        mask = sb("mask", [P, 4, N], BF16)
        rw_rows = sb("rw_rows", [P, 2, N])

        a_hi = sb("a_hi", [P, 2, N], BF16)
        a_lo = sb("a_lo", [P, 2, N], BF16)
        am = sb("a_masked", [P, 4, 2, 2, N], BF16)
        sil = sb("sil", [P, 2, N])
        gated = sb("gated", [P, 2, N])
        w0 = sb("weighted0", [P, 2, N])
        w1 = sb("weighted1", [P, 2, N])
        wc = sb("mixed", [P, 2, N])
        g1_hi, g1_lo = sb("g1_hi", [P, FT, N], BF16), sb("g1_lo", [P, FT, N], BF16)
        gc_hi, gc_lo = sb("gc_hi", [P, FT, N], BF16), sb("gc_lo", [P, FT, N], BF16)
        pm = [sil[:, 0, :], sil[:, 1, :], gated[:, 0, :]]
        m_hi, m_lo = a_hi, a_lo
        out_sb = wc[:, :, :].rearrange("p a (b d) -> p (a b) d", d=D)

        X = psum("X", [P, 4, 512])
        Y = psum("Y", [P, 4, 512])
        Y0b = Y[:, 0, :].bitcast(BF16)
        Y3b = Y[:, 3, :].bitcast(BF16)
        BANKS = (2, 3, 0, 1)
        ORDER = [(0, 0)] + [o for f in range(1, FT) for o in ((f, 0), (f - 1, 1))] + [(FT - 1, 1)]
        AT = {o: n for n, o in enumerate(ORDER)}

        def xrow(c, j):
            return xres[:, bass.ds(c * CT + j, 1), :].rearrange("p a l -> p (a l)")

        def xchunk(c):
            return xres[:, bass.ds(c * CT, CT), :].rearrange("p a l -> p (a l)")

        def flat(ap):
            return ap.rearrange("p a b -> p (a b)")

        block = ctx.enter_context(nc.Block())

        def run(eng, step):
            step(None, 0)
            with eng.Fori(0, CHUNKS - 1) as c:
                step(c, c + 1)
            step(CHUNKS - 1, None)

        @block.sync
        def _(sp):
            for name in PER:
                sp.sem_inc(sem(name), PER[name])

            def step(c, e):
                if e is not None:
                    need(sp, "hq", e, CT)
                    for j in range(CT):
                        src = t["summ_dram"][bass.ds((e * CT + j) * 2, 2), :].unsqueeze(1).to_broadcast([2, S, D])
                        sp.dma_start(summ[:, j, :], src).then_inc(sem("summ_in"), 16)
                if c is not None:
                    need(sp, "out_sb", c, CT)
                    sp.dma_start(t["out_dram"][:, bass.ds(c * CT, CT), :], out_sb[:, :, :]).then_inc(sem("stored"), 16)

            run(sp, step)
            need(sp, "stored", CHUNKS - 1, 16)

        @block.gpsimd
        def _(pool):
            consts = sem("consts")
            nc.gpsimd.memset(sel_ones[:, :, :], 1.0).then_inc(consts, 1)
            nc.gpsimd.memset(gpack[:, :, :], 0.0).then_inc(consts, 1)
            nc.gpsimd.iota(top_i[:, :, :], pattern=[[0, CT], [1, E]], base=0, channel_multiplier=0).then_inc(consts, 1)
            pool.wait_ge(consts, 3)
            nc.gpsimd.tensor_copy(experts[:, :, :], top_i[:, :, :]).then_inc(consts, 1)
            nc.gpsimd.affine_select(
                out=sel[:, 0:4, :].rearrange("p (a b) (m r) -> p a b m r", a=2, m=4),
                in_=sel_ones[:, :, :].rearrange("p (a b) (m r) -> p a b m r", a=2, m=4),
                compare_op=ALU.is_equal, fill=0.0, base=0, pattern=[[-8, 2], [-4, 2], [-1, 4], [0, R]],
                channel_multiplier=1).then_inc(consts, 1)
            nc.gpsimd.affine_select(out=sel[:, 4:6, :], in_=sel_ones[:, 0:2, :], compare_op=ALU.is_ge, fill=0.0,
                                    base=-16, pattern=[[-3, 2], [0, P]], channel_multiplier=1).then_inc(consts, 1)
            pool.wait_ge(consts, 6)
            nc.gpsimd.affine_select(out=sel[:, 4:6, :], in_=sel[:, 4:6, :], compare_op=ALU.is_ge, fill=0.0,
                                    base=18, pattern=[[3, 2], [0, P]], channel_multiplier=-1).then_inc(consts, 1)
            for k, value in enumerate((-0.5, 0.5, 2.718281828459045)):
                nc.gpsimd.memset(powers[:, k, :], value).then_inc(consts, 1)
            pool.wait_ge(consts, 10)

            def rstd(c, mv_name, name, k):
                need(pool, mv_name, c, 1)
                nc.gpsimd.tensor_scalar(sm[:, 1, :], mv[:, :, 1], EPS, 1.0, ALU.add, ALU.mult).then_inc(sem("pool_pre"), 1)
                need(pool, "pool_pre", c, k)
                nc.gpsimd.tensor_tensor(sm[:, 0, :], sm[:, 1, :], powers[:, 0, :], ALU.pow).then_inc(sem(name), 1)

            def weigh(c, o):
                f, slot = ORDER[o]
                need(pool, "gated", c, o + 1)
                if slot == 0:
                    need(pool, "mixed", c, max(f - 1, 0))
                    nc.gpsimd.tensor_tensor(w0[:, f % 2, :], gated[:, o % 2, :], rw_rows[:, 0, :], ALU.mult
                                            ).then_inc(sem("weighted"), 1)
                else:
                    need(pool, "g1_lo", c, max(f - 1, 0))
                    nc.gpsimd.tensor_tensor(w1[:, f % 2, :], gated[:, o % 2, :], rw_rows[:, 1, :], ALU.mult
                                            ).then_inc(sem("weighted"), 1)
                    need(pool, "weighted", c, o + 1)
                    need(pool, "gc_lo", c, max(f - 1, 0))
                    if f == 0:
                        need(pool, "stored", c, 0)
                    nc.gpsimd.tensor_tensor(wc[:, f % 2, :], w0[:, f % 2, :], w1[:, f % 2, :], ALU.add
                                            ).then_inc(sem("mixed"), 1)

            def main(c, s):
                if s == 0:
                    need(pool, "spread", c, 6)
                    weigh(c, 0)
                elif s < FT:
                    weigh(c, 2 * s - 1)
                    weigh(c, 2 * s)
                elif s == FT:
                    weigh(c, 2 * FT - 1)

            def pre(c, s):
                if s == 0:
                    need(pool, "mv1", c, 1)
                    nc.gpsimd.tensor_tensor(sm[:, 2, :], mv[:, :, 1], powers[:, 1, :], ALU.pow).then_inc(sem("pool_pre"), 1)
                    need(pool, "pool_pre", c, 1)
                    rstd(c, "mv1", "pow1", 2)
                    need(pool, "q_in", c, 1)
                    need(pool, "xqT_ps", c, 0)
                    nc.gpsimd.tensor_scalar(flat(xq[:, :, :]), flat(d4[:, :, :]), -ROUND, 1.0, ALU.add, ALU.mult
                                            ).then_inc(sem("xq"), 1)
                elif 2 <= s <= 5:
                    j = s - 2
                    need(pool, "hr", c, j + 1)
                    need(pool, "hqT_ps", c, j - 1)
                    nc.gpsimd.tensor_scalar(hq[:, j % 2, :], h[:, j % 2, :], -ROUND, 1.0, ALU.add, ALU.mult
                                            ).then_inc(sem("hq"), 1)
                elif s == 6:
                    need(pool, "ssq", c, 4)
                    nc.gpsimd.tensor_tensor(sm[:, 9, :], sm[:, 8, :], powers[:, 1, :], ALU.pow).then_inc(sem("norm2"), 1)
                    rstd(c, "mv2", "rstd2", 3)
                    need(pool, "yn", c, 1)
                    need(pool, "summ_in", c, 16 * CT)
                    nc.gpsimd.tensor_tensor(flat(y4[:, :, :]), flat(y4[:, :, :]), flat(summ[:, :, :]), ALU.add
                                            ).then_inc(sem("ys"), 1)
                    rstd(c, "mv3", "rstd3", 4)
                    need(pool, "yn2", c, 1)
                    nc.gpsimd.tensor_tensor(y4[:, :, :], y4[:, :, :], t["gamma"][:, :].unsqueeze(1).to_broadcast([P, CT, D]),
                                            ALU.mult).then_inc(sem("pool_pre"), 1)
                    need(pool, "pool_pre", c, 5)
                    nc.gpsimd.tensor_tensor(y4[:, :, :], y4[:, :, :], t["beta"][:, :].unsqueeze(1).to_broadcast([P, CT, D]),
                                            ALU.add).then_inc(sem("yb"), 1)
                elif s == 7:
                    rstd(c, "mv4", "rstd4", 6)
                    need(pool, "gap", c, 1)
                    nc.gpsimd.tensor_tensor(sm[:, 12, :], powers[:, 2, :], sm[:, 11, :], ALU.pow).then_inc(sem("exp_gap"), 1)

            def step(c, e):
                for s in range(9):
                    if c is not None:
                        main(c, s)
                    if e is not None:
                        pre(e, s)

            run(pool, step)

        @block.scalar
        def _(act):
            def silu(c, o):
                f, slot = ORDER[o]
                need(act, "fd" if slot else "f0", c, f + 1)
                need(act, "gated", c, o - 1)
                if o == 0:
                    need(act, "m_lo", c, 0)
                nc.scalar.activation(sil[:, o % 2, :], X[:, 2 * (f % 2), :], ACT.Silu).then_inc(sem("silu"), 1)

            def high(c, f):
                need(act, "weighted", c, AT[f, 1] + 1)
                need(act, "p_ps", c, 0)
                nc.scalar.copy(g1_hi[:, f, :], w1[:, f % 2, :]).then_inc(sem("g1_hi"), 1)
                need(act, "mixed", c, f + 1)
                need(act, "down", c, 0)
                nc.scalar.copy(gc_hi[:, f, :], wc[:, f % 2, :]).then_inc(sem("gc_hi"), 1)

            def main(c, s):
                if s == 0:
                    for q in range(4):
                        need(act, "a_ps", c, q + 1)
                        need(act, "a_masked", c, q - 1)
                        if q == 0:
                            need(act, "down", c, 0)
                        nc.scalar.copy(a_hi[:, q % 2, :], X[:, q, :]).then_inc(sem("a_hi"), 1)
                    silu(c, 0)
                elif s <= FT:
                    if s < FT:
                        silu(c, 2 * s - 1)
                    silu(c, 2 * s if s < FT else 2 * FT - 1)
                    if s >= 2:
                        high(c, s - 2)
                    if s == FT:
                        high(c, FT - 1)

            def pre(c, s):
                if s == 0:
                    need(act, "xqT_ps", c, 1)
                    need(act, "hp", c, 0)
                    nc.scalar.copy(flat(xqT[:, :, :]), Y0b).then_inc(sem("xqT"), 1)
                if 1 <= s <= 4:
                    j = s - 1
                    need(act, "hp", c, j + 1)
                    need(act, "hq", c, j - 1)
                    if j == 0:
                        need(act, "logits_ps", c, 0)
                        need(act, "x_lo", c, 0)
                    if j == 1:
                        need(act, "ys", c, 0)
                    need(act, "ssq", c, j)
                    nc.scalar.activation(h[:, j % 2, :], flat(Y[:, 1:3, :]), ACT.Gelu, scale=sm[:, 10, j:j + 1]
                                         ).then_inc(sem("gelu"), 1)
                    need(act, "gelu", c, j + 1)
                    nc.scalar.activation(junk[:, :], h[:, j % 2, :], ACT.Square, accum_out=sm[:, 8, j:j + 1]
                                         ).then_inc(sem("ssq"), 1)
                if 2 <= s <= 5:
                    j = s - 2
                    need(act, "hqT_ps", c, j + 1)
                    need(act, "y", c, j)
                    nc.scalar.copy(flat(hqT[:, :, :]), Y3b).then_inc(sem("hqT"), 1)
                if s == 7:
                    need(act, "zT", c, 1)
                    need(act, "hq", c, CT - 1)
                    nc.scalar.copy(flat(xTf[:, :, :]), flat(Y[:, 1:3, :])).then_inc(sem("xTf"), 1)
                    need(act, "xTf", c, 1)
                    nc.scalar.copy(flat(xT_hi[:, :, :]), flat(xTf[:, :, :])).then_inc(sem("x_hi"), 1)
                if s == 8:
                    for v in range(6):
                        need(act, "spread_ps", c, v + 1)
                        dst = mask[:, v, :] if v < 4 else rw_rows[:, v - 4, :]
                        nc.scalar.copy(dst, Y[:, 2 + v % 2, :]).then_inc(sem("spread"), 1)

            def step(c, e):
                for s in range(9):
                    if c is not None:
                        main(c, s)
                    if e is not None:
                        if s == 8 and c is not None:
                            need(act, "m_hi", c, 2)
                            need(act, "mixed", c, FT)
                        pre(e, s)

            run(act, step)

        @block.vector
        def _(dve):
            links = {}

            def link(ins, c, name="dve_pre", apart=False):
                links[name] = links.get(name, 0) % PER[name] + 1
                ins.then_inc(sem(name), 1)
                need(dve, name, c, links[name], apart=apart)

            def small(dst, c, op, *args, **kw):
                link(op(sm[:, dst, :], *args, **kw), c)

            def stats(rows, c, name):
                for j in range(CT):
                    last = nc.vector.bn_stats(st6[:, j, :], rows(j))
                link(last, c, apart=True)
                for j in range(CT):
                    last = nc.vector.bn_aggr(mv[:, j, :], st6[:, j, :])
                last.then_inc(sem(name), 1)
                need(dve, name, c, 1)

            def normed(rows, dst, c, name):
                for j in range(CT):
                    last = nc.vector.tensor_scalar(dst(j), rows(j), mv[:, j, 0:1], sm[:, 0, j:j + 1], ALU.subtract, ALU.mult)
                last.then_inc(sem(name), 1)

            def gate(c, o):
                f, slot = ORDER[o]
                need(dve, "silu", c, o + 1)
                need(dve, "weighted", c, o - 1)
                nc.vector.tensor_tensor(gated[:, o % 2, :], sil[:, o % 2, :], X[:, 2 * (f % 2) + 1, :], ALU.mult
                                        ).then_inc(sem("gated"), 1)

            def low(c, f):
                need(dve, "g1_hi", c, f + 1)
                nc.vector.tensor_tensor(g1_lo[:, f, :], w1[:, f % 2, :], g1_hi[:, f, :], ALU.subtract).then_inc(sem("g1_lo"), 1)
                need(dve, "gc_hi", c, f + 1)
                nc.vector.tensor_tensor(gc_lo[:, f, :], wc[:, f % 2, :], gc_hi[:, f, :], ALU.subtract).then_inc(sem("gc_lo"), 1)

            def main(c, s):
                if s == 0:
                    need(dve, "fd", c, 0)
                    need(dve, "spread", c, 6)
                    for q in range(4):
                        need(dve, "a_hi", c, q + 1)
                        need(dve, "a_masked", c, q - 1)
                        nc.vector.tensor_tensor(a_lo[:, q % 2, :], X[:, q, :], a_hi[:, q % 2, :], ALU.subtract
                                                ).then_inc(sem("a_lo"), 1)
                        need(dve, "a_lo", c, q + 1)
                        for slot in range(2):
                            for b, part in enumerate((a_hi, a_lo)):
                                last = nc.vector.tensor_tensor(am[:, q, slot, b, :], part[:, q % 2, :],
                                                               mask[:, 2 * slot + q % 2, :], ALU.mult)
                        last.then_inc(sem("a_masked"), 1)
                    gate(c, 0)
                elif s <= FT:
                    if s < FT:
                        gate(c, 2 * s - 1)
                    gate(c, 2 * s if s < FT else 2 * FT - 1)
                    if s >= 2:
                        low(c, s - 2)
                    if s == FT:
                        low(c, FT - 1)
                else:
                    for k in range(2):
                        for w in range(2):
                            q = 2 * k + w
                            need(dve, "p_ps", c, q + 1)
                            if w == 0:
                                need(dve, "m_lo", c, k)
                            nc.vector.tensor_tensor(pm[w], X[:, BANKS[q], :], mask[:, 2 * w + k, :], ALU.mult
                                                    ).then_inc(sem("p_read"), 1)
                        need(dve, "p_read", c, 2 * k + 2)
                        link(nc.vector.tensor_tensor(pm[2], pm[0], pm[1], ALU.add), c, "dve_main")
                        need(dve, "down", c, 0)
                        nc.vector.tensor_copy(m_hi[:, k, :], pm[2]).then_inc(sem("m_hi"), 1)
                        need(dve, "m_hi", c, k + 1)
                        nc.vector.tensor_tensor(m_lo[:, k, :], pm[2], m_hi[:, k, :], ALU.subtract
                                                ).then_inc(sem("m_lo"), 1)

            def store(c, j):
                need(dve, "down", c, j + 1)
                nc.vector.scalar_tensor_tensor(out=out_sb[:, j, :], in0=X[:, BANKS[j], 0:D], scalar=t["tanh"][:, 3:4],
                                               in1=xrow(c, j), op0=ALU.mult, op1=ALU.add).then_inc(sem("out_sb"), 1)

            def pre(c, s):
                V = nc.vector
                if s == 0:
                    stats(lambda j: xrow(c, j), c, "mv1")
                    for j in range(CT):
                        last = V.tensor_scalar(d4[:, j, :], xrow(c, j), mv[:, j, 0:1], None, ALU.subtract)
                    link(last, c)
                    small(3, c, V.tensor_reduce, d4[:, :, :], AX.X, ALU.max, apply_absolute_value=True)
                    need(dve, "pow1", c, 1)
                    small(4, c, V.tensor_tensor, sm[:, 2, :], sm[:, 0, :], ALU.mult)
                    small(4, c, V.tensor_scalar, sm[:, 4, :], float(D) ** 0.5, 1e-12, ALU.mult, ALU.max)
                    small(5, c, V.reciprocal, sm[:, 4, :])
                    small(4, c, V.tensor_tensor, sm[:, 0, :], sm[:, 5, :], ALU.mult)
                    small(4, c, V.tensor_scalar, sm[:, 4, :], float(D) ** 0.5, None, ALU.mult)
                    small(5, c, V.tensor_tensor, sm[:, 4, :], sm[:, 3, :], ALU.mult)
                    small(5, c, V.tensor_scalar, sm[:, 5, :], EPS, 1.0 / 127.0, ALU.max, ALU.mult)
                    small(6, c, V.reciprocal, sm[:, 5, :])
                    small(7, c, V.tensor_tensor, sm[:, 4, :], sm[:, 6, :], ALU.mult)
                    need(dve, "gelu", c, 0)
                    small(10, c, V.tensor_scalar, sm[:, 5, :], t["mean1"][:, :], None, ALU.mult)
                    for j in range(CT):
                        last = V.tensor_scalar(d4[:, j, :], d4[:, j, :], sm[:, 7, j:j + 1], ROUND, ALU.mult, ALU.add)
                    last.then_inc(sem("q_in"), 1)
                if 2 <= s <= 5:
                    j = s - 2
                    if j == 0:
                        need(dve, "norm2", c, 0)
                    need(dve, "gelu", c, j + 1)
                    link(V.tensor_reduce(sm[:, 13, j:j + 1], h[:, j % 2, :], AX.X, ALU.max, apply_absolute_value=True), c)
                    link(V.tensor_scalar(sm[:, 14, j:j + 1], sm[:, 13, j:j + 1], TINY, 1.0 / 127.0, ALU.max, ALU.mult), c)
                    link(V.reciprocal(sm[:, 15, j:j + 1], sm[:, 14, j:j + 1]), c)
                    need(dve, "ssq", c, j + 1)
                    V.tensor_scalar(h[:, j % 2, :], h[:, j % 2, :], sm[:, 15, j:j + 1], ROUND, ALU.mult, ALU.add).then_inc(sem("hr"), 1)
                if 3 <= s <= 6:
                    j = s - 3
                    need(dve, "y", c, j + 1)
                    V.tensor_copy(y2[:, j, :], Y[:, 0, 0:D]).then_inc(sem("y2"), 1)
                if s == 6:
                    need(dve, "norm2", c, 1)
                    small(4, c, V.tensor_scalar, sm[:, 9, :], 1e-12, None, ALU.max)
                    small(5, c, V.reciprocal, sm[:, 4, :])
                    small(4, c, V.tensor_tensor, sm[:, 13, :], sm[:, 5, :], ALU.mult)
                    small(4, c, V.tensor_scalar, sm[:, 4, :], float(F1) ** 0.5, EPS, ALU.mult, ALU.max)
                    small(4, c, V.tensor_scalar, sm[:, 4, :], 1.0 / 127.0, None, ALU.mult)
                    small(4, c, V.tensor_scalar, sm[:, 4, :], t["mean2"][:, :], t["tanh"][:, 2:3], ALU.mult, ALU.mult)
                    need(dve, "y2", c, 4)
                    for j in range(CT):
                        last = V.scalar_tensor_tensor(out=xrow(c, j), in0=y2[:, j, :], scalar=sm[:, 4, j:j + 1],
                                                      in1=xrow(c, j), op0=ALU.mult, op1=ALU.add)
                    link(last, c, apart=True)
                    stats(lambda j: xrow(c, j), c, "mv2")
                    need(dve, "rstd2", c, 1)
                    normed(lambda j: xrow(c, j), lambda j: y4[:, j, :], c, "yn")
                    need(dve, "ys", c, 1, apart=True)
                    stats(lambda j: y4[:, j, :], c, "mv3")
                    need(dve, "rstd3", c, 1)
                    normed(lambda j: y4[:, j, :], lambda j: y4[:, j, :], c, "yn2")
                    need(dve, "yb", c, 1)
                    V.scalar_tensor_tensor(out=xchunk(c), in0=flat(y4[:, :, :]), scalar=t["tanh"][:, 1:2], in1=xchunk(c),
                                           op0=ALU.mult, op1=ALU.add).then_inc(sem("x3"), 1)
                    need(dve, "x3", c, 1, apart=True)
                    stats(lambda j: xrow(c, j), c, "mv4")
                if s == 7:
                    need(dve, "rstd4", c, 1)
                    need(dve, "x3", c, 1)
                    normed(lambda j: xrow(c, j), lambda j: y4[:, j, :], c, "z")
                    need(dve, "x_hi", c, 1)
                    V.tensor_tensor(flat(xT_lo[:, :, :]), flat(xTf[:, :, :]), flat(xT_hi[:, :, :]), ALU.subtract
                                    ).then_inc(sem("x_lo"), 1)
                    need(dve, "logits_ps", c, 1)
                    V.tensor_copy(flat(logits[:, :, :]), Y[:, 0, 0:CT * E]).then_inc(sem("logits"), 1)
                    need(dve, "logits", c, 1, apart=True)
                    for j in range(CT):
                        last = V.max(top[:, j, :], logits[:, j, :])
                    link(last, c, apart=True)
                    for j in range(CT):
                        last = V.max_index(top_i[:, j, :], top[:, j, :], logits[:, j, :])
                    link(last, c)
                    need(dve, "exp_gap", c, 0)
                    V.tensor_tensor(sm[:, 11, :], top[:, :, 1], top[:, :, 0], ALU.subtract).then_inc(sem("gap"), 1)
                    link(V.tensor_copy(top_f[:, :, :], top_i[:, :, 0:2]), c)
                    need(dve, "gT_ps", c, 0)
                    link(V.tensor_tensor(gpack[:, :, 0:8], experts[:, :, :], top_f[:, :, 0:1].to_broadcast([P, CT, E]),
                                         ALU.is_equal), c)
                    link(V.tensor_tensor(onehot[:, :, :], experts[:, :, :], top_f[:, :, 1:2].to_broadcast([P, CT, E]),
                                         ALU.is_equal), c)
                    link(V.tensor_tensor(gpack[:, :, 8:16], onehot[:, :, :], gpack[:, :, 0:8], ALU.subtract), c)
                    need(dve, "exp_gap", c, 1)
                    small(4, c, V.tensor_scalar, sm[:, 12, :], 1.0, None, ALU.add)
                    link(V.reciprocal(rw[:, :, 0], sm[:, 4, :]), c)
                    link(V.tensor_tensor(rw[:, :, 1], sm[:, 12, :], rw[:, :, 0], ALU.mult), c)
                    part = gpack[:, :, 16:22].rearrange("p a (s i) -> p i a s", i=3)
                    link(V.tensor_copy(part[:, 0], rw[:, :, :]), c)
                    link(V.tensor_tensor(rw_rest[:, :, :], rw[:, :, :], part[:, 0], ALU.subtract), c)
                    link(V.tensor_copy(part[:, 1], rw_rest[:, :, :]), c)
                    V.tensor_tensor(part[:, 2], rw_rest[:, :, :], part[:, 1], ALU.subtract).then_inc(sem("routing"), 1)
                if s == 8:
                    need(dve, "gT_ps", c, 1)
                    V.tensor_copy(gT[:, :], Y0b[0:32, 0:N]).then_inc(sem("gT"), 1)

            def step(c, e):
                for s in range(9):
                    if c is not None:
                        main(c, s)
                    if e is not None:
                        pre(e, s)
                if c is not None:
                    for j in range(CT):
                        store(c, j)

            run(dve, step)
            assert all(links[n] == PER[n] for n in links), links

        @block.tensor
        def _(pe):
            pe.wait_ge(sem("consts"), 10)
            mm = nc.tensor.matmul
            PARTS = ((0, 0), (1, 0), (0, 1))

            def products(out, pairs, start, stop):
                n = len(pairs) * 3
                for i, (lhs, rhs) in enumerate(pairs):
                    for k, (a, b) in enumerate(PARTS):
                        last = mm(out, lhs[a], rhs[b], start=start and i == k == 0, stop=stop and 3 * i + k == n - 1,
                                  skip_group_check=True)
                return last

            def lora(w, k, f, slot, out, stop):
                q = 2 * w + k
                wt = ("B1", "B3")[w]
                fs = slice(f * P, (f + 1) * P)
                return products(out, [((t[wt + "_hi"][:, k, fs], t[wt + "_lo"][:, k, fs]),
                                       (am[:, q, slot, 0, :], am[:, q, slot, 1, :]))], False, stop)

            def first(c, f):
                if f < 2:
                    need(pe, "a_lo", c, 4)
                    need(pe, "p_read", c, 0)
                else:
                    need(pe, "gated", c, AT[f - 2, 1] + 1)
                if f == 0:
                    need(pe, "a_masked", c, 4)
                for w, wt in enumerate(("W1", "W3")):
                    out = X[:, 2 * (f % 2) + w, :]
                    fs = slice(f * P, (f + 1) * P)
                    products(out, [((t[wt + "_hi"][:, k, fs], t[wt + "_lo"][:, k, fs]),
                                    (xT_hi[:, k, :], xT_lo[:, k, :])) for k in range(2)], True, False)
                    for k in range(2):
                        last = lora(w, k, f, 0, out, k == 1)
                last.then_inc(sem("f0"), 1)

            def second(c, f):
                need(pe, "gated", c, AT[f, 0] + 1)
                for w in range(2):
                    for k in range(2):
                        last = lora(w, k, f, 1, X[:, 2 * (f % 2) + w, :], k == 1)
                last.then_inc(sem("fd"), 1)

            def down(c, j):
                need(pe, "p_read", c, j + 1)
                js = slice(j * P, (j + 1) * P)
                out = X[:, BANKS[j], 0:D]
                products(out, [((gc_hi[:, f, js], gc_lo[:, f, js]), (t["W2_hi"][:, f, :], t["W2_lo"][:, f, :]))
                               for f in range(FT)], True, False)
                need(pe, "m_lo", c, 2)
                products(out, [((m_hi[:, k, js], m_lo[:, k, js]), (t["B2_hi"][:, k, :], t["B2_lo"][:, k, :]))
                               for k in range(2)], False, True).then_inc(sem("down"), 1)

            def main(c, s):
                if s == 0:
                    need(pe, "x_lo", c, 1)
                    need(pe, "x_hi", c, 1)
                    need(pe, "out_sb", c, 0)
                    for q in range(4):
                        wt, es = ("A1", "A3")[q // 2], slice(q % 2 * P, (q % 2 + 1) * P)
                        products(X[:, q, :], [((t[wt + "_hi"][:, k, es], t[wt + "_lo"][:, k, es]),
                                               (xT_hi[:, k, :], xT_lo[:, k, :])) for k in range(2)], True, True
                                 ).then_inc(sem("a_ps"), 1)
                    first(c, 0)
                elif s < FT:
                    first(c, s)
                    second(c, s - 1)
                elif s == FT:
                    second(c, s - 1)

            def back(c, q):
                if q < 2:
                    need(pe, "gated", c, AT[FT - 2, 1] + 1)
                else:
                    need(pe, "gated", c, 2 * FT)
                es = slice(q // 2 * P, (q // 2 + 1) * P)
                hi, lo = (g1_hi, g1_lo) if q % 2 else (gc_hi, gc_lo)
                for f in range(FT):
                    if q < 2:
                        need(pe, "g1_lo" if q % 2 else "gc_lo", c, f + 1)
                    last = products(X[:, BANKS[q], :], [((t["A2_hi"][:, f, es], t["A2_lo"][:, f, es]),
                                                         (hi[:, f, :], lo[:, f, :]))], f == 0, f == FT - 1)
                last.then_inc(sem("p_ps"), 1)

            def up(c, j):
                if j == 0:
                    need(pe, "xqT", c, 1)
                    need(pe, "xTf", c, 0)
                    need(pe, "spread", c, 0)
                need(pe, "gelu", c, j)
                for n in range(2):
                    for k in range(2):
                        last = mm(Y[:, 1 + n, :], xqT[:, k, j * P:(j + 1) * P], t["w1T"][:, k, n * 512:(n + 1) * 512],
                                  start=(k == 0), stop=(k == 1))
                last.then_inc(sem("hp"), 1)

            def second_product(c, j):
                need(pe, "hq", c, j + 1)
                need(pe, "hqT", c, j)
                if j == 0:
                    need(pe, "spread", c, 0)
                for n in range(8):
                    last = nc.tensor.transpose(Y3b[:, n * P:(n + 1) * P], hq[:, j % 2, n * P:(n + 1) * P], identb[:, :])
                last.then_inc(sem("hqT_ps"), 1)
                need(pe, "hqT", c, j + 1)
                need(pe, "xqT" if j == 0 else "y2", c, max(j, 1))
                for n in range(8):
                    last = mm(Y[:, 0, 0:D], hqT[:, n, :], t["w2T"][:, n, :], start=(n == 0), stop=(n == 7))
                last.then_inc(sem("y"), 1)

            def pre(c, s):
                if s == 0:
                    need(pe, "xq", c, 1)
                    need(pe, "gT", c, 0)
                    for k in range(2):
                        for j in range(CT):
                            last = nc.tensor.transpose(Y0b[:, (k * CT + j) * P:(k * CT + j + 1) * P],
                                                       xq[:, j, k * P:(k + 1) * P], identb[:, :])
                    last.then_inc(sem("xqT_ps"), 1)
                if 1 <= s <= 4:
                    up(c, s - 1)
                if 2 <= s <= 5:
                    second_product(c, s - 2)

            def turn_z(c):
                need(pe, "z", c, 1)
                need(pe, "gelu", c, 4)
                for k in range(2):
                    for j in range(CT):
                        last = nc.tensor.transpose(Y[:, 1 + k, j * P:(j + 1) * P], y4[:, j, k * P:(k + 1) * P], ident[:, :])
                last.then_inc(sem("zT"), 1)

            def route(c):
                need(pe, "xTf", c, 1)
                need(pe, "y2", c, 4)
                for j in range(CT):
                    for k in range(2):
                        last = mm(Y[:, 0, j * E:(j + 1) * E], xTf[:, k, j * P:(j + 1) * P], t["WgT"][:, k, :],
                                  start=(k == 0), stop=(k == 1), skip_group_check=True)
                last.then_inc(sem("logits_ps"), 1)

            def turn_routing(c):
                need(pe, "routing", c, 1)
                need(pe, "logits", c, 1)
                for j in range(CT):
                    last = nc.tensor.transpose(Y0b[0:32, j * P:(j + 1) * P], gpack[:, j, :], identb[:, :])
                last.then_inc(sem("gT_ps"), 1)

            def spread(c):
                need(pe, "gT", c, 1)
                need(pe, "hqT", c, 4)
                need(pe, "xTf", c, 1)
                for v in range(6):
                    if v >= 2:
                        need(pe, "spread", c, v - 1)
                    mm(Y[:, 2 + v % 2, :], sel[:, v, :], gT[:, :], start=True, stop=True).then_inc(sem("spread_ps"), 1)

            def step(c, e):
                for s in range(FT + 1):
                    if c is not None:
                        main(c, s)
                    if e is not None:
                        pre(e, s)
                if c is not None:
                    back(c, 0)
                    back(c, 1)
                if e is not None:
                    turn_z(e)
                if c is not None:
                    back(c, 2)
                if e is not None:
                    route(e)
                if c is not None:
                    back(c, 3)
                    down(c, 0)
                if e is not None:
                    turn_routing(e)
                if c is not None:
                    down(c, 1)
                if e is not None:
                    spread(e)
                if c is not None:
                    down(c, 2)
                    down(c, 3)

            run(pe, step)


def load_x(nc, t):
    with ExitStack() as ctx:
        x_in = ctx.enter_context(nc.semaphore("x_in"))
        block = ctx.enter_context(nc.Block())

        @block.sync
        def _(sp):
            sp.dma_start(t["x"][:, :, :], t["x_dram"]).then_inc(x_in, 16)
            sp.wait_ge(x_in, 16)


def store_x(nc, t):
    with ExitStack() as ctx:
        x_out = ctx.enter_context(nc.semaphore("x_out"))
        block = ctx.enter_context(nc.Block())

        @block.sync
        def _(sp):
            sp.dma_start(t["out_dram"], t["x"][:, :, :]).then_inc(x_out, 16)
            sp.wait_ge(x_out, 16)


def program(nc, a, out, stages=3):
    with ExitStack() as ctx:
        def sb(name, shape, dt=F32):
            return ctx.enter_context(nc.sbuf_tensor(name, shape, dt))

        t = {"passed": ctx.enter_context(nc.semaphore("passed"))}
        t |= {"x": sb("x", [P, TILES, D]), "ident": sb("ident", [P, P]), "identb": sb("identb", [P, P], BF16)}
        t |= {"g": sb("g", [P, 8]), "tanh": sb("tanh", [P, 4]), "gain0": sb("gain0", [P, 1])}
        t |= {"mean1": sb("mean1", [P, 1]), "mean2": sb("mean2", [P, 1])}
        t |= {"gamma": sb("gamma", [P, D]), "beta": sb("beta", [P, D]), "WgT": sb("WgT", [P, 2, E])}
        for n, shape in (("W1", [P, 2, F]), ("W3", [P, 2, F]), ("B1", [P, 2, F]), ("B3", [P, 2, F]),
                         ("A1", [P, 2, ER]), ("A3", [P, 2, ER]), ("B2", [P, 2, D]), ("W2", [P, FT, D]), ("A2", [P, FT, ER])):
            t[n + "_hi"] = sb(n + "_hi", shape, BF16)
            t[n + "_lo"] = sb(n + "_lo", shape, BF16)
        t["w1T"] = sb("w1T", [P, 2, F1], BF16)
        t["w2T"] = sb("w2T", [P, F1 // P, D], BF16)

        def tiles_of(ap):
            return ap.rearrange("(n b) s d -> (b s) n d", b=2)

        def rows(ap):
            return ap.rearrange("(n p) d -> p n d", p=P)

        def column(ap, n):
            return ap.unsqueeze(0).to_broadcast([P, n])

        t["x_dram"], t["ctx_dram"], t["out_dram"] = tiles_of(a["x"]), tiles_of(a["ctx_2048"]), tiles_of(out)
        t["g_xattn_dram"], t["g_ffn_dram"] = column(a["g_xattn"], 2), column(a["g_ffn"], 2)
        t["gamma0_dram"] = column(a["L0_xattn_gamma"], 1)
        t["decay_dram"] = column(a["L1_xattn_decay"], 1)
        t["w1_dram"], t["w2_dram"] = rows(a["L0_ffn_w1"]), rows(a["L0_ffn_w2"])
        for n in ("W1", "W3", "W2"):
            t[n + "_dram"] = rows(a["L1_ffn_" + n])
        for n in ("A1", "A3", "A2"):
            t[n + "_dram"] = a["L1_ffn_" + n].rearrange("e r h -> (e r) h").rearrange("(n p) h -> p n h", p=P)
        for n in ("B1", "B3", "B2"):
            b = a["L1_ffn_" + n].rearrange("e (n p) r -> n p e r", p=P)
            t[n + "_dram"] = [b[i] for i in range(2 if n == "B2" else FT)]
        t["Win_dram"], t["Wout_dram"] = rows(a["L1_xattn_W_in"]), rows(a["L1_xattn_W_out"])
        t["b_in_dram"] = a["L1_xattn_b_in"].rearrange("(n p) -> p n", p=P)
        t["b_out_dram"] = a["L1_xattn_b_out"].unsqueeze(0)
        t["Wg_dram"] = a["L1_ffn_Wg"]
        t["gamma_dram"], t["beta_dram"] = column(a["L1_xattn_gamma"], D), column(a["L1_xattn_beta"], D)
        t["summ_dram"] = nc.dram_tensor("summaries", (NB, D), F32, kind="Internal").ap()
        t["q_parts_dram"] = nc.dram_tensor("q_parts_scratch", (2, 3, DH, 2 * HEADS, D), BF16, kind="Internal").ap()
        t["k_parts_dram"] = nc.dram_tensor("k_parts_scratch", (2, 5, DH, 2 * HEADS, D), BF16, kind="Internal").ap()
        t["pv_dram"] = nc.dram_tensor("pv_scratch", (2, 2, 2, P, D), F32, kind="Internal").ap()

        def k_windows(u, h):
            rows = t["k_parts_dram"][u, :, :, h * 8:h * 8 + 8, :].rearrange("a d h l -> (a d) (h l)")
            return bass.AP(rows.tensor, rows.offset, [[8 * 2 * HEADS * D, 3], [2 * HEADS * D, 24], [1, HEADS * D]])

        t["k_windows"] = k_windows
        with ExitStack() as early:
            t["ctx"] = early.enter_context(nc.sbuf_tensor("ctx", [P, TILES, D], F32))
            load_x(nc, t)
            with ExitStack() as own:
                turned = {n: own.enter_context(nc.sbuf_tensor(n + "T", [P, 2, D], F32)) for n in ("Win", "Wout")}
                prepare(nc, t, turned)
            if stages >= 2:
                attention(nc, t)
        if stages >= 3:
            tokens(nc, t)
        else:
            store_x(nc, t)


_INS = ["x", "ctx_2048", "g_xattn", "g_ffn", "L0_xattn_gamma", "L0_ffn_w1", "L0_ffn_w2", "L1_xattn_decay",
        "L1_xattn_W_in", "L1_xattn_b_in", "L1_xattn_W_out", "L1_xattn_b_out", "L1_xattn_gamma", "L1_xattn_beta",
        "L1_ffn_Wg", "L1_ffn_W1", "L1_ffn_W2", "L1_ffn_W3", "L1_ffn_A1", "L1_ffn_B1", "L1_ffn_A2", "L1_ffn_B2",
        "L1_ffn_A3", "L1_ffn_B3"]


def kernel(**inputs):
    import numpy as _np
    import concourse.bacc as _bacc
    from concourse import mybir as _mybir
    from concourse.bass_utils import run_bass_kernel_spmd as _run

    nc = _bacc.Bacc("TRN2", target_bir_lowering=False, num_devices=1)
    arrays, args = {}, {}
    for name in _INS:
        a = _np.ascontiguousarray(inputs[name])
        if a.ndim == 0:
            a = a.reshape(1)
        arrays[f"in_{name}_dram"] = a
        args[name] = nc.dram_tensor(f"in_{name}_dram", a.shape, _mybir.dt.from_np(a.dtype), kind="ExternalInput").ap()
    out = nc.dram_tensor("out_dram", (NB, S, D), F32, kind="ExternalOutput").ap()
    program(nc, args, out)
    r = _run(nc, [arrays], core_ids=[0])
    return r.results[0]["out_dram"]
```

```python
from contextlib import ExitStack

import concourse.bass as bass
from concourse import mybir

ALU = mybir.AluOpType
ACT = mybir.ActivationFunctionType
AX = mybir.AxisListType
BF16 = mybir.dt.bfloat16
F32 = mybir.dt.float32
U32 = mybir.dt.uint32

P = 128
NB, S, D = 64, 64, 256
TILES = NB * S // P
HEADS, DH = 8, 8
HALVES = 2 * TILES
F1 = 1024
F, E, R = 896, 8, 32
FT = F // P
ER = E * R
ROUND = 1.5 * 2.0**23
EPS = 1e-5


class Sems:

    def __init__(self, nc, ctx, prefix):
        self.nc, self.ctx, self.prefix, self.made = nc, ctx, prefix, {}

    def __call__(self, name):
        if name not in self.made:
            self.made[name] = self.ctx.enter_context(self.nc.semaphore(f"{self.prefix}_{name}"))
        return self.made[name]


def at_least(eng, sem, value, passed=None):
    if not isinstance(value, int) or value > 0:
        eng.wait_ge(sem, value)
        if passed is not None and not isinstance(value, int):
            eng.sem_inc(passed, 1)


def prepare(nc, t, sb_out):
    with ExitStack() as ctx:
        sem = Sems(nc, ctx, "prep")

        def sb(name, shape, dt=F32):
            return ctx.enter_context(nc.sbuf_tensor(name, shape, dt))

        nat = {n: sb(f"nat_{n}", [P, FT, D]) for n in ("W1", "W3", "B1", "B3")}
        nat |= {n: sb(f"nat_{n}", [P, 2, D]) for n in ("A1", "A3", "B2", "Win", "Wout")}
        nat |= {n: sb(f"nat_{n}", [P, 2, F]) for n in ("W2", "A2")}
        nat["w1"] = sb("nat_w1", [P, 8, D])
        nat["w2"] = sb("nat_w2", [P, 2, F1])
        nat_Wg = sb("nat_Wg", [E, D])
        tern = sb("tern", [P, 8 * D], BF16)
        tern1 = tern[:, :].rearrange("p (a b) -> p a b", b=D)
        tern2 = tern[:, :].rearrange("p (a b) -> p a b", b=F1)
        ones = sb("ones", [P, P])
        part = sb("part", [P, 8])
        powers = sb("powers", [P, 2, S])
        decays = sb("decays", [P, S])
        unit = sb("unit", [P, 2, S])
        wide = sb("wide", [P, 126])
        kvs = sb("kvs", [NB, D])
        kvsT = sb("kvsT", [P, 2, NB])
        uT = sb("uT", [P, 2, NB])
        bcol = sb("bcol", [P, 2])
        brow = sb("brow", [1, D])
        summ = sb("summ", [NB, D])
        tmp = sb("tmp", [P, 16])

        def psum(name, shape, dt=F32):
            return ctx.enter_context(nc.psum_tensor(name, shape, dt))

        turn = psum("turn", [P, 4, 512])
        turnb = psum("turnb", [P, 2, 1024], BF16)
        small = psum("small", [P, 512])
        acc = psum("acc", [P, 512])
        ident, identb = t["ident"], t["identb"]

        groups = []
        for n in ("W1", "W3", "B1", "B3"):
            hi, lo = t[n + "_hi"], t[n + "_lo"]
            for k in range(2):
                for f0, f1 in ((0, 4), (4, 7)):
                    groups.append((n, [nat[n][:, f, k * P:(k + 1) * P] for f in range(f0, f1)],
                                   hi[:, k, f0 * P:f1 * P], lo[:, k, f0 * P:f1 * P]))
        for n in ("A1", "A3", "B2"):
            groups.append((n, [nat[n][:, m, k * P:(k + 1) * P] for k in range(2) for m in range(2)],
                           t[n + "_hi"][:, :, :].rearrange("p a b -> p (a b)"),
                           t[n + "_lo"][:, :, :].rearrange("p a b -> p (a b)")))
        for n in ("W2", "A2"):
            for f0, f1 in ((0, 2), (2, 4), (4, 6), (6, 7)):
                groups.append((n, [nat[n][:, m, f * P:(f + 1) * P] for f in range(f0, f1) for m in range(2)],
                               t[n + "_hi"][:, f0:f1, :].rearrange("p a b -> p (a b)"),
                               t[n + "_lo"][:, f0:f1, :].rearrange("p a b -> p (a b)")))
        for n in ("Win", "Wout"):
            groups.append((n, [nat[n][:, m, k * P:(k + 1) * P] for k in range(2) for m in range(2)],
                           sb_out[n][:, :, :].rearrange("p a b -> p (a b)"), None))
        NG = len(groups)

        block = ctx.enter_context(nc.Block())

        @block.sync
        def _(sp):
            def load(dst, src, name):
                sp.dma_start(dst, src).then_inc(sem("in_" + name), 16)

            load(t["ctx"][:, :, :], t["ctx_dram"], "ctx")
            load(t["g"][:, 0:2], t["g_xattn_dram"], "gains")
            load(t["g"][:, 2:4], t["g_ffn_dram"], "gains")
            load(t["g"][:, 4:5], t["gamma0_dram"], "gains")
            load(t["g"][:, 5:6], t["decay_dram"], "gains")
            load(nat["w1"][:, :, :], t["w1_dram"], "w1")
            load(nat["w2"][:, :, :], t["w2_dram"], "w2")
            for n in ("W1", "W3", "W2", "A1", "A3", "A2", "Win", "Wout"):
                load(nat[n][:, :, :], t[n + "_dram"], n)
            for n in ("B1", "B3"):
                for f in range(FT):
                    load(nat[n][:, f, :].rearrange("p (e r) -> p e r", e=E), t[n + "_dram"][f], n)
            for m in range(2):
                load(nat["B2"][:, m, :].rearrange("p (e r) -> p e r", e=E), t["B2_dram"][m], "B2")
            sp.dma_start(bcol[:, :], t["b_in_dram"], allow_slow_non_contiguous=True).then_inc(sem("in_rest"), 16)
            load(brow[:, :], t["b_out_dram"], "rest")
            load(nat_Wg[:, :], t["Wg_dram"], "rest")
            load(t["gamma"][:, :], t["gamma_dram"], "rest")
            load(t["beta"][:, :], t["beta_dram"], "rest")
            sp.wait_ge(sem("summ"), 1)
            sp.dma_start(t["summ_dram"], summ[:, :]).then_inc(sem("summ_out"), 16)
            sp.wait_ge(sem("summ_out"), 16)
            sp.wait_ge(sem("in_rest"), 80)

        @block.gpsimd
        def _(pool):
            nc.gpsimd.memset(ones[:, :], 1.0).then_inc(sem("ones"), 1)
            nc.gpsimd.memset(unit[:, :, :], 1.0).then_inc(sem("pm"), 1)
            nc.gpsimd.memset(wide[:, :], 0.0).then_inc(sem("wide0"), 1)
            pool.wait_ge(sem("ones"), 1)
            nc.gpsimd.affine_select(out=ident[:, :], in_=ones[:, :], compare_op=ALU.is_equal, fill=0.0,
                                    base=0, pattern=[[-1, P]], channel_multiplier=1).then_inc(sem("ident"), 1)
            pool.wait_ge(sem("ident"), 1)
            nc.gpsimd.tensor_copy(identb[:, :], ident[:, :]).then_inc(sem("ident"), 1)
            pool.wait_ge(sem("pm"), 1)
            nc.gpsimd.affine_select(out=powers[:, :, :], in_=unit[:, :, :], compare_op=ALU.is_equal, fill=0.0,
                                    base=-(S - 1), pattern=[[-S, 2], [1, S]],
                                    channel_multiplier=1).then_inc(sem("pm"), 1)

        @block.scalar
        def _(act):
            act.wait_ge(sem("in_gains"), 64)
            nc.scalar.activation(t["tanh"][:, 0:4], t["g"][:, 0:4], ACT.Tanh).then_inc(sem("tanh"), 1)
            nc.scalar.activation(tmp[:, 0:1], t["g"][:, 5:6], ACT.Exp, scale=-1.0).then_inc(sem("expd"), 1)
            for i, (n, tiles, hi, lo) in enumerate(groups):
                act.wait_ge(sem("turned"), i + 1)
                nc.scalar.copy(hi, turn[:, i % 4, 0:len(tiles) * P]).then_inc(sem("hi"), 1)

        @block.vector
        def _(dve):
            count = [0]

            def link(ins):
                count[0] += 1
                ins.then_inc(sem("dve"), 1)
                dve.wait_ge(sem("dve"), count[0])

            dve.wait_ge(sem("tanh"), 1)
            nc.vector.tensor_tensor(t["gain0"][:, :], t["tanh"][:, 0:1], t["g"][:, 4:5], ALU.mult).then_inc(sem("gain0"), 1)
            dve.wait_ge(sem("expd"), 1)
            link(nc.vector.tensor_scalar(tmp[:, 1:2], tmp[:, 0:1], 1.0, None, ALU.add))
            link(nc.vector.reciprocal(tmp[:, 2:3], tmp[:, 1:2]))
            dve.wait_ge(sem("pm"), 2)
            link(nc.vector.tensor_scalar(decays[:, :], unit[:, 0, :], tmp[:, 2:3], None, ALU.mult))
            link(nc.vector.tensor_tensor_scan(decays[:, :], decays[:, :], unit[:, 0, :], 0.0, ALU.mult, ALU.add))
            link(nc.vector.tensor_reduce(tmp[:, 3:4], decays[:, :], AX.X, ALU.add))
            link(nc.vector.tensor_scalar(tmp[:, 4:5], tmp[:, 3:4], 1.0 / S, None, ALU.mult))
            for b in range(2):
                link(nc.vector.tensor_tensor(powers[:, b, :], powers[:, b, :], decays[:, :], ALU.mult))
            link(nc.vector.tensor_reduce(tmp[:, 5:7], powers[:, :, :], AX.X, ALU.add))
            dve.wait_ge(sem("wide0"), 1)
            nc.vector.tensor_scalar(wide[:, 62:64], tmp[:, 5:7], 1.0 / S, None, ALU.mult).then_inc(sem("wide"), 1)
            for j, (n, dst, out) in enumerate((("w1", t["mean1"], tern1), ("w2", t["mean2"], tern2))):
                dve.wait_ge(sem("in_" + n), 16)
                link(nc.vector.tensor_reduce(part[:, j:j + 1], nat[n][:, :, :], AX.XY, ALU.add,
                                             apply_absolute_value=True))
                count[0] += 1
                nc.vector.tensor_copy(part[:, 2 + j:3 + j], part[:, j:j + 1]).then_inc(sem("dve"), 1)
                dve.wait_ge(sem("dve"), count[0])
                nc.vector.tensor_copy(part[:, 4 + j:5 + j], part[:, j:j + 1]).then_inc(sem("wsum"), 1)
                dve.wait_ge(sem("total"), j + 1)
                link(nc.vector.tensor_scalar(dst[:, :], small[:, j:j + 1], 1.0 / (F1 * D), EPS, ALU.mult, ALU.max))
                link(nc.vector.reciprocal(tmp[:, 8 + j:9 + j], dst[:, :]))
                link(nc.vector.tensor_scalar(nat[n][:, :, :], nat[n][:, :, :], tmp[:, 8 + j:9 + j], ROUND, ALU.mult, ALU.add))
                link(nc.vector.tensor_scalar(nat[n][:, :, :], nat[n][:, :, :], -ROUND, 1.0, ALU.add, ALU.min))
                if j == 1:
                    dve.wait_ge(sem("turnedb"), 2)
                nc.vector.tensor_scalar(out[:, :, :], nat[n][:, :, :], -1.0, None, ALU.max).then_inc(sem("tern"), 1)
            for i in range(4):
                dve.wait_ge(sem("turnedb"), i + 1)
                dst = t["w1T"] if i < 2 else t["w2T"]
                flat = dst[:, :, :].rearrange("p a b -> p (a b)")[:, (i % 2) * 1024:(i % 2 + 1) * 1024]
                nc.vector.tensor_copy(flat, turnb[:, i % 2, :]).then_inc(sem("ternT"), 1)
            for i, (n, tiles, hi, lo) in enumerate(groups):
                dve.wait_ge(sem("hi"), i + 1)
                if lo is not None:
                    nc.vector.tensor_tensor(lo, turn[:, i % 4, 0:len(tiles) * P], hi, ALU.subtract).then_inc(sem("lo"), 1)
                else:
                    nc.vector.tensor_copy(tmp[:, 10:11], tmp[:, 8:9]).then_inc(sem("lo"), 1)
                    dve.wait_ge(sem("lo"), i + 1)
            dve.wait_ge(sem("WgT"), 1)
            nc.vector.tensor_copy(t["WgT"][:, :, :], small[:, 400:416].rearrange("p (a b) -> p a b", a=2)).then_inc(sem("WgT_sb"), 1)
            dve.wait_ge(sem("kvs"), 1)
            nc.vector.tensor_copy(kvs[:, :], acc[0:NB, 0:D]).then_inc(sem("kvs_sb"), 1)
            dve.wait_ge(sem("kvsT"), 1)
            nc.vector.tensor_copy(kvsT[:, :, :], small[:, 128:256].rearrange("p (a b) -> p a b", a=2)).then_inc(sem("kvsT_sb"), 1)
            dve.wait_ge(sem("in_rest"), 80)
            link(nc.vector.tensor_scalar(bcol[:, :], bcol[:, :], tmp[:, 4:5], None, ALU.mult))
            for n in ("gamma", "beta"):
                nc.vector.tensor_scalar(t[n][:, :], t[n][:, :], t["tanh"][:, 1:2], None, ALU.mult).then_inc(sem("gb"), 1)
            dve.wait_ge(sem("u"), 1)
            for m in range(2):
                nc.vector.tensor_scalar(uT[:, m, :], small[:, 256 + 64 * m:320 + 64 * m], bcol[:, m:m + 1], None,
                                        ALU.add).then_inc(sem("u_sb"), 1)
            dve.wait_ge(sem("s"), 1)
            nc.vector.tensor_copy(summ[:, :], acc[0:NB, D:2 * D]).then_inc(sem("summ"), 1)

        @block.tensor
        def _(pe):
            pe.wait_ge(sem("ident"), 2)
            pe.wait_ge(sem("wide"), 1)
            pe.wait_ge(sem("in_ctx"), 16)
            for i in range(TILES):
                last = nc.tensor.matmul(acc[0:NB, 0:D], wide[:, 62 - 2 * i:126 - 2 * i], t["ctx"][:, i, :],
                                        start=(i == 0), stop=(i == TILES - 1))
            last.then_inc(sem("kvs"), 1)
            for j in range(2):
                pe.wait_ge(sem("wsum"), j + 1)
                nc.tensor.matmul(small[:, j:j + 1], ones[:, :], part[:, 4 + j:5 + j], start=True, stop=True
                                 ).then_inc(sem("total"), 1)
            for i in range(4):
                pe.wait_ge(sem("tern"), 1 + i // 2)
                if i >= 2:
                    pe.wait_ge(sem("ternT"), i - 1)
                for c in range(8):
                    if i < 2:
                        src = tern1[:, c, i * P:(i + 1) * P]
                    else:
                        f, m = divmod(8 * (i - 2) + c, 2)
                        src = tern2[:, m, f * P:(f + 1) * P]
                    last = nc.tensor.transpose(turnb[:, i % 2, c * P:(c + 1) * P], src, identb[:, :])
                last.then_inc(sem("turnedb"), 1)
            for i, (n, tiles, hi, lo) in enumerate(groups):
                pe.wait_ge(sem("in_" + n), {"B1": 16 * FT, "B3": 16 * FT, "B2": 32}.get(n, 16))
                if i >= 4:
                    pe.wait_ge(sem("lo"), i - 3)
                for c, src in enumerate(tiles):
                    last = nc.tensor.transpose(turn[:, i % 4, c * P:(c + 1) * P], src, ident[:, :])
                last.then_inc(sem("turned"), 1)
            pe.wait_ge(sem("in_rest"), 80)
            for m in range(2):
                last = nc.tensor.transpose(small[:, 400 + 8 * m:408 + 8 * m], nat_Wg[:, m * P:(m + 1) * P], ident[0:E, 0:E])
            last.then_inc(sem("WgT"), 1)
            pe.wait_ge(sem("kvs_sb"), 1)
            for m in range(2):
                last = nc.tensor.transpose(small[:, 128 + 64 * m:192 + 64 * m], kvs[:, m * P:(m + 1) * P], ident[0:NB, 0:NB])
            last.then_inc(sem("kvsT"), 1)
            pe.wait_ge(sem("kvsT_sb"), 1)
            pe.wait_ge(sem("hi"), NG)
            for m in range(2):
                for k in range(2):
                    last = nc.tensor.matmul(small[:, 256 + 64 * m:320 + 64 * m], sb_out["Win"][:, k, m * P:(m + 1) * P],
                                            kvsT[:, k, :], start=(k == 0), stop=(k == 1))
            last.then_inc(sem("u"), 1)
            pe.wait_ge(sem("u_sb"), 2)
            for k in range(2):
                nc.tensor.matmul(acc[0:NB, D:2 * D], uT[:, k, :], sb_out["Wout"][:, k, :], start=(k == 0), stop=False)
            nc.tensor.matmul(acc[0:NB, D:2 * D], ones[0:1, 0:NB], brow[:, :], start=False, stop=True).then_inc(sem("s"), 1)


class Step:

    def __init__(self, i, s):
        self.i, self.s = i, s
        self.static = isinstance(i, int)

    def half(self, k=0):
        return self.i * 4 + (self.s + k)

    def quarter(self, k=0):
        return self.i + (self.s + k) // 4

    def tile(self, k=0):
        return self.i * 2 + (self.s + k) // 2

    def slot(self, k=0, m=4):
        return (self.s + k) % m

    def in_range(self, k, n=HALVES):
        return not self.static or 0 <= 4 * self.i + self.s + k < n


def attention(nc, t):
    with ExitStack() as ctx:
        sem = Sems(nc, ctx, "att")

        def sb(name, shape, dt=F32):
            return ctx.enter_context(nc.sbuf_tensor(name, shape, dt))

        def psum(name, shape, dt=F32):
            return ctx.enter_context(nc.psum_tensor(name, shape, dt))

        q_pack = sb("q_pack", [P, 4, HEADS, D], BF16)
        k_pack = sb("k_pack", [P, 4, HEADS, D], BF16)
        q_parts = sb("q_parts", [P, 2, 3, D], BF16)
        k_parts = sb("k_parts", [P, 2, 3, D], BF16)
        z = sb("z", [P, 2, D])
        q_rest = sb("q_rest", [P, D])
        k_rest = sb("k_rest", [P, D])
        probs = sb("probs", [P, HEADS, 2, D])
        vT = sb("vT", [P, 2, 2, 2 * HEADS, 32])
        pv_sb = sb("pv_sb", [P, 2, 2, D])
        nd = sb("nd", [P, 2, 2, D])
        stat6 = sb("stat6", [P, 6])
        mean_var = sb("mean_var", [P, 2, 2])
        rstd = sb("rstd", [P, 2, 2])
        half_neg = sb("half_neg", [P, 1])
        neg_max = sb("neg_max", [P, 2, HEADS, 2])
        neg_rest = sb("neg_rest", [P, 2 * HEADS])
        neg_parts = sb("neg_parts", [P, 2, 3, 2 * HEADS], BF16)
        neg_rows = sb("neg_rows", [3 * 2 * HEADS, 2, P], BF16)

        s1 = psum("s1", [P, 4, 512])
        s2 = psum("s2", [P, 2, 512])
        pv = psum("pv", [P, 2, D])
        misc = psum("misc", [P, 512])
        negT = misc[0:48, 256:320].bitcast(BF16)

        xres, ctx_sb, identb = t["x"], t["ctx"], t["identb"]
        q_dram, k_dram, pv_dram = t["q_parts_dram"], t["k_parts_dram"], t["pv_dram"]
        SCALE = float(DH) ** -0.5

        first, last_step = -6, HALVES + 2
        LOOP = (1, (HALVES - 8) // 4)

        TURN_AT = 1
        NEG_AT = 3

        PV_AT = 2

        def run(eng, step):
            for n in range(first, 4 * LOOP[0]):
                step(Step(n // 4, n % 4))
            with eng.Fori(*LOOP) as i:
                for s in range(4):
                    step(Step(i, s))
            for n in range(4 * LOOP[1], last_step + 1):
                step(Step(n // 4, n % 4))

        block = ctx.enter_context(nc.Block())

        @block.sync
        def _(sp):
            def step(n):
                if n.in_range(3):
                    h, slot, u = n.slot(3, 2), n.slot(3), n.slot(3) // 2
                    at_least(sp, sem(f"parts_out{u}"), n.quarter(3) * 128 + 128, passed=t["passed"])
                    at_least(sp, sem("s2_done"), n.half(0) * 8, passed=t["passed"])
                    rows = q_dram[u, :, :, h * 8:h * 8 + 8, :].rearrange("a d h l -> (a d) (h l)")
                    sp.dma_start(q_pack[0:72, slot, :, :].rearrange("p h l -> p (h l)"),
                                 rows.unsqueeze(0).to_broadcast([3, 24, HEADS * D])).then_inc(sem(f"pack_in{slot}"), 16)
                    sp.dma_start(k_pack[0:72, slot, :, :].rearrange("p h l -> p (h l)"),
                                 t["k_windows"](u, h)).then_inc(sem(f"pack_in{slot}"), 16)
                if n.in_range(-1):
                    b, u = n.slot(-1, 2), n.slot(-1) // 2
                    at_least(sp, sem("pv_sb"), n.half(0), passed=t["passed"])
                    if b == 0:
                        at_least(sp, sem(f"nd_in{u}"), n.quarter(-1) * 32, passed=t["passed"])
                    sp.dma_start(pv_dram[u, b].rearrange("g p l -> p g l"), pv_sb[:, b, :, :]
                                 ).then_inc(sem(f"pv_out{b}"), 16)
                if n.s % 2 == 0 and n.in_range(4):
                    u = n.slot(4) // 2
                    at_least(sp, sem("q_parts"), n.tile(4) + 1, passed=t["passed"])
                    at_least(sp, sem("k_parts"), n.tile(4) + 1, passed=t["passed"])
                    for b in range(2):
                        at_least(sp, sem(f"pack_in{2 * u + b}"), n.quarter(4) * 32, passed=t["passed"])
                    for a in range(3):
                        sp.dma_start(q_dram[u, a].rearrange("d h l -> h d l"), q_parts[:, u, a, :]
                                     ).then_inc(sem(f"parts_out{u}"), 16)
                    for a in range(5):
                        sp.dma_start(k_dram[u, a].rearrange("d h l -> h d l"), k_parts[:, u, a % 3, :]
                                     ).then_inc(sem(f"parts_out{u}"), 16)
                if n.s % 2 == 1 and n.in_range(-3):
                    u = n.slot(-3) // 2
                    for b in range(2):
                        at_least(sp, sem(f"pv_out{b}"), n.tile(-3) * 16 + 16, passed=t["passed"])
                    at_least(sp, sem("x_done"), n.tile(-3), passed=t["passed"])
                    for k in range(2):
                        src = pv_dram[u].rearrange("b g (j r) l -> (b g j) r l", r=32)[:, 8 * k:8 * k + 8, :]
                        sp.dma_start(nd[:, u, k, :], src).then_inc(sem(f"nd_in{u}"), 16)

            run(sp, step)

        @block.gpsimd
        def _(pool):
            for tile_ in (q_pack, k_pack):
                nc.gpsimd.memset(tile_[:, :, :, :], 0.0).then_inc(sem("zeroed"), 1)
            nc.gpsimd.memset(vT[:, :, :, :, :], 0.0).then_inc(sem("zeroed"), 1)
            nc.gpsimd.memset(half_neg[:, :], -0.5).then_inc(sem("zeroed"), 1)
            pool.wait_ge(sem("zeroed"), 4)
            nc.gpsimd.memset(k_pack[96:99, :, :, :], 1.0).then_inc(sem("constants"), 1)
            pool.wait_ge(sem("constants"), 1)
            nc.gpsimd.memset(vT[:, :, :, :, 8:16], 1.0).then_inc(sem("constants"), 1)

            def step(n):
                if n.s % 2 == 0 and n.in_range(6):
                    T, u = n.tile(6), n.slot(6) // 2
                    at_least(pool, sem("mean_var"), T + 1, passed=t["passed"])
                    nc.gpsimd.tensor_scalar(rstd[:, u, 0:1], mean_var[:, u, 1:2], EPS, 1.0, ALU.add, ALU.mult
                                            ).then_inc(sem("var_eps"), 1)
                    at_least(pool, sem("var_eps"), T + 1, passed=t["passed"])
                    nc.gpsimd.tensor_tensor(rstd[:, u, 1:2], rstd[:, u, 0:1], half_neg[:, :], ALU.pow
                                            ).then_inc(sem("rstd"), 1)
                    at_least(pool, sem("z"), T + 1, passed=t["passed"])
                    at_least(pool, sem(f"parts_out{u}"), n.quarter(6) * 128, passed=t["passed"])
                    split(z[:, u, :], q_parts, q_rest, u, T, "q")
                if n.s % 2 == 1 and n.in_range(5):
                    T, u = n.tile(5), n.slot(5) // 2
                    at_least(pool, sem("vT_psum"), T - 1, passed=t["passed"])
                    at_least(pool, sem(f"parts_out{u}"), n.quarter(5) * 128, passed=t["passed"])
                    split(ctx_sb[:, bass.ds(T, 1), :].rearrange("p a l -> p (a l)"), k_parts, k_rest, u, T, "k")
                if n.s % 2 == 0 and n.in_range(-4):
                    T, u = n.tile(-4), n.slot(-4) // 2
                    row = xres[:, bass.ds(T, 1), :].rearrange("p a l -> p (a l)")
                    at_least(pool, sem("recip"), T * 2 + 2, passed=t["passed"])
                    nc.gpsimd.tensor_tensor(nd[:, u, 0, :], nd[:, u, 0, :], nd[:, u, 1, :], ALU.mult
                                            ).then_inc(sem("ratio"), 1)
                    at_least(pool, sem("ratio"), T + 1, passed=t["passed"])
                    nc.gpsimd.tensor_scalar(nd[:, u, 1, :], nd[:, u, 0, :], t["gain0"][:, :], 1.0, ALU.mult, ALU.mult
                                            ).then_inc(sem("gained"), 1)
                    at_least(pool, sem("gained"), T + 1, passed=t["passed"])
                    nc.gpsimd.tensor_tensor(row, row, nd[:, u, 1, :], ALU.add).then_inc(sem("x_done"), 1)

            def split(src, parts, rest, u, T, name):
                done = sem(name + "_split")
                nc.gpsimd.tensor_copy(parts[:, u, 0, :], src).then_inc(done, 1)
                at_least(pool, done, T * 3 + 1, passed=t["passed"])
                nc.gpsimd.tensor_tensor(rest[:, :], src, parts[:, u, 0, :], ALU.subtract).then_inc(done, 1)
                at_least(pool, done, T * 3 + 2, passed=t["passed"])
                nc.gpsimd.tensor_copy(parts[:, u, 1, :], rest[:, :]).then_inc(done, 1)
                at_least(pool, done, T * 3 + 3, passed=t["passed"])
                nc.gpsimd.tensor_tensor(parts[:, u, 2, :], rest[:, :], parts[:, u, 1, :], ALU.subtract
                                        ).then_inc(sem(name + "_parts"), 1)
                at_least(pool, sem(name + "_parts"), T + 1, passed=t["passed"])

            run(pool, step)
            pool.wait_ge(sem("x_done"), TILES)

        @block.scalar
        def _(act):
            def step(n):
                for hd in range(HEADS):
                    if n.in_range(0):
                        at_least(act, sem("s2_done"), n.half(0) * 8 + (hd + 1))
                        at_least(act, sem("pv_group"), n.half(0) * 2 + (hd // 4 - 1))
                        nc.scalar.activation(probs[:, hd, :, :].rearrange("p a q -> p (a q)"), s2[:, hd % 2, :],
                                             ACT.Exp, scale=SCALE).then_inc(sem("exp_done"), 1)
                    if hd == PV_AT and n.in_range(-1):
                        at_least(act, sem("pv_group"), n.half(0) * 2)
                        at_least(act, sem(f"pv_out{n.slot(-1, 2)}"), n.tile(-1) * 16)
                        nc.scalar.copy(pv_sb[:, n.slot(-1, 2), :, :], pv[:, :, :]).then_inc(sem("pv_sb"), 1)
                    if hd == NEG_AT and n.in_range(1):
                        at_least(act, sem("neg_rows"), n.half(2), passed=t["passed"])
                        act.dma_start(q_pack[96:99, n.slot(1), :, :], neg_rows[:, n.slot(1, 2), :]
                                      ).then_inc(sem(f"neg_in{n.slot(1, 2)}"), 16)
                    if hd == 7 and n.s % 2 == 1 and n.in_range(1):
                        T, u = n.tile(1), n.slot(1) // 2
                        at_least(act, sem("vT_psum"), T + 1)
                        at_least(act, sem("pv_group"), n.half(0) * 2 - 2)
                        if n.static:
                            at_least(act, sem("constants"), 2)
                        nc.scalar.copy(vT[:, u, :, :, 0:8], misc[:, 0:256].rearrange("p (a h d) -> p a h d", a=2, d=8)
                                       ).then_inc(sem("vT"), 1)

            run(act, step)

        @block.vector
        def _(dve):
            def step(n):
                for p in range(4):
                    if n.in_range(2):
                        at_least(dve, sem("s1_done"), n.half(2) * 4 + (p + 1))
                        if p == 0:
                            at_least(dve, sem("neg_parts"), n.half(1))
                        nc.vector.tensor_reduce(
                            neg_max[:, n.slot(0, 2), 2 * p:2 * p + 2, :],
                            s1[:, 2 * (p % 2):2 * (p % 2) + 2, :].rearrange("p a (b l) -> p a b l", b=2),
                            AX.X, ALU.max, negate=True).then_inc(sem("max_done"), 1)
                    if p == 0 and n.s % 2 == 0 and n.in_range(6):
                        T = n.tile(6)
                        row = xres[:, bass.ds(T, 1), :].rearrange("p a l -> p (a l)")
                        at_least(dve, sem("mean_var"), T, passed=t["passed"])
                        nc.vector.bn_stats(stat6[:, :], row).then_inc(sem("stats"), 1)
                    if p == 1 and n.s % 2 == 0 and n.in_range(6):
                        T, u = n.tile(6), n.slot(6) // 2
                        at_least(dve, sem("stats"), T + 1, passed=t["passed"])
                        at_least(dve, sem("z"), T - 1, passed=t["passed"])
                        nc.vector.bn_aggr(mean_var[:, u, :], stat6[:, :]).then_inc(sem("mean_var"), 1)
                    if p == TURN_AT // 2 and n.in_range(1):
                        at_least(dve, sem("negT"), n.half(2))
                        at_least(dve, sem(f"neg_in{n.slot(1, 2)}"), n.tile(1) * 16)
                        nc.vector.tensor_copy(neg_rows[:, n.slot(1, 2), :], negT).then_inc(sem("neg_rows"), 1)
                    if p in (1, 2) and n.s % 2 == 0 and n.in_range(-4):
                        T, u, half = n.tile(-4), n.slot(-4) // 2, slice((p - 1) * P, p * P)
                        at_least(dve, sem(f"nd_in{u}"), n.quarter(-4) * 32 + 32)
                        nc.vector.reciprocal(nd[:, u, 1, half], nd[:, u, 1, half]).then_inc(sem("recip"), 1)
                    if p == 3 and n.s % 2 == 0 and n.in_range(6):
                        T, u = n.tile(6), n.slot(6) // 2
                        row = xres[:, bass.ds(T, 1), :].rearrange("p a l -> p (a l)")
                        at_least(dve, sem("rstd"), T + 1)
                        at_least(dve, sem("q_parts"), T - 1)
                        nc.vector.tensor_scalar(z[:, u, :], row, mean_var[:, u, 0:1], rstd[:, u, 1:2],
                                                ALU.subtract, ALU.mult).then_inc(sem("z"), 1)
                if n.in_range(2):
                    b = n.slot(0, 2)
                    flat = neg_max[:, b, :, :].rearrange("p a b -> p (a b)")
                    h = n.half(2)
                    at_least(dve, sem("max_done"), h * 4 + 4)
                    at_least(dve, sem("negT"), h - 1)
                    nc.vector.tensor_copy(neg_parts[:, b, 0, :], flat).then_inc(sem("neg_split"), 1)
                    dve.wait_ge(sem("neg_split"), h * 3 + 1)
                    nc.vector.tensor_tensor(neg_rest[:, :], flat, neg_parts[:, b, 0, :], ALU.subtract
                                            ).then_inc(sem("neg_split"), 1)
                    dve.wait_ge(sem("neg_split"), h * 3 + 2)
                    nc.vector.tensor_copy(neg_parts[:, b, 1, :], neg_rest[:, :]).then_inc(sem("neg_split"), 1)
                    dve.wait_ge(sem("neg_split"), h * 3 + 3)
                    nc.vector.tensor_tensor(neg_parts[:, b, 2, :], neg_rest[:, :], neg_parts[:, b, 1, :], ALU.subtract
                                            ).then_inc(sem("neg_parts"), 1)

            run(dve, step)

        @block.tensor
        def _(pe):
            pe.wait_ge(sem("constants"), 2)

            def pv_group(n, k, g, a):
                if not n.in_range(k):
                    return
                b, u = n.slot(k, 2), n.slot(k) // 2
                if a == 0:
                    at_least(pe, sem("exp_done"), n.half(k) * 8 + (4 * g + 4))
                    if g == 0:
                        at_least(pe, sem("vT"), n.tile(k) + 1)
                        at_least(pe, sem("pv_sb"), n.half(k))
                for j in range(4):
                    last = nc.tensor.matmul(pv[32 * j:32 * j + 32, g, :], vT[:, u, a, 8 * b + 4 * g + j, :],
                                            probs[:, 4 * g + j, a, :], start=(a == 0), stop=(a == 1),
                                            skip_group_check=True)
                if a == 1:
                    last.then_inc(sem("pv_group"), 1)

            def step(n):
                for p in range(4):
                    if n.in_range(2):
                        slot = n.slot(2)
                        if p == 0:
                            at_least(pe, sem(f"pack_in{slot}"), n.quarter(2) * 32 + 32)
                        at_least(pe, sem("max_done"), n.half(2) * 4 + (p - 1))
                        for hd in (2 * p, 2 * p + 1):
                            for m in range(2):
                                last = nc.tensor.matmul(s1[:, 2 * (p % 2) + hd % 2, m * D:(m + 1) * D],
                                                        q_pack[0:96, slot, hd, m * P:(m + 1) * P],
                                                        k_pack[0:96, slot, hd, :], start=True, stop=True)
                        last.then_inc(sem("s1_done"), 1)
                    if p % 2 == 1:
                        pv_group(n, -1 if p == 1 else 0, 1 if p == 1 else 0, 1)
                    for hd in (2 * p, 2 * p + 1):
                        if n.in_range(0):
                            slot = n.slot(0)
                            if hd == 0:
                                at_least(pe, sem(f"neg_in{n.slot(0, 2)}"), n.tile(0) * 16 + 16)
                                at_least(pe, sem(f"pack_in{slot}"), n.quarter(0) * 32 + 32)
                            at_least(pe, sem("exp_done"), n.half(0) * 8 + (hd - 1))
                            for m in range(2):
                                last = nc.tensor.matmul(s2[:, hd % 2, m * D:(m + 1) * D],
                                                        k_pack[0:99, slot, hd, m * P:(m + 1) * P],
                                                        q_pack[0:99, slot, hd, :], start=True, stop=True)
                            last.then_inc(sem("s2_done"), 1)
                        if hd == TURN_AT:
                            if n.in_range(1):
                                at_least(pe, sem("neg_parts"), n.half(2), passed=t["passed"])
                                at_least(pe, sem("neg_rows"), n.half(1), passed=t["passed"])
                                at_least(pe, sem("vT"), n.tile(2), passed=t["passed"])
                                nc.tensor.transpose(negT, neg_parts[:, n.slot(1, 2), :, :].rearrange("p a b -> p (a b)"),
                                                    identb[:, :]).then_inc(sem("negT"), 1)
                        if hd == 0:
                            pv_group(n, -1, 1, 0)
                        if hd == 4:
                            pv_group(n, 0, 0, 0)
                    if p == 2 and n.s % 2 == 1 and n.in_range(1):
                        T, u = n.tile(1), n.slot(1) // 2
                        at_least(pe, sem("k_parts"), T + 1)
                        at_least(pe, sem("vT"), T)
                        at_least(pe, sem("neg_rows"), n.half(2))
                        for m in range(2):
                            for a in range(3):
                                last = nc.tensor.matmul(misc[:, m * P:(m + 1) * P], k_parts[:, u, a, m * P:(m + 1) * P],
                                                        identb[:, :], start=(a == 0), stop=(a == 2))
                        last.then_inc(sem("vT_psum"), 1)

            run(pe, step)


CT = 4
CHUNKS = TILES // CT
N = CT * P
TINY = EPS * 1e-12 / 32.0

PER = {
    "dve_pre": 48, "mv1": 1, "pow1": 1, "q_in": 1, "xq": 1, "xqT_ps": 1, "xqT": 1, "hp": 4, "gelu": 4, "ssq": 4,
    "absmax": 4, "hr": 4, "hq": 4, "hqT_ps": 4, "hqT": 4, "y": 4, "y2": 4, "norm2": 1, "pool_pre": 5, "mv2": 1,
    "rstd2": 1, "xm": 1, "ys": 1, "mv3": 1, "rstd3": 1, "xb": 1, "x3": 1, "mv4": 1, "rstd4": 1, "z": 1,
    "zT": 1, "xTf": 1, "x_hi": 1, "x_lo": 1, "logits_ps": 1, "logits": 1, "gap": 1, "exp_gap": 1, "routing": 1,
    "gT_ps": 1, "gT": 1, "spread_ps": 6, "spread": 6, "summ_in": 16 * CT,
    "a_ps": 4, "a_hi": 4, "a_lo": 4, "a_masked": 4, "f0": 7, "fd": 7, "silu": 14, "gated": 14, "weighted": 14,
    "mixed": 7, "g1_hi": 7, "gc_hi": 7, "g1_lo": 7, "gc_lo": 7, "p_ps": 4, "p_read": 4, "m_hi": 2, "m_lo": 2,
    "dve_main": 2, "down": 4, "out_sb": 4, "stored": 16,
}


def tokens(nc, t):
    with ExitStack() as ctx:
        sem = Sems(nc, ctx, "tok")

        def sb(name, shape, dt=F32):
            return ctx.enter_context(nc.sbuf_tensor(name, shape, dt))

        def psum(name, shape, dt=F32):
            return ctx.enter_context(nc.psum_tensor(name, shape, dt))

        def need(eng, name, c, k, apart=False):
            apart = apart or eng.engine in (nc.gpsimd.engine, nc.sync.engine)
            at_least(eng, sem(name), c * PER[name] + (PER[name] + k), passed=t["passed"] if apart else None)

        xres, identb, ident = t["x"], t["identb"], t["ident"]

        st6 = sb("st6", [P, CT, 6])
        mv = sb("mv", [P, CT, 2])
        sm = sb("sm", [P, 16, CT])
        powers = sb("exponents", [P, 3, CT])
        d4 = sb("d4", [P, CT, D])
        xq = sb("xq", [P, CT, D], BF16)
        xqT = sb("xqT", [P, 2, N], BF16)
        h = sb("h", [P, 2, F1])
        junk = sb("junk", [P, F1], BF16)
        hq = sb("hq", [P, 2, F1], BF16)
        hqT = sb("hqT", [P, 8, P], BF16)
        y2 = sb("y2", [P, CT, D])
        xTf = h[:, 0, :].rearrange("p (a b) -> p a b", b=N)
        summ = h[:, 1, :].rearrange("p (a b) -> p a b", b=D)
        y4 = d4
        xT_hi = sb("xT_hi", [P, 2, N], BF16)
        xT_lo = sb("xT_lo", [P, 2, N], BF16)
        logits = sb("logits", [P, CT, E])
        top = sb("top", [P, CT, 8])
        top_i = sb("top_i", [P, CT, 8], U32)
        top_f = sb("top_f", [P, CT, 2])
        experts = sb("experts", [P, CT, E])
        onehot = sb("onehot", [P, CT, E])
        rw = sb("rw", [P, CT, 2])
        rw_rest = sb("rw_rest", [P, CT, 2])
        gpack = sb("gpack", [P, CT, 32], BF16)
        gT = sb("gT", [32, N], BF16)
        sel = sb("sel", [32, 6, P], BF16)
        sel_ones = sb("sel_ones", [32, 4, P], BF16)
        mask = sb("mask", [P, 4, N], BF16)
        rw_rows = sb("rw_rows", [P, 2, N])

        a_hi = sb("a_hi", [P, 2, N], BF16)
        a_lo = sb("a_lo", [P, 2, N], BF16)
        am = sb("a_masked", [P, 4, 2, 2, N], BF16)
        sil = sb("sil", [P, 2, N])
        gated = sb("gated", [P, 2, N])
        w0 = sb("weighted0", [P, 2, N])
        w1 = sb("weighted1", [P, 2, N])
        wc = sb("mixed", [P, 2, N])
        g1_hi, g1_lo = sb("g1_hi", [P, FT, N], BF16), sb("g1_lo", [P, FT, N], BF16)
        gc_hi, gc_lo = sb("gc_hi", [P, FT, N], BF16), sb("gc_lo", [P, FT, N], BF16)
        pm = [sil[:, 0, :], sil[:, 1, :], gated[:, 0, :]]
        m_hi, m_lo = a_hi, a_lo
        out_sb = wc[:, :, :].rearrange("p a (b d) -> p (a b) d", d=D)

        X = psum("X", [P, 4, 512])
        Y = psum("Y", [P, 4, 512])
        Y0b = Y[:, 0, :].bitcast(BF16)
        Y3b = Y[:, 3, :].bitcast(BF16)
        BANKS = (2, 3, 0, 1)
        ORDER = [(0, 0)] + [o for f in range(1, FT) for o in ((f, 0), (f - 1, 1))] + [(FT - 1, 1)]
        AT = {o: n for n, o in enumerate(ORDER)}

        def xrow(c, j):
            return xres[:, bass.ds(c * CT + j, 1), :].rearrange("p a l -> p (a l)")

        def xchunk(c):
            return xres[:, bass.ds(c * CT, CT), :].rearrange("p a l -> p (a l)")

        def xchunk4(c):
            return xres[:, bass.ds(c * CT, CT), :]

        def flat(ap):
            return ap.rearrange("p a b -> p (a b)")

        block = ctx.enter_context(nc.Block())

        def run(eng, step):
            step(None, 0)
            with eng.Fori(0, CHUNKS - 1) as c:
                step(c, c + 1)
            step(CHUNKS - 1, None)

        @block.sync
        def _(sp):
            for name in PER:
                sp.sem_inc(sem(name), PER[name])

            def step(c, e):
                if e is not None:
                    need(sp, "hq", e, CT)
                    for j in range(CT):
                        src = t["summ_dram"][bass.ds((e * CT + j) * 2, 2), :].unsqueeze(1).to_broadcast([2, S, D])
                        sp.dma_start(summ[:, j, :], src).then_inc(sem("summ_in"), 16)
                if c is not None:
                    need(sp, "out_sb", c, CT)
                    sp.dma_start(t["out_dram"][:, bass.ds(c * CT, CT), :], out_sb[:, :, :]).then_inc(sem("stored"), 16)

            run(sp, step)
            need(sp, "stored", CHUNKS - 1, 16)

        @block.gpsimd
        def _(pool):
            consts = sem("consts")
            nc.gpsimd.memset(sel_ones[:, :, :], 1.0).then_inc(consts, 1)
            nc.gpsimd.memset(gpack[:, :, :], 0.0).then_inc(consts, 1)
            nc.gpsimd.iota(top_i[:, :, :], pattern=[[0, CT], [1, E]], base=0, channel_multiplier=0).then_inc(consts, 1)
            pool.wait_ge(consts, 3)
            nc.gpsimd.tensor_copy(experts[:, :, :], top_i[:, :, :]).then_inc(consts, 1)
            nc.gpsimd.affine_select(
                out=sel[:, 0:4, :].rearrange("p (a b) (m r) -> p a b m r", a=2, m=4),
                in_=sel_ones[:, :, :].rearrange("p (a b) (m r) -> p a b m r", a=2, m=4),
                compare_op=ALU.is_equal, fill=0.0, base=0, pattern=[[-8, 2], [-4, 2], [-1, 4], [0, R]],
                channel_multiplier=1).then_inc(consts, 1)
            nc.gpsimd.affine_select(out=sel[:, 4:6, :], in_=sel_ones[:, 0:2, :], compare_op=ALU.is_ge, fill=0.0,
                                    base=-16, pattern=[[-3, 2], [0, P]], channel_multiplier=1).then_inc(consts, 1)
            pool.wait_ge(consts, 6)
            nc.gpsimd.affine_select(out=sel[:, 4:6, :], in_=sel[:, 4:6, :], compare_op=ALU.is_ge, fill=0.0,
                                    base=18, pattern=[[3, 2], [0, P]], channel_multiplier=-1).then_inc(consts, 1)
            for k, value in enumerate((-0.5, 0.5, 2.718281828459045)):
                nc.gpsimd.memset(powers[:, k, :], value).then_inc(consts, 1)
            pool.wait_ge(consts, 10)

            def rstd(c, mv_name, name, k):
                need(pool, mv_name, c, 1)
                nc.gpsimd.tensor_scalar(sm[:, 1, :], mv[:, :, 1], EPS, 1.0, ALU.add, ALU.mult).then_inc(sem("pool_pre"), 1)
                need(pool, "pool_pre", c, k)
                nc.gpsimd.tensor_tensor(sm[:, 0, :], sm[:, 1, :], powers[:, 0, :], ALU.pow).then_inc(sem(name), 1)

            def weigh(c, o):
                f, slot = ORDER[o]
                need(pool, "gated", c, o + 1)
                if slot == 0:
                    need(pool, "mixed", c, max(f - 1, 0))
                    nc.gpsimd.tensor_tensor(w0[:, f % 2, :], gated[:, o % 2, :], rw_rows[:, 0, :], ALU.mult
                                            ).then_inc(sem("weighted"), 1)
                else:
                    need(pool, "g1_lo", c, max(f - 1, 0))
                    nc.gpsimd.tensor_tensor(w1[:, f % 2, :], gated[:, o % 2, :], rw_rows[:, 1, :], ALU.mult
                                            ).then_inc(sem("weighted"), 1)
                    need(pool, "weighted", c, o + 1)
                    need(pool, "gc_lo", c, max(f - 1, 0))
                    if f == 0:
                        need(pool, "stored", c, 0)
                    nc.gpsimd.tensor_tensor(wc[:, f % 2, :], w0[:, f % 2, :], w1[:, f % 2, :], ALU.add
                                            ).then_inc(sem("mixed"), 1)

            def scale_and_round(c):
                need(pool, "mv1", c, 1)
                nc.gpsimd.tensor_tensor(sm[:, 2, :], mv[:, :, 1], powers[:, 1, :], ALU.pow).then_inc(sem("pool_pre"), 1)
                need(pool, "pool_pre", c, 1)
                rstd(c, "mv1", "pow1", 2)
                need(pool, "q_in", c, 1)
                need(pool, "xqT_ps", c, 0)
                nc.gpsimd.tensor_scalar(flat(xq[:, :, :]), flat(d4[:, :, :]), -ROUND, 1.0, ALU.add, ALU.mult
                                        ).then_inc(sem("xq"), 1)

            def hidden_rounded(c, j):
                need(pool, "hr", c, j + 1)
                need(pool, "hqT_ps", c, j - 1)
                nc.gpsimd.tensor_scalar(hq[:, j % 2, :], h[:, j % 2, :], -ROUND, 1.0, ALU.add, ALU.mult
                                        ).then_inc(sem("hq"), 1)

            def step(c, e):
                if e is not None:
                    scale_and_round(e)
                if c is not None:
                    need(pool, "spread", c, 6)
                    weigh(c, 0)
                for s in range(1, FT):
                    if e is not None and 2 <= s <= 5:
                        hidden_rounded(e, s - 2)
                    if e is not None and s == 6:
                        need(pool, "ssq", e, 4)
                        nc.gpsimd.tensor_tensor(sm[:, 9, :], sm[:, 8, :], powers[:, 1, :], ALU.pow
                                                ).then_inc(sem("norm2"), 1)
                    if c is not None:
                        weigh(c, 2 * s - 1)
                        weigh(c, 2 * s)
                if c is not None:
                    weigh(c, 2 * FT - 1)
                if e is not None:
                    rstd(e, "mv2", "rstd2", 3)
                    need(pool, "xm", e, 1)
                    nc.gpsimd.tensor_tensor(xchunk4(e), xchunk4(e), t["beta"][:, :].unsqueeze(1).to_broadcast([P, CT, D]),
                                            ALU.add).then_inc(sem("xb"), 1)
                    rstd(e, "mv3", "rstd3", 4)
                    rstd(e, "mv4", "rstd4", 5)
                    need(pool, "gap", e, 1)
                    nc.gpsimd.tensor_tensor(sm[:, 12, :], powers[:, 2, :], sm[:, 11, :], ALU.pow).then_inc(sem("exp_gap"), 1)

            run(pool, step)

        @block.scalar
        def _(act):
            def silu(c, o):
                f, slot = ORDER[o]
                need(act, "fd" if slot else "f0", c, f + 1)
                need(act, "gated", c, o - 1)
                if o == 0:
                    need(act, "m_lo", c, 0)
                nc.scalar.activation(sil[:, o % 2, :], X[:, 2 * (f % 2), :], ACT.Silu).then_inc(sem("silu"), 1)

            def high(c, f):
                need(act, "weighted", c, AT[f, 1] + 1)
                need(act, "p_ps", c, 0)
                nc.scalar.copy(g1_hi[:, f, :], w1[:, f % 2, :]).then_inc(sem("g1_hi"), 1)
                need(act, "mixed", c, f + 1)
                need(act, "down", c, 0)
                nc.scalar.copy(gc_hi[:, f, :], wc[:, f % 2, :]).then_inc(sem("gc_hi"), 1)

            def a_high(c, q):
                need(act, "a_ps", c, q + 1)
                need(act, "a_masked", c, q - 1)
                if q == 0:
                    need(act, "down", c, 0)
                nc.scalar.copy(a_hi[:, q % 2, :], X[:, q, :]).then_inc(sem("a_hi"), 1)

            def spread(c):
                need(act, "m_lo", c, 0)
                need(act, "mixed", c, 0)
                for v in range(6):
                    need(act, "spread_ps", c, v + 1)
                    dst = mask[:, v, :] if v < 4 else rw_rows[:, v - 4, :]
                    nc.scalar.copy(dst, Y[:, 2 + v % 2, :]).then_inc(sem("spread"), 1)

            def x_turned(c):
                need(act, "xqT_ps", c, 1)
                need(act, "hp", c, 0)
                nc.scalar.copy(flat(xqT[:, :, :]), Y0b).then_inc(sem("xqT"), 1)

            def hidden(c, j):
                need(act, "hp", c, j + 1)
                need(act, "hq", c, j - 1)
                if j == 0:
                    need(act, "logits_ps", c, 0)
                    need(act, "x_lo", c, 0)
                if j == 1:
                    need(act, "ys", c, 0)
                need(act, "ssq", c, j)
                nc.scalar.activation(h[:, j % 2, :], flat(Y[:, 1:3, :]), ACT.Gelu, scale=sm[:, 10, j:j + 1]
                                     ).then_inc(sem("gelu"), 1)
                need(act, "gelu", c, j + 1)
                nc.scalar.activation(junk[:, :], h[:, j % 2, :], ACT.Square, accum_out=sm[:, 8, j:j + 1]
                                     ).then_inc(sem("ssq"), 1)

            def hidden_turned(c, j):
                need(act, "hqT_ps", c, j + 1)
                need(act, "y", c, j)
                nc.scalar.copy(flat(hqT[:, :, :]), Y3b).then_inc(sem("hqT"), 1)

            def z_turned(c):
                need(act, "zT", c, 1)
                need(act, "hq", c, CT - 1)
                nc.scalar.copy(flat(xTf[:, :, :]), flat(Y[:, 1:3, :])).then_inc(sem("xTf"), 1)
                need(act, "xTf", c, 1)
                nc.scalar.copy(flat(xT_hi[:, :, :]), flat(xTf[:, :, :])).then_inc(sem("x_hi"), 1)

            def step(c, e):
                if c is not None:
                    a_high(c, 0)
                    a_high(c, 1)
                    a_high(c, 2)
                    a_high(c, 3)
                    silu(c, 0)
                for s in range(1, FT):
                    if e is not None and 2 <= s <= 5:
                        hidden(e, s - 2)
                    if c is not None:
                        silu(c, 2 * s - 1)
                    if e is not None and s == 1:
                        x_turned(e)
                    if e is not None and s >= 3:
                        hidden_turned(e, s - 3)
                    if c is not None:
                        silu(c, 2 * s)
                        if s >= 2:
                            high(c, s - 2)
                if c is not None:
                    silu(c, 2 * FT - 1)
                    high(c, FT - 2)
                    high(c, FT - 1)
                if e is not None:
                    z_turned(e)
                    spread(e)

            run(act, step)

        @block.vector
        def _(dve):
            links = {}

            def link(ins, c, name="dve_pre", apart=False):
                links[name] = links.get(name, 0) % PER[name] + 1
                ins.then_inc(sem(name), 1)
                need(dve, name, c, links[name], apart=apart)

            def small(dst, c, op, *args, **kw):
                link(op(sm[:, dst, :], *args, **kw), c)

            def stats(rows, c, name):
                for j in range(CT):
                    last = nc.vector.bn_stats(st6[:, j, :], rows(j))
                link(last, c, apart=True)
                for j in range(CT):
                    last = nc.vector.bn_aggr(mv[:, j, :], st6[:, j, :])
                last.then_inc(sem(name), 1)
                need(dve, name, c, 1)

            def normed(rows, dst, c, name):
                for j in range(CT):
                    last = nc.vector.tensor_scalar(dst(j), rows(j), mv[:, j, 0:1], sm[:, 0, j:j + 1], ALU.subtract, ALU.mult)
                last.then_inc(sem(name), 1)

            def gate(c, o):
                f, slot = ORDER[o]
                need(dve, "silu", c, o + 1)
                need(dve, "weighted", c, o - 1)
                nc.vector.tensor_tensor(gated[:, o % 2, :], sil[:, o % 2, :], X[:, 2 * (f % 2) + 1, :], ALU.mult
                                        ).then_inc(sem("gated"), 1)

            def low(c, f):
                need(dve, "g1_hi", c, f + 1)
                nc.vector.tensor_tensor(g1_lo[:, f, :], w1[:, f % 2, :], g1_hi[:, f, :], ALU.subtract).then_inc(sem("g1_lo"), 1)
                need(dve, "gc_hi", c, f + 1)
                nc.vector.tensor_tensor(gc_lo[:, f, :], wc[:, f % 2, :], gc_hi[:, f, :], ALU.subtract).then_inc(sem("gc_lo"), 1)

            def masked(c):
                need(dve, "fd", c, 0)
                for q in range(4):
                    need(dve, "a_hi", c, q + 1)
                    need(dve, "a_masked", c, q - 1)
                    nc.vector.tensor_tensor(a_lo[:, q % 2, :], X[:, q, :], a_hi[:, q % 2, :], ALU.subtract
                                            ).then_inc(sem("a_lo"), 1)
                    need(dve, "a_lo", c, q + 1)
                    need(dve, "spread", c, 4)
                    for slot in range(2):
                        for b, part in enumerate((a_hi, a_lo)):
                            last = nc.vector.tensor_tensor(am[:, q, slot, b, :], part[:, q % 2, :],
                                                           mask[:, 2 * slot + q % 2, :], ALU.mult)
                    last.then_inc(sem("a_masked"), 1)

            def back_masked(c, k):
                for w in range(2):
                    q = 2 * k + w
                    need(dve, "p_ps", c, q + 1)
                    if w == 0:
                        need(dve, "m_lo", c, k)
                    nc.vector.tensor_tensor(pm[w], X[:, BANKS[q], :], mask[:, 2 * w + k, :], ALU.mult
                                            ).then_inc(sem("p_read"), 1)

            def back_parts(c, k):
                need(dve, "p_read", c, 2 * k + 2)
                link(nc.vector.tensor_tensor(pm[2], pm[0], pm[1], ALU.add), c, "dve_main")
                need(dve, "down", c, 0)
                nc.vector.tensor_copy(m_hi[:, k, :], pm[2]).then_inc(sem("m_hi"), 1)
                need(dve, "m_hi", c, k + 1)
                nc.vector.tensor_tensor(m_lo[:, k, :], pm[2], m_hi[:, k, :], ALU.subtract).then_inc(sem("m_lo"), 1)

            def store(c, j):
                need(dve, "down", c, j + 1)
                nc.vector.scalar_tensor_tensor(out=out_sb[:, j, :], in0=X[:, BANKS[j], 0:D], scalar=t["tanh"][:, 3:4],
                                               in1=xrow(c, j), op0=ALU.mult, op1=ALU.add).then_inc(sem("out_sb"), 1)

            V = nc.vector

            def centered(c):
                need(dve, "zT", c, 0)
                stats(lambda j: xrow(c, j), c, "mv1")
                for j in range(CT):
                    last = V.tensor_scalar(d4[:, j, :], xrow(c, j), mv[:, j, 0:1], None, ALU.subtract)
                link(last, c)
                small(3, c, V.tensor_reduce, d4[:, :, :], AX.X, ALU.max, apply_absolute_value=True)

            def rounded(c):
                need(dve, "pow1", c, 1)
                small(4, c, V.tensor_tensor, sm[:, 2, :], sm[:, 0, :], ALU.mult)
                small(4, c, V.tensor_scalar, sm[:, 4, :], float(D) ** 0.5, 1e-12, ALU.mult, ALU.max)
                small(5, c, V.reciprocal, sm[:, 4, :])
                small(4, c, V.tensor_tensor, sm[:, 0, :], sm[:, 5, :], ALU.mult)
                small(4, c, V.tensor_scalar, sm[:, 4, :], float(D) ** 0.5, None, ALU.mult)
                small(5, c, V.tensor_tensor, sm[:, 4, :], sm[:, 3, :], ALU.mult)
                small(5, c, V.tensor_scalar, sm[:, 5, :], EPS, 1.0 / 127.0, ALU.max, ALU.mult)
                small(6, c, V.reciprocal, sm[:, 5, :])
                small(7, c, V.tensor_tensor, sm[:, 4, :], sm[:, 6, :], ALU.mult)
                need(dve, "gelu", c, 0)
                small(10, c, V.tensor_scalar, sm[:, 5, :], t["mean1"][:, :], None, ALU.mult)
                for j in range(CT):
                    last = V.tensor_scalar(d4[:, j, :], d4[:, j, :], sm[:, 7, j:j + 1], ROUND, ALU.mult, ALU.add)
                last.then_inc(sem("q_in"), 1)

            def hidden_scaled(c, j):
                if j == 0:
                    need(dve, "norm2", c, 0)
                need(dve, "gelu", c, j + 1)
                link(V.tensor_reduce(sm[:, 13, j:j + 1], h[:, j % 2, :], AX.X, ALU.max, apply_absolute_value=True), c)
                link(V.tensor_scalar(sm[:, 14, j:j + 1], sm[:, 13, j:j + 1], TINY, 1.0 / 127.0, ALU.max, ALU.mult), c)
                link(V.reciprocal(sm[:, 15, j:j + 1], sm[:, 14, j:j + 1]), c)
                need(dve, "ssq", c, j + 1)
                V.tensor_scalar(h[:, j % 2, :], h[:, j % 2, :], sm[:, 15, j:j + 1], ROUND, ALU.mult, ALU.add).then_inc(sem("hr"), 1)

            def y_out(c, j):
                need(dve, "y", c, j + 1)
                V.tensor_copy(y2[:, j, :], Y[:, 0, 0:D]).then_inc(sem("y2"), 1)

            def first_factors(c):
                need(dve, "norm2", c, 1)
                small(4, c, V.tensor_scalar, sm[:, 9, :], 1e-12, None, ALU.max)
                small(5, c, V.reciprocal, sm[:, 4, :])
                small(4, c, V.tensor_tensor, sm[:, 13, :], sm[:, 5, :], ALU.mult)
                small(4, c, V.tensor_scalar, sm[:, 4, :], float(F1) ** 0.5, EPS, ALU.mult, ALU.max)
                small(4, c, V.tensor_scalar, sm[:, 4, :], 1.0 / 127.0, None, ALU.mult)
                small(4, c, V.tensor_scalar, sm[:, 4, :], t["mean2"][:, :], t["tanh"][:, 2:3], ALU.mult, ALU.mult)

            def add_first(c):
                need(dve, "y2", c, 4)
                for j in range(CT):
                    last = V.scalar_tensor_tensor(out=xrow(c, j), in0=y2[:, j, :], scalar=sm[:, 4, j:j + 1],
                                                  in1=xrow(c, j), op0=ALU.mult, op1=ALU.add)
                link(last, c, apart=True)
                stats(lambda j: xrow(c, j), c, "mv2")

            def minus_mean(c):
                for j in range(CT):
                    last = V.tensor_scalar(y4[:, j, :], xrow(c, j), mv[:, j, 0:1], None, ALU.subtract)
                last.then_inc(sem("xm"), 1)

            def plus_summary(c):
                need(dve, "rstd2", c, 1)
                need(dve, "xm", c, 1)
                need(dve, "summ_in", c, 16 * CT)
                for j in range(CT):
                    last = V.scalar_tensor_tensor(out=y4[:, j, :], in0=y4[:, j, :], scalar=sm[:, 0, j:j + 1],
                                                  in1=summ[:, j, :], op0=ALU.mult, op1=ALU.add)
                last.then_inc(sem("ys"), 1)
                need(dve, "ys", c, 1, apart=True)
                stats(lambda j: y4[:, j, :], c, "mv3")

            def add_block(c):
                for j in range(CT):
                    last = V.scalar_tensor_tensor(out=y4[:, j, :], in0=y4[:, j, :], scalar=mv[:, j, 0:1],
                                                  in1=t["gamma"][:, :], op0=ALU.subtract, op1=ALU.mult)
                link(last, c)
                need(dve, "rstd3", c, 1)
                need(dve, "xb", c, 1)
                for j in range(CT):
                    last = V.scalar_tensor_tensor(out=xrow(c, j), in0=y4[:, j, :], scalar=sm[:, 0, j:j + 1],
                                                  in1=xrow(c, j), op0=ALU.mult, op1=ALU.add)
                last.then_inc(sem("x3"), 1)
                need(dve, "x3", c, 1, apart=True)
                stats(lambda j: xrow(c, j), c, "mv4")

            def last_norm(c):
                need(dve, "rstd4", c, 1)
                normed(lambda j: xrow(c, j), lambda j: y4[:, j, :], c, "z")

            def x_low(c):
                need(dve, "x_hi", c, 1)
                V.tensor_tensor(flat(xT_lo[:, :, :]), flat(xTf[:, :, :]), flat(xT_hi[:, :, :]), ALU.subtract
                                ).then_inc(sem("x_lo"), 1)

            def top_two(c):
                need(dve, "logits_ps", c, 1)
                V.tensor_copy(flat(logits[:, :, :]), Y[:, 0, 0:CT * E]).then_inc(sem("logits"), 1)
                need(dve, "logits", c, 1, apart=True)
                for j in range(CT):
                    last = V.max(top[:, j, :], logits[:, j, :])
                link(last, c, apart=True)
                for j in range(CT):
                    last = V.max_index(top_i[:, j, :], top[:, j, :], logits[:, j, :])
                link(last, c)
                need(dve, "exp_gap", c, 0)
                V.tensor_tensor(sm[:, 11, :], top[:, :, 1], top[:, :, 0], ALU.subtract).then_inc(sem("gap"), 1)
                link(V.tensor_copy(top_f[:, :, :], top_i[:, :, 0:2]), c)
                need(dve, "gT_ps", c, 0)
                link(V.tensor_tensor(gpack[:, :, 0:8], experts[:, :, :], top_f[:, :, 0:1].to_broadcast([P, CT, E]),
                                     ALU.is_equal), c)
                link(V.tensor_tensor(onehot[:, :, :], experts[:, :, :], top_f[:, :, 1:2].to_broadcast([P, CT, E]),
                                     ALU.is_equal), c)
                link(V.tensor_tensor(gpack[:, :, 8:16], onehot[:, :, :], gpack[:, :, 0:8], ALU.subtract), c)
                need(dve, "exp_gap", c, 1)
                small(4, c, V.tensor_scalar, sm[:, 12, :], 1.0, None, ALU.add)
                link(V.reciprocal(rw[:, :, 0], sm[:, 4, :]), c)
                link(V.tensor_tensor(rw[:, :, 1], sm[:, 12, :], rw[:, :, 0], ALU.mult), c)
                part = gpack[:, :, 16:22].rearrange("p a (s i) -> p i a s", i=3)
                link(V.tensor_copy(part[:, 0], rw[:, :, :]), c)
                link(V.tensor_tensor(rw_rest[:, :, :], rw[:, :, :], part[:, 0], ALU.subtract), c)
                link(V.tensor_copy(part[:, 1], rw_rest[:, :, :]), c)
                V.tensor_tensor(part[:, 2], rw_rest[:, :, :], part[:, 1], ALU.subtract).then_inc(sem("routing"), 1)

            def routing_turned(c):
                need(dve, "gT_ps", c, 1)
                V.tensor_copy(gT[:, :], Y0b[0:32, 0:N]).then_inc(sem("gT"), 1)

            def step(c, e):
                if c is not None:
                    masked(c)
                if e is not None:
                    centered(e)
                if c is not None:
                    gate(c, 0)
                if e is not None:
                    rounded(e)
                for s in range(1, FT):
                    if e is not None and 2 <= s <= 5:
                        hidden_scaled(e, s - 2)
                    if c is not None:
                        gate(c, 2 * s - 1)
                    if e is not None and 3 < s:
                        y_out(e, s - 4)
                    if c is not None:
                        gate(c, 2 * s)
                        if s >= 2:
                            low(c, s - 2)
                if e is not None:
                    y_out(e, CT - 1)
                    first_factors(e)
                if c is not None:
                    gate(c, 2 * FT - 1)
                if e is not None:
                    add_first(e)
                    minus_mean(e)
                if c is not None:
                    low(c, FT - 2)
                if e is not None:
                    plus_summary(e)
                if c is not None:
                    low(c, FT - 1)
                if e is not None:
                    add_block(e)
                if c is not None:
                    back_masked(c, 0)
                if e is not None:
                    last_norm(e)
                if c is not None:
                    back_parts(c, 0)
                if e is not None:
                    x_low(e)
                    top_two(e)
                if c is not None:
                    back_masked(c, 1)
                    back_parts(c, 1)
                if e is not None:
                    routing_turned(e)
                if c is not None:
                    for j in range(CT):
                        store(c, j)

            run(dve, step)
            assert all(links[n] == PER[n] for n in links), links

        @block.tensor
        def _(pe):
            pe.wait_ge(sem("consts"), 10)
            mm = nc.tensor.matmul
            PARTS = ((0, 0), (1, 0), (0, 1))

            def products(out, pairs, start, stop):
                n = len(pairs) * 3
                for i, (lhs, rhs) in enumerate(pairs):
                    for k, (a, b) in enumerate(PARTS):
                        last = mm(out, lhs[a], rhs[b], start=start and i == k == 0, stop=stop and 3 * i + k == n - 1,
                                  skip_group_check=True)
                return last

            def lora(w, k, f, slot, out, stop):
                q = 2 * w + k
                wt = ("B1", "B3")[w]
                fs = slice(f * P, (f + 1) * P)
                return products(out, [((t[wt + "_hi"][:, k, fs], t[wt + "_lo"][:, k, fs]),
                                       (am[:, q, slot, 0, :], am[:, q, slot, 1, :]))], False, stop)

            def first(c, f):
                if f < 2:
                    need(pe, "a_lo", c, 2 * f + 2)
                    need(pe, "p_read", c, 0)
                else:
                    need(pe, "gated", c, AT[f - 2, 1] + 1)
                for w, wt in enumerate(("W1", "W3")):
                    out = X[:, 2 * (f % 2) + w, :]
                    fs = slice(f * P, (f + 1) * P)
                    products(out, [((t[wt + "_hi"][:, k, fs], t[wt + "_lo"][:, k, fs]),
                                    (xT_hi[:, k, :], xT_lo[:, k, :])) for k in range(2)], True, False)
                for w in range(2):
                    out = X[:, 2 * (f % 2) + w, :]
                    for k in range(2):
                        if f == 0:
                            need(pe, "a_masked", c, 2 * w + k + 1)
                        last = lora(w, k, f, 0, out, k == 1)
                last.then_inc(sem("f0"), 1)

            def second(c, f):
                need(pe, "gated", c, AT[f, 0] + 1)
                for w in range(2):
                    for k in range(2):
                        last = lora(w, k, f, 1, X[:, 2 * (f % 2) + w, :], k == 1)
                last.then_inc(sem("fd"), 1)

            def down(c, j):
                need(pe, "p_read", c, j + 1)
                js = slice(j * P, (j + 1) * P)
                products(X[:, BANKS[j], 0:D], [((gc_hi[:, f, js], gc_lo[:, f, js]),
                                                (t["W2_hi"][:, f, :], t["W2_lo"][:, f, :])) for f in range(FT)],
                         True, False)

            def down_lora(c, j):
                need(pe, "m_lo", c, 2)
                js = slice(j * P, (j + 1) * P)
                products(X[:, BANKS[j], 0:D], [((m_hi[:, k, js], m_lo[:, k, js]),
                                                (t["B2_hi"][:, k, :], t["B2_lo"][:, k, :])) for k in range(2)],
                         False, True).then_inc(sem("down"), 1)

            def a_products(c):
                need(pe, "x_lo", c, 1)
                need(pe, "x_hi", c, 1)
                need(pe, "out_sb", c, 0)
                for q in range(4):
                    wt, es = ("A1", "A3")[q // 2], slice(q % 2 * P, (q % 2 + 1) * P)
                    products(X[:, q, :], [((t[wt + "_hi"][:, k, es], t[wt + "_lo"][:, k, es]),
                                           (xT_hi[:, k, :], xT_lo[:, k, :])) for k in range(2)], True, True
                             ).then_inc(sem("a_ps"), 1)

            def back(c, q, fs):
                if q < 2:
                    need(pe, "gated", c, AT[FT - 2, 1] + 1)
                else:
                    need(pe, "gated", c, 2 * FT)
                es = slice(q // 2 * P, (q // 2 + 1) * P)
                hi, lo = (g1_hi, g1_lo) if q % 2 else (gc_hi, gc_lo)
                for f in fs:
                    if q < 2:
                        need(pe, "g1_lo" if q % 2 else "gc_lo", c, f + 1)
                    last = products(X[:, BANKS[q], :], [((t["A2_hi"][:, f, es], t["A2_lo"][:, f, es]),
                                                         (hi[:, f, :], lo[:, f, :]))], f == 0, f == FT - 1)
                if f == FT - 1:
                    last.then_inc(sem("p_ps"), 1)

            def up(c, j):
                if j == 0:
                    need(pe, "xqT", c, 1)
                    need(pe, "xTf", c, 0)
                    need(pe, "spread", c, 0)
                need(pe, "gelu", c, j)
                for n in range(2):
                    for k in range(2):
                        last = mm(Y[:, 1 + n, :], xqT[:, k, j * P:(j + 1) * P], t["w1T"][:, k, n * 512:(n + 1) * 512],
                                  start=(k == 0), stop=(k == 1))
                last.then_inc(sem("hp"), 1)

            def turn_hidden(c, j):
                need(pe, "hq", c, j + 1)
                need(pe, "hqT", c, j)
                if j == 0:
                    need(pe, "spread", c, 0)
                for n in range(8):
                    last = nc.tensor.transpose(Y3b[:, n * P:(n + 1) * P], hq[:, j % 2, n * P:(n + 1) * P], identb[:, :])
                last.then_inc(sem("hqT_ps"), 1)

            def second_product(c, j):
                need(pe, "hqT", c, j + 1)
                need(pe, "xqT" if j == 0 else "y2", c, max(j, 1))
                for n in range(8):
                    last = mm(Y[:, 0, 0:D], hqT[:, n, :], t["w2T"][:, n, :], start=(n == 0), stop=(n == 7))
                last.then_inc(sem("y"), 1)

            def turn_xq(c):
                need(pe, "xq", c, 1)
                need(pe, "gT", c, 0)
                for k in range(2):
                    for j in range(CT):
                        last = nc.tensor.transpose(Y0b[:, (k * CT + j) * P:(k * CT + j + 1) * P],
                                                   xq[:, j, k * P:(k + 1) * P], identb[:, :])
                last.then_inc(sem("xqT_ps"), 1)

            def turn_z(c):
                need(pe, "z", c, 1)
                need(pe, "gelu", c, 4)
                for k in range(2):
                    for j in range(CT):
                        last = nc.tensor.transpose(Y[:, 1 + k, j * P:(j + 1) * P], y4[:, j, k * P:(k + 1) * P], ident[:, :])
                last.then_inc(sem("zT"), 1)

            def route(c):
                need(pe, "xTf", c, 1)
                need(pe, "y2", c, 4)
                for j in range(CT):
                    for k in range(2):
                        last = mm(Y[:, 0, j * E:(j + 1) * E], xTf[:, k, j * P:(j + 1) * P], t["WgT"][:, k, :],
                                  start=(k == 0), stop=(k == 1), skip_group_check=True)
                last.then_inc(sem("logits_ps"), 1)

            def turn_routing(c):
                need(pe, "routing", c, 1)
                need(pe, "logits", c, 1)
                for j in range(CT):
                    last = nc.tensor.transpose(Y0b[0:32, j * P:(j + 1) * P], gpack[:, j, :], identb[:, :])
                last.then_inc(sem("gT_ps"), 1)

            def spread(c, vs):
                need(pe, "gT", c, 1)
                need(pe, "hqT", c, 4)
                need(pe, "xTf", c, 1)
                for v in vs:
                    if v >= 2:
                        need(pe, "spread", c, v - 1)
                    mm(Y[:, 2 + v % 2, :], sel[:, v, :], gT[:, :], start=True, stop=True).then_inc(sem("spread_ps"), 1)

            def step(c, e):
                if c is not None:
                    a_products(c)
                    first(c, 0)
                for s in range(1, FT):
                    if c is not None:
                        first(c, s)
                    if e is not None and s >= 3:
                        turn_hidden(e, s - 3)
                    if c is not None:
                        second(c, s - 1)
                    if e is not None and s == 1:
                        turn_xq(e)
                    if e is not None and s <= 4:
                        up(e, s - 1)
                    if e is not None and s >= 3:
                        second_product(e, s - 3)
                if c is not None:
                    second(c, FT - 1)
                    back(c, 0, range(FT - 1))
                    back(c, 1, range(FT - 1))
                    back(c, 0, (FT - 1,))
                    back(c, 1, (FT - 1,))
                    back(c, 2, range(FT))
                    back(c, 3, range(4))
                if e is not None:
                    turn_z(e)
                if c is not None:
                    back(c, 3, range(4, FT))
                if e is not None:
                    route(e)
                if c is not None:
                    for j in range(3):
                        down(c, j)
                if e is not None:
                    turn_routing(e)
                if c is not None:
                    down(c, 3)
                for k in range(3):
                    if e is not None:
                        spread(e, (2 * k, 2 * k + 1))
                    if c is not None:
                        for j in ((0, 1), (2,), (3,))[k]:
                            down_lora(c, j)

            run(pe, step)


def load_x(nc, t):
    with ExitStack() as ctx:
        x_in = ctx.enter_context(nc.semaphore("x_in"))
        block = ctx.enter_context(nc.Block())

        @block.sync
        def _(sp):
            sp.dma_start(t["x"][:, :, :], t["x_dram"]).then_inc(x_in, 16)
            sp.wait_ge(x_in, 16)


def store_x(nc, t):
    with ExitStack() as ctx:
        x_out = ctx.enter_context(nc.semaphore("x_out"))
        block = ctx.enter_context(nc.Block())

        @block.sync
        def _(sp):
            sp.dma_start(t["out_dram"], t["x"][:, :, :]).then_inc(x_out, 16)
            sp.wait_ge(x_out, 16)


def program(nc, a, out, stages=3):
    with ExitStack() as ctx:
        def sb(name, shape, dt=F32):
            return ctx.enter_context(nc.sbuf_tensor(name, shape, dt))

        t = {"passed": ctx.enter_context(nc.semaphore("passed"))}
        t |= {"x": sb("x", [P, TILES, D]), "ident": sb("ident", [P, P]), "identb": sb("identb", [P, P], BF16)}
        t |= {"g": sb("g", [P, 8]), "tanh": sb("tanh", [P, 4]), "gain0": sb("gain0", [P, 1])}
        t |= {"mean1": sb("mean1", [P, 1]), "mean2": sb("mean2", [P, 1])}
        t |= {"gamma": sb("gamma", [P, D]), "beta": sb("beta", [P, D]), "WgT": sb("WgT", [P, 2, E])}
        for n, shape in (("W1", [P, 2, F]), ("W3", [P, 2, F]), ("B1", [P, 2, F]), ("B3", [P, 2, F]),
                         ("A1", [P, 2, ER]), ("A3", [P, 2, ER]), ("B2", [P, 2, D]), ("W2", [P, FT, D]), ("A2", [P, FT, ER])):
            t[n + "_hi"] = sb(n + "_hi", shape, BF16)
            t[n + "_lo"] = sb(n + "_lo", shape, BF16)
        t["w1T"] = sb("w1T", [P, 2, F1], BF16)
        t["w2T"] = sb("w2T", [P, F1 // P, D], BF16)

        def tiles_of(ap):
            return ap.rearrange("(n b) s d -> (b s) n d", b=2)

        def rows(ap):
            return ap.rearrange("(n p) d -> p n d", p=P)

        def column(ap, n):
            return ap.unsqueeze(0).to_broadcast([P, n])

        t["x_dram"], t["ctx_dram"], t["out_dram"] = tiles_of(a["x"]), tiles_of(a["ctx_2048"]), tiles_of(out)
        t["g_xattn_dram"], t["g_ffn_dram"] = column(a["g_xattn"], 2), column(a["g_ffn"], 2)
        t["gamma0_dram"] = column(a["L0_xattn_gamma"], 1)
        t["decay_dram"] = column(a["L1_xattn_decay"], 1)
        t["w1_dram"], t["w2_dram"] = rows(a["L0_ffn_w1"]), rows(a["L0_ffn_w2"])
        for n in ("W1", "W3", "W2"):
            t[n + "_dram"] = rows(a["L1_ffn_" + n])
        for n in ("A1", "A3", "A2"):
            t[n + "_dram"] = a["L1_ffn_" + n].rearrange("e r h -> (e r) h").rearrange("(n p) h -> p n h", p=P)
        for n in ("B1", "B3", "B2"):
            b = a["L1_ffn_" + n].rearrange("e (n p) r -> n p e r", p=P)
            t[n + "_dram"] = [b[i] for i in range(2 if n == "B2" else FT)]
        t["Win_dram"], t["Wout_dram"] = rows(a["L1_xattn_W_in"]), rows(a["L1_xattn_W_out"])
        t["b_in_dram"] = a["L1_xattn_b_in"].rearrange("(n p) -> p n", p=P)
        t["b_out_dram"] = a["L1_xattn_b_out"].unsqueeze(0)
        t["Wg_dram"] = a["L1_ffn_Wg"]
        t["gamma_dram"], t["beta_dram"] = column(a["L1_xattn_gamma"], D), column(a["L1_xattn_beta"], D)
        t["summ_dram"] = nc.dram_tensor("summaries", (NB, D), F32, kind="Internal").ap()
        t["q_parts_dram"] = nc.dram_tensor("q_parts_scratch", (2, 3, DH, 2 * HEADS, D), BF16, kind="Internal").ap()
        t["k_parts_dram"] = nc.dram_tensor("k_parts_scratch", (2, 5, DH, 2 * HEADS, D), BF16, kind="Internal").ap()
        t["pv_dram"] = nc.dram_tensor("pv_scratch", (2, 2, 2, P, D), F32, kind="Internal").ap()

        def k_windows(u, h):
            rows = t["k_parts_dram"][u, :, :, h * 8:h * 8 + 8, :].rearrange("a d h l -> (a d) (h l)")
            return bass.AP(rows.tensor, rows.offset, [[8 * 2 * HEADS * D, 3], [2 * HEADS * D, 24], [1, HEADS * D]])

        t["k_windows"] = k_windows
        with ExitStack() as early:
            t["ctx"] = early.enter_context(nc.sbuf_tensor("ctx", [P, TILES, D], F32))
            load_x(nc, t)
            with ExitStack() as own:
                turned = {n: own.enter_context(nc.sbuf_tensor(n + "T", [P, 2, D], F32)) for n in ("Win", "Wout")}
                prepare(nc, t, turned)
            if stages >= 2:
                attention(nc, t)
        if stages >= 3:
            tokens(nc, t)
        else:
            store_x(nc, t)


_INS = ["x", "ctx_2048", "g_xattn", "g_ffn", "L0_xattn_gamma", "L0_ffn_w1", "L0_ffn_w2", "L1_xattn_decay",
        "L1_xattn_W_in", "L1_xattn_b_in", "L1_xattn_W_out", "L1_xattn_b_out", "L1_xattn_gamma", "L1_xattn_beta",
        "L1_ffn_Wg", "L1_ffn_W1", "L1_ffn_W2", "L1_ffn_W3", "L1_ffn_A1", "L1_ffn_B1", "L1_ffn_A2", "L1_ffn_B2",
        "L1_ffn_A3", "L1_ffn_B3"]


def kernel(**inputs):
    import numpy as _np
    import concourse.bacc as _bacc
    from concourse import mybir as _mybir
    from concourse.bass_utils import run_bass_kernel_spmd as _run

    nc = _bacc.Bacc("TRN2", target_bir_lowering=False, num_devices=1)
    arrays, args = {}, {}
    for name in _INS:
        a = _np.ascontiguousarray(inputs[name])
        if a.ndim == 0:
            a = a.reshape(1)
        arrays[f"in_{name}_dram"] = a
        args[name] = nc.dram_tensor(f"in_{name}_dram", a.shape, _mybir.dt.from_np(a.dtype), kind="ExternalInput").ap()
    out = nc.dram_tensor("out_dram", (NB, S, D), F32, kind="ExternalOutput").ap()
    program(nc, args, out)
    r = _run(nc, [arrays], core_ids=[0])
    return r.results[0]["out_dram"]
```

```python
from contextlib import ExitStack

import concourse.bass as bass
from concourse import mybir

ALU = mybir.AluOpType
ACT = mybir.ActivationFunctionType
AX = mybir.AxisListType
BF16 = mybir.dt.bfloat16
F32 = mybir.dt.float32
U32 = mybir.dt.uint32

P = 128
NB, S, D = 64, 64, 256
TILES = NB * S // P
HEADS, DH = 8, 8
HALVES = 2 * TILES
F1 = 1024
F, E, R = 896, 8, 32
FT = F // P
ER = E * R
ROUND = 1.5 * 2.0**23
EPS = 1e-5


class Sems:

    def __init__(self, nc, ctx, prefix):
        self.nc, self.ctx, self.prefix, self.made = nc, ctx, prefix, {}

    def __call__(self, name):
        if name not in self.made:
            self.made[name] = self.ctx.enter_context(self.nc.semaphore(f"{self.prefix}_{name}"))
        return self.made[name]


def at_least(eng, sem, value, passed=None):
    if not isinstance(value, int) or value > 0:
        eng.wait_ge(sem, value)
        if passed is not None and not isinstance(value, int):
            eng.sem_inc(passed, 1)


def prepare(nc, t, sb_out):
    with ExitStack() as ctx:
        sem = Sems(nc, ctx, "prep")

        def sb(name, shape, dt=F32):
            return ctx.enter_context(nc.sbuf_tensor(name, shape, dt))

        nat = t["nat"] | {n: sb(f"nat_{n}", [P, 2, D]) for n in ("Win", "Wout")}
        nat_Wg = sb("nat_Wg", [E, D])
        tern = sb("tern", [P, 8 * D], BF16)
        tern1 = tern[:, :].rearrange("p (a b) -> p a b", b=D)
        tern2 = tern[:, :].rearrange("p (a b) -> p a b", b=F1)
        ones = sb("ones", [P, P])
        part = sb("part", [P, 8])
        powers = sb("powers", [P, 2, S])
        decays = sb("decays", [P, S])
        unit = sb("unit", [P, 2, S])
        wide = sb("wide", [P, 126])
        kvs = sb("kvs", [NB, D])
        kvsT = sb("kvsT", [P, 2, NB])
        uT = sb("uT", [P, 2, NB])
        bcol = sb("bcol", [P, 2])
        brow = sb("brow", [1, D])
        summ = sb("summ", [NB, D])
        tmp = sb("tmp", [P, 16])

        def psum(name, shape, dt=F32):
            return ctx.enter_context(nc.psum_tensor(name, shape, dt))

        turn = psum("turn", [P, 4, 512])
        turnb = psum("turnb", [P, 2, 1024], BF16)
        small = psum("small", [P, 512])
        acc = psum("acc", [P, 512])
        ident, identb = t["ident"], t["identb"]

        groups = []
        for n in ("W1", "W3", "B1", "B3"):
            hi, lo = t[n + "_hi"], t[n + "_lo"]
            for k in range(2):
                for f0, f1 in ((0, 4), (4, 7)):
                    groups.append((n, [nat[n][:, f, k * P:(k + 1) * P] for f in range(f0, f1)],
                                   hi[:, k, f0 * P:f1 * P], lo[:, k, f0 * P:f1 * P]))
        for n in ("A1", "A3", "B2"):
            groups.append((n, [nat[n][:, m, k * P:(k + 1) * P] for k in range(2) for m in range(2)],
                           t[n + "_hi"][:, :, :].rearrange("p a b -> p (a b)"),
                           t[n + "_lo"][:, :, :].rearrange("p a b -> p (a b)")))
        for n in ("W2", "A2"):
            for f0, f1 in ((0, 2), (2, 4), (4, 6), (6, 7)):
                groups.append((n, [nat[n][:, m, f * P:(f + 1) * P] for f in range(f0, f1) for m in range(2)],
                               t[n + "_hi"][:, f0:f1, :].rearrange("p a b -> p (a b)"),
                               t[n + "_lo"][:, f0:f1, :].rearrange("p a b -> p (a b)")))
        for n in ("Win", "Wout"):
            groups.append((n, [nat[n][:, m, k * P:(k + 1) * P] for k in range(2) for m in range(2)],
                           sb_out[n][:, :, :].rearrange("p a b -> p (a b)"), None))
        NG = len(groups)
        TERNARY_AT = (6, 14)

        block = ctx.enter_context(nc.Block())

        @block.sync
        def _(sp):
            def load(dst, src, name):
                sp.dma_start(dst, src).then_inc(sem("in_" + name), 16)

            for n in ("Win", "Wout"):
                load(nat[n][:, :, :], t[n + "_dram"], n)
            sp.dma_start(bcol[:, :], t["b_in_dram"], allow_slow_non_contiguous=True).then_inc(sem("in_rest"), 16)
            load(brow[:, :], t["b_out_dram"], "rest")
            load(nat_Wg[:, :], t["Wg_dram"], "rest")
            load(t["gamma"][:, :], t["gamma_dram"], "rest")
            load(t["beta"][:, :], t["beta_dram"], "rest")
            sp.wait_ge(sem("summ"), 1)
            sp.dma_start(t["summ_dram"], summ[:, :]).then_inc(sem("summ_out"), 16)
            sp.wait_ge(sem("summ_out"), 16)
            sp.wait_ge(sem("in_rest"), 80)

        @block.gpsimd
        def _(pool):
            nc.gpsimd.memset(ones[:, :], 1.0).then_inc(sem("ones"), 1)
            nc.gpsimd.memset(unit[:, :, :], 1.0).then_inc(sem("pm"), 1)
            nc.gpsimd.memset(wide[:, :], 0.0).then_inc(sem("wide0"), 1)
            pool.wait_ge(sem("pm"), 1)
            nc.gpsimd.affine_select(out=powers[:, :, :], in_=unit[:, :, :], compare_op=ALU.is_equal, fill=0.0,
                                    base=-(S - 1), pattern=[[-S, 2], [1, S]],
                                    channel_multiplier=1).then_inc(sem("pm"), 1)

        @block.scalar
        def _(act):
            for i, (n, tiles, hi, lo) in enumerate(groups):
                act.wait_ge(sem("turned"), i + 1)
                nc.scalar.copy(hi, turn[:, i % 4, 0:len(tiles) * P]).then_inc(sem("hi"), 1)

        @block.vector
        def _(dve):
            count = [0]

            def link(ins):
                count[0] += 1
                ins.then_inc(sem("dve"), 1)
                dve.wait_ge(sem("dve"), count[0])

            link(nc.vector.tensor_scalar(tmp[:, 1:2], t["expd"][:, :], 1.0, None, ALU.add))
            link(nc.vector.reciprocal(tmp[:, 2:3], tmp[:, 1:2]))
            dve.wait_ge(sem("pm"), 2)
            link(nc.vector.tensor_scalar(decays[:, :], unit[:, 0, :], tmp[:, 2:3], None, ALU.mult))
            link(nc.vector.tensor_tensor_scan(decays[:, :], decays[:, :], unit[:, 0, :], 0.0, ALU.mult, ALU.add))
            link(nc.vector.tensor_reduce(tmp[:, 3:4], decays[:, :], AX.X, ALU.add))
            link(nc.vector.tensor_scalar(tmp[:, 4:5], tmp[:, 3:4], 1.0 / S, None, ALU.mult))
            for b in range(2):
                link(nc.vector.tensor_tensor(powers[:, b, :], powers[:, b, :], decays[:, :], ALU.mult))
            link(nc.vector.tensor_reduce(tmp[:, 5:7], powers[:, :, :], AX.X, ALU.add))
            dve.wait_ge(sem("wide0"), 1)
            nc.vector.tensor_scalar(wide[:, 62:64], tmp[:, 5:7], 1.0 / S, None, ALU.mult).then_inc(sem("wide"), 1)
            for j, n in enumerate(("w1", "w2")):
                link(nc.vector.tensor_reduce(part[:, j:j + 1], nat[n][:, :, :], AX.XY, ALU.add,
                                             apply_absolute_value=True))
                link(nc.vector.tensor_copy(part[:, 2 + j:3 + j], part[:, j:j + 1]))
                nc.vector.tensor_copy(part[:, 4 + j:5 + j], part[:, j:j + 1]).then_inc(sem("wsum"), 1)

            def ternary(j, n, dst, out):
                dve.wait_ge(sem("total"), 2)
                link(nc.vector.tensor_scalar(dst[:, :], small[:, j:j + 1], 1.0 / (F1 * D), EPS, ALU.mult, ALU.max))
                link(nc.vector.reciprocal(tmp[:, 8 + j:9 + j], dst[:, :]))
                link(nc.vector.tensor_scalar(nat[n][:, :, :], nat[n][:, :, :], tmp[:, 8 + j:9 + j], ROUND, ALU.mult, ALU.add))
                link(nc.vector.tensor_scalar(nat[n][:, :, :], nat[n][:, :, :], -ROUND, 1.0, ALU.add, ALU.min))
                if j == 1:
                    dve.wait_ge(sem("turnedb"), 2)
                nc.vector.tensor_scalar(out[:, :, :], nat[n][:, :, :], -1.0, None, ALU.max).then_inc(sem("tern"), 1)

            def ternary_turned(i):
                dve.wait_ge(sem("turnedb"), i + 1)
                dst = t["w1T"] if i < 2 else t["w2T"]
                flat = dst[:, :, :].rearrange("p a b -> p (a b)")[:, (i % 2) * 1024:(i % 2 + 1) * 1024]
                nc.vector.tensor_copy(flat, turnb[:, i % 2, :]).then_inc(sem("ternT"), 1)

            ternary(0, "w1", t["mean1"], tern1)
            for i, (n, tiles, hi, lo) in enumerate(groups):
                if i == TERNARY_AT[0]:
                    ternary(1, "w2", t["mean2"], tern2)
                    ternary_turned(0)
                    ternary_turned(1)
                if i == TERNARY_AT[1]:
                    ternary_turned(2)
                    ternary_turned(3)
                dve.wait_ge(sem("hi"), i + 1)
                if lo is not None:
                    nc.vector.tensor_tensor(lo, turn[:, i % 4, 0:len(tiles) * P], hi, ALU.subtract).then_inc(sem("lo"), 1)
                else:
                    nc.vector.tensor_copy(tmp[:, 10:11], tmp[:, 8:9]).then_inc(sem("lo"), 1)
                    dve.wait_ge(sem("lo"), i + 1)
            dve.wait_ge(sem("WgT"), 1)
            nc.vector.tensor_copy(t["WgT"][:, :, :], small[:, 400:416].rearrange("p (a b) -> p a b", a=2)).then_inc(sem("WgT_sb"), 1)
            dve.wait_ge(sem("kvs"), 1)
            nc.vector.tensor_copy(kvs[:, :], acc[0:NB, 0:D]).then_inc(sem("kvs_sb"), 1)
            dve.wait_ge(sem("kvsT"), 1)
            nc.vector.tensor_copy(kvsT[:, :, :], small[:, 128:256].rearrange("p (a b) -> p a b", a=2)).then_inc(sem("kvsT_sb"), 1)
            dve.wait_ge(sem("in_rest"), 80)
            link(nc.vector.tensor_scalar(bcol[:, :], bcol[:, :], tmp[:, 4:5], None, ALU.mult))
            for n in ("gamma", "beta"):
                nc.vector.tensor_scalar(t[n][:, :], t[n][:, :], t["tanh"][:, 1:2], None, ALU.mult).then_inc(sem("gb"), 1)
            dve.wait_ge(sem("u"), 1)
            for m in range(2):
                nc.vector.tensor_scalar(uT[:, m, :], small[:, 256 + 64 * m:320 + 64 * m], bcol[:, m:m + 1], None,
                                        ALU.add).then_inc(sem("u_sb"), 1)
            dve.wait_ge(sem("s"), 1)
            nc.vector.tensor_copy(summ[:, :], acc[0:NB, D:2 * D]).then_inc(sem("summ"), 1)

        @block.tensor
        def _(pe):
            pe.wait_ge(sem("ones"), 1)
            for j in range(2):
                pe.wait_ge(sem("wsum"), j + 1)
                nc.tensor.matmul(small[:, j:j + 1], ones[:, :], part[:, 4 + j:5 + j], start=True, stop=True
                                 ).then_inc(sem("total"), 1)

            def turn_ternary(i):
                pe.wait_ge(sem("tern"), 1 + i // 2)
                if i >= 2:
                    pe.wait_ge(sem("ternT"), i - 1)
                for c in range(8):
                    if i < 2:
                        src = tern1[:, c, i * P:(i + 1) * P]
                    else:
                        f, m = divmod(8 * (i - 2) + c, 2)
                        src = tern2[:, m, f * P:(f + 1) * P]
                    last = nc.tensor.transpose(turnb[:, i % 2, c * P:(c + 1) * P], src, identb[:, :])
                last.then_inc(sem("turnedb"), 1)

            pe.wait_ge(sem("wide"), 1)
            for i in range(max(NG, TILES)):
                if i in TERNARY_AT:
                    j = TERNARY_AT.index(i)
                    turn_ternary(2 * j)
                    turn_ternary(2 * j + 1)
                if i < NG:
                    n, tiles, hi, lo = groups[i]
                    if n in ("Win", "Wout"):
                        pe.wait_ge(sem("in_" + n), 16)
                    if i >= 4:
                        pe.wait_ge(sem("lo"), i - 3)
                    for c, src in enumerate(tiles):
                        last = nc.tensor.transpose(turn[:, i % 4, c * P:(c + 1) * P], src, ident[:, :])
                    last.then_inc(sem("turned"), 1)
                if i < TILES:
                    last = nc.tensor.matmul(acc[0:NB, 0:D], wide[:, 62 - 2 * i:126 - 2 * i], t["ctx"][:, i, :],
                                            start=(i == 0), stop=(i == TILES - 1))
                    if i == TILES - 1:
                        last.then_inc(sem("kvs"), 1)
            pe.wait_ge(sem("in_rest"), 80)
            for m in range(2):
                last = nc.tensor.transpose(small[:, 400 + 8 * m:408 + 8 * m], nat_Wg[:, m * P:(m + 1) * P], ident[0:E, 0:E])
            last.then_inc(sem("WgT"), 1)
            pe.wait_ge(sem("kvs_sb"), 1)
            for m in range(2):
                last = nc.tensor.transpose(small[:, 128 + 64 * m:192 + 64 * m], kvs[:, m * P:(m + 1) * P], ident[0:NB, 0:NB])
            last.then_inc(sem("kvsT"), 1)
            pe.wait_ge(sem("kvsT_sb"), 1)
            pe.wait_ge(sem("hi"), NG)
            for m in range(2):
                for k in range(2):
                    last = nc.tensor.matmul(small[:, 256 + 64 * m:320 + 64 * m], sb_out["Win"][:, k, m * P:(m + 1) * P],
                                            kvsT[:, k, :], start=(k == 0), stop=(k == 1))
            last.then_inc(sem("u"), 1)
            pe.wait_ge(sem("u_sb"), 2)
            for k in range(2):
                nc.tensor.matmul(acc[0:NB, D:2 * D], uT[:, k, :], sb_out["Wout"][:, k, :], start=(k == 0), stop=False)
            nc.tensor.matmul(acc[0:NB, D:2 * D], ones[0:1, 0:NB], brow[:, :], start=False, stop=True).then_inc(sem("s"), 1)


class Step:

    def __init__(self, i, s):
        self.i, self.s = i, s
        self.static = isinstance(i, int)

    def half(self, k=0):
        return self.i * 4 + (self.s + k)

    def quarter(self, k=0):
        return self.i + (self.s + k) // 4

    def tile(self, k=0):
        return self.i * 2 + (self.s + k) // 2

    def slot(self, k=0, m=4):
        return (self.s + k) % m

    def in_range(self, k, n=HALVES):
        return not self.static or 0 <= 4 * self.i + self.s + k < n


def attention(nc, t):
    with ExitStack() as ctx:
        sem = Sems(nc, ctx, "att")

        def sb(name, shape, dt=F32):
            return ctx.enter_context(nc.sbuf_tensor(name, shape, dt))

        def psum(name, shape, dt=F32):
            return ctx.enter_context(nc.psum_tensor(name, shape, dt))

        def carve(start, size):
            return t["area"][:, start:start + size]

        size = 4 * HEADS * D
        q_pack, k_pack = (carve(k * size, size).rearrange("p (s h l) -> p s h l", s=4, h=HEADS) for k in range(2))
        probs = carve(2 * size, size).bitcast(F32).rearrange("p (h a l) -> p h a l", h=HEADS, a=2)
        pv_sb, nd = (carve(3 * size + k * 8 * D, 8 * D).bitcast(F32).rearrange("p (a b l) -> p a b l", a=2, b=2)
                     for k in range(2))
        q_parts = sb("q_parts", [P, 2, 3, D], BF16)
        k_parts = sb("k_parts", [P, 2, 3, D], BF16)
        z = sb("z", [P, 2, D])
        q_rest = sb("q_rest", [P, D])
        k_rest = sb("k_rest", [P, D])
        vT = sb("vT", [P, 2, 2, 2 * HEADS, 32])
        ones = sb("att_ones", [P, P])
        stat6 = sb("stat6", [P, 6])
        mean_var = sb("mean_var", [P, 2, 2])
        rstd = sb("rstd", [P, 2, 2])
        half_neg = sb("half_neg", [P, 1])
        neg_max = sb("neg_max", [P, 2, HEADS, 2])
        neg_rest = sb("neg_rest", [P, 2 * HEADS])
        neg_parts = sb("neg_parts", [P, 2, 3, 2 * HEADS], BF16)
        neg_rows = sb("neg_rows", [3 * 2 * HEADS, 2, P], BF16)

        s1 = psum("s1", [P, 4, 512])
        s2 = psum("s2", [P, 2, 512])
        pv = psum("pv", [P, 2, D])
        misc = psum("misc", [P, 512])
        negT = misc[0:48, 256:320].bitcast(BF16)

        xres, ctx_sb, identb = t["x"], t["ctx"], t["identb"]
        q_dram, k_dram, pv_dram = t["q_parts_dram"], t["k_parts_dram"], t["pv_dram"]
        SCALE = float(DH) ** -0.5

        first, last_step = -6, HALVES + 2
        LOOP = (2, (HALVES - 8) // 4)

        S1_AT = (-1, 1, 3, 4)
        GROUP_AT = (-1, 0, 5, 6)
        TURN_AT = 1
        NEG_AT = 4
        NEG_COPY = 1
        V_AT = 7
        PV_AT = 0

        def run(eng, step, inputs=()):
            for n in range(first, 4 * LOOP[0]):
                step(Step(n // 4, n % 4))
            for name in inputs:
                for i in range(len(LOADS) - 1):
                    eng.wait_ge(sem(f"{name}{i}"), 16)
                eng.wait_ge(sem(f"{name}{len(LOADS) - 1}"), 16 * -(-(TILES - LOADS[-1][0]) // PER_STEP))
            with eng.Fori(*LOOP) as i:
                for s in range(4):
                    step(Step(i, s))
            for n in range(4 * LOOP[1], last_step + 1):
                step(Step(n // 4, n % 4))

        block = ctx.enter_context(nc.Block())

        LOADS = ((0, 1), (1, 7), (7, TILES))
        PER_STEP = 2

        def loaded(eng, name, T):
            if isinstance(T, int):
                eng.wait_ge(sem(f"{name}{sum(T >= end for _, end in LOADS)}"), 16)

        nat = t["nat"]
        weights = [(nat[n][:, :, :], t[n + "_dram"]) for n in ("w1", "w2", "W1", "W3", "W2", "A1", "A3", "A2")]
        weights += [(nat[n][:, f, :].rearrange("p (e r) -> p e r", e=E), t[n + "_dram"][f])
                    for n, count in (("B1", FT), ("B3", FT), ("B2", 2)) for f in range(count)]
        LAST = last_step + 1 - 4 * LOOP[1]

        @block.sync
        def _(sp):
            for dst, src in ((t["g"][:, 0:2], t["g_xattn_dram"]), (t["g"][:, 2:4], t["g_ffn_dram"]),
                             (t["g"][:, 4:5], t["gamma0_dram"]), (t["g"][:, 5:6], t["decay_dram"])):
                sp.dma_start(dst, src).then_inc(sem("gains_in"), 16)
            def load_rows(i, a, b):
                sp.dma_start(t["x"][:, a:b, :], t["x_dram"][:, a:b, :]).then_inc(sem(f"x_in{i}"), 16)
                sp.dma_start(t["ctx"][:, a:b, :], t["ctx_dram"][:, a:b, :]).then_inc(sem(f"ctx_in{i}"), 16)

            for i in range(len(LOADS) - 1):
                load_rows(i, *LOADS[i])

            def step(n):
                if n.static and n.i < LOOP[0]:
                    a = LOADS[-1][0] + PER_STEP * (4 * n.i + n.s - first)
                    if a < TILES:
                        load_rows(len(LOADS) - 1, a, min(a + PER_STEP, TILES))
                elif n.static:
                    for dst, src in weights[4 * (n.i - LOOP[1]) + n.s::LAST]:
                        sp.dma_start(dst, src).then_inc(sem("weights_in"), 16)
                if n.in_range(3):
                    if n.static:
                        sp.wait_ge(sem("pack_zeroed"), 2)
                    h, slot, u = n.slot(3, 2), n.slot(3), n.slot(3) // 2
                    at_least(sp, sem(f"parts_out{u}"), n.quarter(3) * 128 + 128, passed=t["passed"])
                    at_least(sp, sem("s2_done"), n.half(0) * 8, passed=t["passed"])
                    rows = q_dram[u, :, :, h * 8:h * 8 + 8, :].rearrange("a d h l -> (a d) (h l)")
                    sp.dma_start(q_pack[0:72, slot, :, :].rearrange("p h l -> p (h l)"),
                                 rows.unsqueeze(0).to_broadcast([3, 24, HEADS * D])).then_inc(sem(f"pack_in{slot}"), 16)
                    sp.dma_start(k_pack[0:72, slot, :, :].rearrange("p h l -> p (h l)"),
                                 t["k_windows"](u, h)).then_inc(sem(f"pack_in{slot}"), 16)
                if n.in_range(-1):
                    b, u = n.slot(-1, 2), n.slot(-1) // 2
                    at_least(sp, sem("pv_sb"), n.half(0), passed=t["passed"])
                    if b == 0:
                        at_least(sp, sem(f"nd_in{u}"), n.quarter(-1) * 32, passed=t["passed"])
                    sp.dma_start(pv_dram[u, b].rearrange("g p l -> p g l"), pv_sb[:, b, :, :]
                                 ).then_inc(sem(f"pv_out{b}"), 16)
                for odd, k in ((1, 5), (0, 4)):
                    if n.s % 2 != odd or not n.in_range(k):
                        continue
                    u = n.slot(k) // 2
                    at_least(sp, sem("q_parts" if odd else "k_parts"), n.tile(k) + 1, passed=t["passed"])
                    for b in range(2):
                        at_least(sp, sem(f"pack_in{2 * u + b}"), n.quarter(k) * 32, passed=t["passed"])
                    if odd:
                        for a in range(3):
                            sp.dma_start(q_dram[u, a].rearrange("d h l -> h d l"), q_parts[:, u, a, :]
                                         ).then_inc(sem(f"parts_out{u}"), 16)
                    else:
                        for a in range(5):
                            sp.dma_start(k_dram[u, a].rearrange("d h l -> h d l"), k_parts[:, u, a % 3, :]
                                         ).then_inc(sem(f"parts_out{u}"), 16)
                if n.s % 2 == 1 and n.in_range(-3):
                    u = n.slot(-3) // 2
                    for b in range(2):
                        at_least(sp, sem(f"pv_out{b}"), n.tile(-3) * 16 + 16, passed=t["passed"])
                    at_least(sp, sem("x_done"), n.tile(-3), passed=t["passed"])
                    for k in range(2):
                        src = pv_dram[u].rearrange("b g (j r) l -> (b g j) r l", r=32)[:, 8 * k:8 * k + 8, :]
                        sp.dma_start(nd[:, u, k, :], src).then_inc(sem(f"nd_in{u}"), 16)

            run(sp, step)
            sp.wait_ge(sem("weights_in"), 16 * len(weights))

        @block.gpsimd
        def _(pool):
            ident = t["ident"]
            nc.gpsimd.memset(ones[:, :], 1.0).then_inc(sem("ones"), 1)
            pool.wait_ge(sem("ones"), 1)
            nc.gpsimd.affine_select(out=ident[:, :], in_=ones[:, :], compare_op=ALU.is_equal, fill=0.0,
                                    base=0, pattern=[[-1, P]], channel_multiplier=1).then_inc(sem("ident"), 1)
            pool.wait_ge(sem("ident"), 1)
            nc.gpsimd.tensor_copy(identb[:, :], ident[:, :]).then_inc(sem("ident"), 1)
            nc.gpsimd.memset(vT[:, :, :, :, :], 0.0).then_inc(sem("zeroed"), 1)
            nc.gpsimd.memset(half_neg[:, :], -0.5).then_inc(sem("zeroed"), 1)
            pool.wait_ge(sem("zeroed"), 2)
            pool.wait_ge(sem("pack_zeroed"), 1)
            nc.gpsimd.memset(k_pack[96:99, :, :, :], 1.0).then_inc(sem("constants"), 1)
            pool.wait_ge(sem("constants"), 1)
            nc.gpsimd.memset(vT[:, :, :, :, 8:16], 1.0).then_inc(sem("constants"), 1)

            def step(n):
                if n.s % 2 == 0 and n.in_range(6):
                    T, u = n.tile(6), n.slot(6) // 2
                    at_least(pool, sem("mean_var"), T + 1, passed=t["passed"])
                    nc.gpsimd.tensor_scalar(rstd[:, u, 0:1], mean_var[:, u, 1:2], EPS, 1.0, ALU.add, ALU.mult
                                            ).then_inc(sem("var_eps"), 1)
                    at_least(pool, sem("var_eps"), T + 1, passed=t["passed"])
                    nc.gpsimd.tensor_tensor(rstd[:, u, 1:2], rstd[:, u, 0:1], half_neg[:, :], ALU.pow
                                            ).then_inc(sem("rstd"), 1)
                    at_least(pool, sem("z"), T + 1, passed=t["passed"])
                    at_least(pool, sem(f"parts_out{u}"), n.quarter(6) * 128, passed=t["passed"])
                    split(z[:, u, :], q_parts, q_rest, u, T, "q")
                if n.s % 2 == 1 and n.in_range(5):
                    T, u = n.tile(5), n.slot(5) // 2
                    loaded(pool, "ctx_in", T)
                    at_least(pool, sem("vT_psum"), T - 1, passed=t["passed"])
                    at_least(pool, sem(f"parts_out{u}"), n.quarter(5) * 128, passed=t["passed"])
                    split(ctx_sb[:, bass.ds(T, 1), :].rearrange("p a l -> p (a l)"), k_parts, k_rest, u, T, "k")
                if n.s % 2 == 0 and n.in_range(-4):
                    T, u = n.tile(-4), n.slot(-4) // 2
                    row = xres[:, bass.ds(T, 1), :].rearrange("p a l -> p (a l)")
                    at_least(pool, sem("recip"), T * 2 + 2, passed=t["passed"])
                    nc.gpsimd.tensor_tensor(nd[:, u, 0, :], nd[:, u, 0, :], nd[:, u, 1, :], ALU.mult
                                            ).then_inc(sem("ratio"), 1)
                    at_least(pool, sem("ratio"), T + 1, passed=t["passed"])
                    if n.static:
                        pool.wait_ge(sem("gain0"), 1)
                    nc.gpsimd.tensor_scalar(nd[:, u, 1, :], nd[:, u, 0, :], t["gain0"][:, :], 1.0, ALU.mult, ALU.mult
                                            ).then_inc(sem("gained"), 1)
                    at_least(pool, sem("gained"), T + 1, passed=t["passed"])
                    nc.gpsimd.tensor_tensor(row, row, nd[:, u, 1, :], ALU.add).then_inc(sem("x_done"), 1)

            def split(src, parts, rest, u, T, name):
                done = sem(name + "_split")
                nc.gpsimd.tensor_copy(parts[:, u, 0, :], src).then_inc(done, 1)
                at_least(pool, done, T * 3 + 1, passed=t["passed"])
                nc.gpsimd.tensor_tensor(rest[:, :], src, parts[:, u, 0, :], ALU.subtract).then_inc(done, 1)
                at_least(pool, done, T * 3 + 2, passed=t["passed"])
                nc.gpsimd.tensor_copy(parts[:, u, 1, :], rest[:, :]).then_inc(done, 1)
                at_least(pool, done, T * 3 + 3, passed=t["passed"])
                nc.gpsimd.tensor_tensor(parts[:, u, 2, :], rest[:, :], parts[:, u, 1, :], ALU.subtract
                                        ).then_inc(sem(name + "_parts"), 1)
                at_least(pool, sem(name + "_parts"), T + 1, passed=t["passed"])

            run(pool, step, ("ctx_in",))
            pool.wait_ge(sem("x_done"), TILES)

        @block.scalar
        def _(act):
            act.wait_ge(sem("gains_in"), 64)
            nc.scalar.activation(t["tanh"][:, 0:4], t["g"][:, 0:4], ACT.Tanh).then_inc(sem("tanh"), 1)
            nc.scalar.activation(t["expd"][:, :], t["g"][:, 5:6], ACT.Exp, scale=-1.0).then_inc(sem("expd"), 1)

            def step(n):
                for hd in range(HEADS):
                    if n.in_range(0):
                        at_least(act, sem("s2_done"), n.half(0) * 8 + (hd + 1))
                        at_least(act, sem("pv_group"), n.half(0) * 2 + (hd // 4 - 1))
                        nc.scalar.activation(probs[:, hd, :, :].rearrange("p a q -> p (a q)"), s2[:, hd % 2, :],
                                             ACT.Exp, scale=SCALE).then_inc(sem("exp_done"), 1)
                    if hd == PV_AT and n.in_range(-1):
                        at_least(act, sem("pv_group"), n.half(0) * 2)
                        at_least(act, sem(f"pv_out{n.slot(-1, 2)}"), n.tile(-1) * 16)
                        nc.scalar.copy(pv_sb[:, n.slot(-1, 2), :, :], pv[:, :, :]).then_inc(sem("pv_sb"), 1)
                    if hd == NEG_AT and n.in_range(1):
                        at_least(act, sem("neg_rows"), n.half(2), passed=t["passed"])
                        act.dma_start(q_pack[96:99, n.slot(1), :, :], neg_rows[:, n.slot(1, 2), :]
                                      ).then_inc(sem(f"neg_in{n.slot(1, 2)}"), 16)
                    if hd == 7 and n.s % 2 == 1 and n.in_range(1):
                        T, u = n.tile(1), n.slot(1) // 2
                        at_least(act, sem("vT_psum"), T + 1)
                        at_least(act, sem("pv_group"), n.half(0) * 2 - 2)
                        if n.static:
                            at_least(act, sem("constants"), 2)
                        nc.scalar.copy(vT[:, u, :, :, 0:8], misc[:, 0:256].rearrange("p (a h d) -> p a h d", a=2, d=8)
                                       ).then_inc(sem("vT"), 1)

            run(act, step)

        @block.vector
        def _(dve):
            for pack in (k_pack, q_pack):
                nc.vector.memset(pack[:, :, :, :], 0.0).then_inc(sem("pack_zeroed"), 1)
            dve.wait_ge(sem("tanh"), 1)
            nc.vector.tensor_tensor(t["gain0"][:, :], t["tanh"][:, 0:1], t["g"][:, 4:5], ALU.mult).then_inc(sem("gain0"), 1)

            def step(n):
                for p in range(4):
                    if n.in_range(2):
                        at_least(dve, sem("s1_done"), n.half(2) * 4 + (p + 1))
                        if p == 0:
                            at_least(dve, sem("neg_parts"), n.half(1))
                        nc.vector.tensor_reduce(
                            neg_max[:, n.slot(0, 2), 2 * p:2 * p + 2, :],
                            s1[:, 2 * (p % 2):2 * (p % 2) + 2, :].rearrange("p a (b l) -> p a b l", b=2),
                            AX.X, ALU.max, negate=True).then_inc(sem("max_done"), 1)
                    if p == 0 and n.s % 2 == 0 and n.in_range(6):
                        T = n.tile(6)
                        row = xres[:, bass.ds(T, 1), :].rearrange("p a l -> p (a l)")
                        loaded(dve, "x_in", T)
                        at_least(dve, sem("mean_var"), T, passed=t["passed"])
                        nc.vector.bn_stats(stat6[:, :], row).then_inc(sem("stats"), 1)
                    if p == 1 and n.s % 2 == 0 and n.in_range(6):
                        T, u = n.tile(6), n.slot(6) // 2
                        at_least(dve, sem("stats"), T + 1, passed=t["passed"])
                        at_least(dve, sem("z"), T - 1, passed=t["passed"])
                        nc.vector.bn_aggr(mean_var[:, u, :], stat6[:, :]).then_inc(sem("mean_var"), 1)
                    if p == NEG_COPY and n.in_range(1):
                        at_least(dve, sem("negT"), n.half(2))
                        at_least(dve, sem(f"neg_in{n.slot(1, 2)}"), n.tile(1) * 16)
                        nc.vector.tensor_copy(neg_rows[:, n.slot(1, 2), :], negT).then_inc(sem("neg_rows"), 1)
                    if p in (1, 2) and n.s % 2 == 0 and n.in_range(-4):
                        T, u, half = n.tile(-4), n.slot(-4) // 2, slice((p - 1) * P, p * P)
                        at_least(dve, sem(f"nd_in{u}"), n.quarter(-4) * 32 + 32)
                        nc.vector.reciprocal(nd[:, u, 1, half], nd[:, u, 1, half]).then_inc(sem("recip"), 1)
                    if p == 3 and n.s % 2 == 0 and n.in_range(6):
                        T, u = n.tile(6), n.slot(6) // 2
                        row = xres[:, bass.ds(T, 1), :].rearrange("p a l -> p (a l)")
                        at_least(dve, sem("rstd"), T + 1)
                        at_least(dve, sem("q_parts"), T - 1)
                        nc.vector.tensor_scalar(z[:, u, :], row, mean_var[:, u, 0:1], rstd[:, u, 1:2],
                                                ALU.subtract, ALU.mult).then_inc(sem("z"), 1)
                if n.in_range(2):
                    split_maxima(n)

            def split_maxima(n):
                b, h = n.slot(2, 2), n.half(2)
                flat = neg_max[:, b, :, :].rearrange("p a b -> p (a b)")
                part = neg_parts[:, b, :, :]
                at_least(dve, sem("max_done"), h * 4 + 4)
                at_least(dve, sem("negT"), h - 1)
                nc.vector.tensor_copy(part[:, 0, :], flat).then_inc(sem("neg_split"), 1)
                dve.wait_ge(sem("neg_split"), h * 3 + 1)
                nc.vector.tensor_tensor(neg_rest[:, :], flat, part[:, 0, :], ALU.subtract).then_inc(sem("neg_split"), 1)
                dve.wait_ge(sem("neg_split"), h * 3 + 2)
                nc.vector.tensor_copy(part[:, 1, :], neg_rest[:, :]).then_inc(sem("neg_split"), 1)
                dve.wait_ge(sem("neg_split"), h * 3 + 3)
                nc.vector.tensor_tensor(part[:, 2, :], neg_rest[:, :], part[:, 1, :], ALU.subtract
                                        ).then_inc(sem("neg_parts"), 1)

            run(dve, step, ("x_in",))

        @block.tensor
        def _(pe):
            pe.wait_ge(sem("constants"), 2)
            pe.wait_ge(sem("ident"), 2)

            def pv_group(n, k, g, a):
                if not n.in_range(k):
                    return
                b, u = n.slot(k, 2), n.slot(k) // 2
                if a == 0:
                    at_least(pe, sem("exp_done"), n.half(k) * 8 + (4 * g + 4))
                    if g == 0:
                        at_least(pe, sem("vT"), n.tile(k) + 1)
                        at_least(pe, sem("pv_sb"), n.half(k))
                for j in range(4):
                    last = nc.tensor.matmul(pv[32 * j:32 * j + 32, g, :], vT[:, u, a, 8 * b + 4 * g + j, :],
                                            probs[:, 4 * g + j, a, :], start=(a == 0), stop=(a == 1),
                                            skip_group_check=True)
                if a == 1:
                    last.then_inc(sem("pv_group"), 1)

            def scores_for_max(n, p):
                slot = n.slot(2)
                if p == 0:
                    at_least(pe, sem(f"pack_in{slot}"), n.quarter(2) * 32 + 32)
                at_least(pe, sem("max_done"), n.half(2) * 4 + (p - 1))
                for hd in (2 * p, 2 * p + 1):
                    for m in range(2):
                        last = nc.tensor.matmul(s1[:, 2 * (p % 2) + hd % 2, m * D:(m + 1) * D],
                                                q_pack[0:96, slot, hd, m * P:(m + 1) * P],
                                                k_pack[0:96, slot, hd, :], start=True, stop=True)
                last.then_inc(sem("s1_done"), 1)

            def scores(n, hd):
                slot = n.slot(0)
                if hd == 0:
                    at_least(pe, sem(f"neg_in{n.slot(0, 2)}"), n.tile(0) * 16 + 16)
                    at_least(pe, sem(f"pack_in{slot}"), n.quarter(0) * 32 + 32)
                at_least(pe, sem("exp_done"), n.half(0) * 8 + (hd - 1))
                for m in range(2):
                    last = nc.tensor.matmul(s2[:, hd % 2, m * D:(m + 1) * D], k_pack[0:99, slot, hd, m * P:(m + 1) * P],
                                            q_pack[0:99, slot, hd, :], start=True, stop=True)
                last.then_inc(sem("s2_done"), 1)

            def turn_maxima(n):
                at_least(pe, sem("neg_parts"), n.half(2), passed=t["passed"])
                at_least(pe, sem("neg_rows"), n.half(1), passed=t["passed"])
                at_least(pe, sem("vT"), n.tile(2), passed=t["passed"])
                nc.tensor.transpose(negT, neg_parts[:, n.slot(1, 2), :, :].rearrange("p a b -> p (a b)"),
                                    identb[:, :]).then_inc(sem("negT"), 1)

            def turn_v(n):
                T, u = n.tile(1), n.slot(1) // 2
                at_least(pe, sem("k_parts"), T + 1)
                at_least(pe, sem("vT"), T)
                at_least(pe, sem("neg_rows"), n.half(2))
                for m in range(2):
                    for a in range(3):
                        last = nc.tensor.matmul(misc[:, m * P:(m + 1) * P], k_parts[:, u, a, m * P:(m + 1) * P],
                                                identb[:, :], start=(a == 0), stop=(a == 2))
                last.then_inc(sem("vT_psum"), 1)

            def step(n):
                for hd in range(-1, HEADS):
                    if hd >= 0 and n.in_range(0):
                        scores(n, hd)
                    if hd == TURN_AT and n.in_range(1):
                        turn_maxima(n)
                    for p in range(4):
                        if hd == S1_AT[p] and n.in_range(2):
                            scores_for_max(n, p)
                    for i, (k, g, a) in enumerate(((-1, 1, 0), (-1, 1, 1), (0, 0, 0), (0, 0, 1))):
                        if hd == GROUP_AT[i]:
                            pv_group(n, k, g, a)
                    if hd == V_AT and n.s % 2 == 1 and n.in_range(1):
                        turn_v(n)

            run(pe, step)


CT = 4
CHUNKS = TILES // CT
N = CT * P
TINY = EPS * 1e-12 / 32.0

PER = {
    "dve_pre": 48, "mv1": 1, "pow1": 1, "q_in": 1, "xq": 1, "xqT_ps": 1, "xqT": 1, "hp": 4, "gelu": 4, "ssq": 4,
    "absmax": 4, "hr": 4, "hq": 4, "hqT_ps": 4, "hqT": 4, "y": 4, "y2": 4, "norm2": 1, "pool_pre": 5, "mv2": 1,
    "rstd2": 1, "xm": 1, "ys": 1, "mv3": 1, "rstd3": 1, "xb": 1, "x3": 1, "mv4": 1, "rstd4": 1, "z": 1,
    "zT": 1, "xTf": 1, "x_hi": 1, "x_lo": 1, "logits_ps": 1, "logits": 1, "gap": 1, "exp_gap": 1, "routing": 1,
    "gT_ps": 1, "gT": 1, "spread_ps": 6, "spread": 6, "summ_in": 16 * CT,
    "a_ps": 4, "a_hi": 4, "a_lo": 4, "a_masked": 8, "f0": 7, "fd": 7, "silu": 14, "gated": 14, "weighted": 14,
    "mixed": 7, "g1_hi": 7, "gc_hi": 7, "g1_lo": 7, "gc_lo": 7, "p_ps": 4, "p_read": 4, "m_hi": 2, "m_lo": 2,
    "dve_main": 2, "down": 4, "out_sb": 4, "stored": 16,
}


def tokens(nc, t):
    with ExitStack() as ctx:
        sem = Sems(nc, ctx, "tok")

        def sb(name, shape, dt=F32):
            return ctx.enter_context(nc.sbuf_tensor(name, shape, dt))

        def psum(name, shape, dt=F32):
            return ctx.enter_context(nc.psum_tensor(name, shape, dt))

        def need(eng, name, c, k, apart=False):
            apart = apart or eng.engine in (nc.gpsimd.engine, nc.sync.engine)
            at_least(eng, sem(name), c * PER[name] + (PER[name] + k), passed=t["passed"] if apart else None)

        xres, identb, ident = t["x"], t["identb"], t["ident"]

        st6 = sb("st6", [P, CT, 6])
        mv = sb("mv", [P, CT, 2])
        sm = sb("sm", [P, 16, CT])
        powers = sb("exponents", [P, 3, CT])
        d4 = sb("d4", [P, CT, D])
        xq = sb("xq", [P, CT, D], BF16)
        xqT = sb("xqT", [P, 2, N], BF16)
        h = sb("h", [P, 2, F1])
        junk = sb("junk", [P, F1], BF16)
        hq = sb("hq", [P, 2, F1], BF16)
        hqT = sb("hqT", [P, 8, P], BF16)
        y2 = sb("y2", [P, CT, D])
        xTf = h[:, 0, :].rearrange("p (a b) -> p a b", b=N)
        summ = h[:, 1, :].rearrange("p (a b) -> p a b", b=D)
        y4 = d4
        xT_hi = sb("xT_hi", [P, 2, N], BF16)
        xT_lo = sb("xT_lo", [P, 2, N], BF16)
        logits = sb("logits", [P, CT, E])
        top = sb("top", [P, CT, 8])
        top_i = sb("top_i", [P, CT, 8], U32)
        top_f = sb("top_f", [P, CT, 2])
        experts = sb("experts", [P, CT, E])
        onehot = sb("onehot", [P, CT, E])
        rw = sb("rw", [P, CT, 2])
        rw_rest = sb("rw_rest", [P, CT, 2])
        gpack = sb("gpack", [P, CT, 32], BF16)
        gT = sb("gT", [32, N], BF16)
        sel = sb("sel", [32, 6, P], BF16)
        mask = sb("mask", [P, 4, N], BF16)
        sel_ones = mask[0:32, :, 0:P]
        rw_rows = sb("rw_rows", [P, 2, N])

        a_hi = sb("a_hi", [P, 4, N], BF16)
        a_lo = sb("a_lo", [P, 4, N], BF16)
        am = sb("a_masked", [P, 4, 2, 2, N], BF16)
        sil = sb("sil", [P, 2, N])
        gated = sb("gated", [P, 2, N])
        w0 = sb("weighted0", [P, 2, N])
        w1 = sb("weighted1", [P, 2, N])
        wc = sb("mixed", [P, 2, N])
        g1_hi, g1_lo = sb("g1_hi", [P, FT, N], BF16), sb("g1_lo", [P, FT, N], BF16)
        gc_hi, gc_lo = sb("gc_hi", [P, FT, N], BF16), sb("gc_lo", [P, FT, N], BF16)
        pm = [sil[:, 0, :], sil[:, 1, :], gated[:, 0, :]]
        m_hi, m_lo = a_hi, a_lo
        out_sb = wc[:, :, :].rearrange("p a (b d) -> p (a b) d", d=D)

        X = psum("X", [P, 4, 512])
        Y = psum("Y", [P, 4, 512])
        Y0b = Y[:, 0, :].bitcast(BF16)
        Y3b = Y[:, 3, :].bitcast(BF16)
        BANKS = (2, 3, 0, 1)
        ORDER = [(0, 0)] + [o for f in range(1, FT) for o in ((f, 0), (f - 1, 1))] + [(FT - 1, 1)]
        AT = {o: n for n, o in enumerate(ORDER)}

        def xrow(c, j):
            return xres[:, bass.ds(c * CT + j, 1), :].rearrange("p a l -> p (a l)")

        def xchunk(c):
            return xres[:, bass.ds(c * CT, CT), :].rearrange("p a l -> p (a l)")

        def xchunk4(c):
            return xres[:, bass.ds(c * CT, CT), :]

        def flat(ap):
            return ap.rearrange("p a b -> p (a b)")

        block = ctx.enter_context(nc.Block())

        def run(eng, step, begin=None):
            if begin:
                begin(0)
            step(None, 0, 1)
            with eng.Fori(0, CHUNKS - 2) as c:
                step(c, c + 1, c + 2)
            step(CHUNKS - 2, CHUNKS - 1, None)
            step(CHUNKS - 1, None, None)

        @block.sync
        def _(sp):
            for name in PER:
                sp.sem_inc(sem(name), PER[name])

            def step(c, e, g):
                if e is not None:
                    need(sp, "hq", e, CT)
                    for j in range(CT):
                        src = t["summ_dram"][bass.ds((e * CT + j) * 2, 2), :].unsqueeze(1).to_broadcast([2, S, D])
                        sp.dma_start(summ[:, j, :], src).then_inc(sem("summ_in"), 16)
                if c is not None:
                    need(sp, "out_sb", c, CT)
                    sp.dma_start(t["out_dram"][:, bass.ds(c * CT, CT), :], out_sb[:, :, :]).then_inc(sem("stored"), 16)

            run(sp, step)
            need(sp, "stored", CHUNKS - 1, 16)

        @block.gpsimd
        def _(pool):
            consts = sem("consts")
            nc.gpsimd.memset(sel_ones[:, :, :], 1.0).then_inc(consts, 1)
            nc.gpsimd.memset(gpack[:, :, :], 0.0).then_inc(consts, 1)
            nc.gpsimd.iota(top_i[:, :, :], pattern=[[0, CT], [1, E]], base=0, channel_multiplier=0).then_inc(consts, 1)
            pool.wait_ge(consts, 3)
            nc.gpsimd.tensor_copy(experts[:, :, :], top_i[:, :, :]).then_inc(consts, 1)
            nc.gpsimd.affine_select(
                out=sel[:, 0:4, :].rearrange("p (a b) (m r) -> p a b m r", a=2, m=4),
                in_=sel_ones[:, :, :].rearrange("p (a b) (m r) -> p a b m r", a=2, m=4),
                compare_op=ALU.is_equal, fill=0.0, base=0, pattern=[[-8, 2], [-4, 2], [-1, 4], [0, R]],
                channel_multiplier=1).then_inc(consts, 1)
            nc.gpsimd.affine_select(out=sel[:, 4:6, :], in_=sel_ones[:, 0:2, :], compare_op=ALU.is_ge, fill=0.0,
                                    base=-16, pattern=[[-3, 2], [0, P]], channel_multiplier=1).then_inc(consts, 1)
            pool.wait_ge(consts, 6)
            nc.gpsimd.affine_select(out=sel[:, 4:6, :], in_=sel[:, 4:6, :], compare_op=ALU.is_ge, fill=0.0,
                                    base=18, pattern=[[3, 2], [0, P]], channel_multiplier=-1).then_inc(consts, 1)
            for k, value in enumerate((-0.5, 0.5, 2.718281828459045)):
                nc.gpsimd.memset(powers[:, k, :], value).then_inc(consts, 1)
            pool.wait_ge(consts, 10)

            def rstd(c, mv_name, name, k):
                need(pool, mv_name, c, 1)
                nc.gpsimd.tensor_scalar(sm[:, 1, :], mv[:, :, 1], EPS, 1.0, ALU.add, ALU.mult).then_inc(sem("pool_pre"), 1)
                need(pool, "pool_pre", c, k)
                nc.gpsimd.tensor_tensor(sm[:, 0, :], sm[:, 1, :], powers[:, 0, :], ALU.pow).then_inc(sem(name), 1)

            def weigh(c, o):
                f, slot = ORDER[o]
                need(pool, "gated", c, o + 1)
                if slot == 0:
                    need(pool, "mixed", c, max(f - 1, 0))
                    nc.gpsimd.tensor_tensor(w0[:, f % 2, :], gated[:, o % 2, :], rw_rows[:, 0, :], ALU.mult
                                            ).then_inc(sem("weighted"), 1)
                else:
                    need(pool, "g1_lo", c, max(f - 1, 0))
                    nc.gpsimd.tensor_tensor(w1[:, f % 2, :], gated[:, o % 2, :], rw_rows[:, 1, :], ALU.mult
                                            ).then_inc(sem("weighted"), 1)
                    need(pool, "weighted", c, o + 1)
                    need(pool, "gc_lo", c, max(f - 1, 0))
                    if f == 0:
                        need(pool, "stored", c, 0)
                    nc.gpsimd.tensor_tensor(wc[:, f % 2, :], w0[:, f % 2, :], w1[:, f % 2, :], ALU.add
                                            ).then_inc(sem("mixed"), 1)

            def begin(c):
                need(pool, "mv1", c, 1)
                nc.gpsimd.tensor_tensor(sm[:, 2, :], mv[:, :, 1], powers[:, 1, :], ALU.pow).then_inc(sem("pool_pre"), 1)
                need(pool, "pool_pre", c, 1)
                rstd(c, "mv1", "pow1", 2)
                need(pool, "q_in", c, 1)
                need(pool, "xqT_ps", c, 0)
                nc.gpsimd.tensor_scalar(flat(xq[:, :, :]), flat(d4[:, :, :]), -ROUND, 1.0, ALU.add, ALU.mult
                                        ).then_inc(sem("xq"), 1)

            def hidden_rounded(c, j):
                need(pool, "hr", c, j + 1)
                need(pool, "hqT_ps", c, j - 1)
                nc.gpsimd.tensor_scalar(hq[:, j % 2, :], h[:, j % 2, :], -ROUND, 1.0, ALU.add, ALU.mult
                                        ).then_inc(sem("hq"), 1)

            def step(c, e, g):
                if c is not None:
                    need(pool, "spread", c, 6)
                    weigh(c, 0)
                for s in range(1, FT):
                    if e is not None and s <= 4:
                        hidden_rounded(e, s - 1)
                    if e is not None and s == 5:
                        need(pool, "ssq", e, 4)
                        nc.gpsimd.tensor_tensor(sm[:, 9, :], sm[:, 8, :], powers[:, 1, :], ALU.pow
                                                ).then_inc(sem("norm2"), 1)
                    if c is not None:
                        weigh(c, 2 * s - 1)
                    if e is not None and s == 6:
                        rstd(e, "mv2", "rstd2", 3)
                    if c is not None:
                        weigh(c, 2 * s)
                if e is not None:
                    rstd(e, "mv3", "rstd3", 4)
                if c is not None:
                    weigh(c, 2 * FT - 1)
                if e is not None:
                    need(pool, "xm", e, 1)
                    nc.gpsimd.tensor_tensor(xchunk4(e), xchunk4(e), t["beta"][:, :].unsqueeze(1).to_broadcast([P, CT, D]),
                                            ALU.add).then_inc(sem("xb"), 1)
                    rstd(e, "mv4", "rstd4", 5)
                    need(pool, "gap", e, 1)
                    nc.gpsimd.tensor_tensor(sm[:, 12, :], powers[:, 2, :], sm[:, 11, :], ALU.pow).then_inc(sem("exp_gap"), 1)
                if g is not None:
                    begin(g)

            run(pool, step, begin)

        @block.scalar
        def _(act):
            def silu(c, o):
                f, slot = ORDER[o]
                need(act, "fd" if slot else "f0", c, f + 1)
                need(act, "gated", c, o - 1)
                if o == 0:
                    need(act, "m_lo", c, 0)
                nc.scalar.activation(sil[:, o % 2, :], X[:, 2 * (f % 2), :], ACT.Silu).then_inc(sem("silu"), 1)

            def high(c, f):
                need(act, "weighted", c, AT[f, 1] + 1)
                need(act, "p_ps", c, 0)
                nc.scalar.copy(g1_hi[:, f, :], w1[:, f % 2, :]).then_inc(sem("g1_hi"), 1)
                need(act, "mixed", c, f + 1)
                need(act, "down", c, 0)
                nc.scalar.copy(gc_hi[:, f, :], wc[:, f % 2, :]).then_inc(sem("gc_hi"), 1)

            def a_high(c, q):
                need(act, "a_ps", c, q + 1)
                if q == 0:
                    need(act, "a_masked", c, 0)
                    need(act, "down", c, 0)
                nc.scalar.copy(a_hi[:, q, :], X[:, q, :]).then_inc(sem("a_hi"), 1)

            def spread(c):
                need(act, "m_lo", c, 0)
                need(act, "mixed", c, 0)
                for v in range(6):
                    need(act, "spread_ps", c, v + 1)
                    dst = mask[:, v, :] if v < 4 else rw_rows[:, v - 4, :]
                    nc.scalar.copy(dst, Y[:, 2 + v % 2, :]).then_inc(sem("spread"), 1)

            def x_turned(c):
                need(act, "xqT_ps", c, 1)
                need(act, "hp", c, 0)
                nc.scalar.copy(flat(xqT[:, :, :]), Y0b).then_inc(sem("xqT"), 1)

            def hidden(c, j):
                need(act, "hp", c, j + 1)
                need(act, "hq", c, j - 1)
                if j == 0:
                    need(act, "logits_ps", c, 0)
                    need(act, "x_lo", c, 0)
                if j == 1:
                    need(act, "ys", c, 0)
                need(act, "ssq", c, j)
                nc.scalar.activation(h[:, j % 2, :], flat(Y[:, 1:3, :]), ACT.Gelu, scale=sm[:, 10, j:j + 1]
                                     ).then_inc(sem("gelu"), 1)
                need(act, "gelu", c, j + 1)
                nc.scalar.activation(junk[:, :], h[:, j % 2, :], ACT.Square, accum_out=sm[:, 8, j:j + 1]
                                     ).then_inc(sem("ssq"), 1)

            def hidden_turned(c, j):
                need(act, "hqT_ps", c, j + 1)
                need(act, "y", c, j)
                nc.scalar.copy(flat(hqT[:, :, :]), Y3b).then_inc(sem("hqT"), 1)

            def z_turned(c):
                need(act, "zT", c, 1)
                need(act, "hq", c, CT - 1)
                nc.scalar.copy(flat(xTf[:, :, :]), flat(Y[:, 1:3, :])).then_inc(sem("xTf"), 1)
                need(act, "xTf", c, 1)
                nc.scalar.copy(flat(xT_hi[:, :, :]), flat(xTf[:, :, :])).then_inc(sem("x_hi"), 1)

            def step(c, e, g):
                if c is not None:
                    a_high(c, 0)
                    a_high(c, 1)
                    a_high(c, 2)
                    a_high(c, 3)
                if e is not None:
                    x_turned(e)
                if c is not None:
                    silu(c, 0)
                for s in range(1, FT):
                    if e is not None and s <= 4:
                        hidden(e, s - 1)
                    if c is not None:
                        silu(c, 2 * s - 1)
                    if e is not None and 2 <= s <= 5:
                        hidden_turned(e, s - 2)
                    if c is not None:
                        silu(c, 2 * s)
                        if s >= 2:
                            high(c, s - 2)
                if c is not None:
                    silu(c, 2 * FT - 1)
                    high(c, FT - 2)
                    high(c, FT - 1)
                if e is not None:
                    z_turned(e)
                    spread(e)

            run(act, step)

        @block.vector
        def _(dve):
            links = {}

            def link(ins, c, name="dve_pre", apart=False):
                links[name] = links.get(name, 0) % PER[name] + 1
                ins.then_inc(sem(name), 1)
                need(dve, name, c, links[name], apart=apart)

            def small(dst, c, op, *args, **kw):
                link(op(sm[:, dst, :], *args, **kw), c)

            def stats(rows, c, name):
                for j in range(CT):
                    last = nc.vector.bn_stats(st6[:, j, :], rows(j))
                link(last, c, apart=True)
                for j in range(CT):
                    last = nc.vector.bn_aggr(mv[:, j, :], st6[:, j, :])
                last.then_inc(sem(name), 1)
                need(dve, name, c, 1)

            def normed(rows, dst, c, name):
                for j in range(CT):
                    last = nc.vector.tensor_scalar(dst(j), rows(j), mv[:, j, 0:1], sm[:, 0, j:j + 1], ALU.subtract, ALU.mult)
                last.then_inc(sem(name), 1)

            def gate(c, o):
                f, slot = ORDER[o]
                need(dve, "silu", c, o + 1)
                need(dve, "weighted", c, o - 1)
                nc.vector.tensor_tensor(gated[:, o % 2, :], sil[:, o % 2, :], X[:, 2 * (f % 2) + 1, :], ALU.mult
                                        ).then_inc(sem("gated"), 1)

            def low(c, f):
                need(dve, "g1_hi", c, f + 1)
                nc.vector.tensor_tensor(g1_lo[:, f, :], w1[:, f % 2, :], g1_hi[:, f, :], ALU.subtract).then_inc(sem("g1_lo"), 1)
                need(dve, "gc_hi", c, f + 1)
                nc.vector.tensor_tensor(gc_lo[:, f, :], wc[:, f % 2, :], gc_hi[:, f, :], ALU.subtract).then_inc(sem("gc_lo"), 1)

            def masked_slot(c, q, slot):
                for b, part in enumerate((a_hi, a_lo)):
                    last = nc.vector.tensor_tensor(am[:, q, slot, b, :], part[:, q, :], mask[:, 2 * slot + q % 2, :], ALU.mult)
                last.then_inc(sem("a_masked"), 1)

            def masked(c):
                need(dve, "fd", c, 0)
                need(dve, "a_masked", c, 0)
                for q in range(2):
                    a_low(c, q)
                for q in range(4):
                    if q >= 2:
                        a_low(c, q)
                    need(dve, "a_lo", c, q + 1)
                    need(dve, "spread", c, 4)
                    masked_slot(c, q, 0)
                for q in range(4):
                    masked_slot(c, q, 1)

            def a_low(c, q):
                need(dve, "a_hi", c, q + 1)
                nc.vector.tensor_tensor(a_lo[:, q, :], X[:, q, :], a_hi[:, q, :], ALU.subtract).then_inc(sem("a_lo"), 1)

            def back_masked(c, k):
                for w in range(2):
                    q = 2 * k + w
                    need(dve, "p_ps", c, q + 1)
                    if w == 0:
                        need(dve, "m_lo", c, k)
                    nc.vector.tensor_tensor(pm[w], X[:, BANKS[q], :], mask[:, 2 * w + k, :], ALU.mult
                                            ).then_inc(sem("p_read"), 1)

            def back_parts(c, k):
                need(dve, "p_read", c, 2 * k + 2)
                link(nc.vector.tensor_tensor(pm[2], pm[0], pm[1], ALU.add), c, "dve_main")
                need(dve, "down", c, 0)
                nc.vector.tensor_copy(m_hi[:, k, :], pm[2]).then_inc(sem("m_hi"), 1)
                need(dve, "m_hi", c, k + 1)
                nc.vector.tensor_tensor(m_lo[:, k, :], pm[2], m_hi[:, k, :], ALU.subtract).then_inc(sem("m_lo"), 1)

            def store(c, j):
                need(dve, "down", c, j + 1)
                nc.vector.scalar_tensor_tensor(out=out_sb[:, j, :], in0=X[:, BANKS[j], 0:D], scalar=t["tanh"][:, 3:4],
                                               in1=xrow(c, j), op0=ALU.mult, op1=ALU.add).then_inc(sem("out_sb"), 1)

            V = nc.vector

            def centered(c):
                need(dve, "zT", c, 0)
                stats(lambda j: xrow(c, j), c, "mv1")
                for j in range(CT):
                    last = V.tensor_scalar(d4[:, j, :], xrow(c, j), mv[:, j, 0:1], None, ALU.subtract)
                link(last, c)
                small(3, c, V.tensor_reduce, d4[:, :, :], AX.X, ALU.max, apply_absolute_value=True)

            def rounded(c):
                need(dve, "pow1", c, 1)
                small(4, c, V.tensor_tensor, sm[:, 2, :], sm[:, 0, :], ALU.mult)
                small(4, c, V.tensor_scalar, sm[:, 4, :], float(D) ** 0.5, 1e-12, ALU.mult, ALU.max)
                small(5, c, V.reciprocal, sm[:, 4, :])
                small(4, c, V.tensor_tensor, sm[:, 0, :], sm[:, 5, :], ALU.mult)
                small(4, c, V.tensor_scalar, sm[:, 4, :], float(D) ** 0.5, None, ALU.mult)
                small(5, c, V.tensor_tensor, sm[:, 4, :], sm[:, 3, :], ALU.mult)
                small(5, c, V.tensor_scalar, sm[:, 5, :], EPS, 1.0 / 127.0, ALU.max, ALU.mult)
                small(6, c, V.reciprocal, sm[:, 5, :])
                small(7, c, V.tensor_tensor, sm[:, 4, :], sm[:, 6, :], ALU.mult)
                need(dve, "gelu", c, 0)
                small(10, c, V.tensor_scalar, sm[:, 5, :], t["mean1"][:, :], None, ALU.mult)
                for j in range(CT):
                    last = V.tensor_scalar(d4[:, j, :], d4[:, j, :], sm[:, 7, j:j + 1], ROUND, ALU.mult, ALU.add)
                last.then_inc(sem("q_in"), 1)

            def hidden_scaled(c, j):
                if j == 0:
                    need(dve, "norm2", c, 0)
                need(dve, "gelu", c, j + 1)
                link(V.tensor_reduce(sm[:, 13, j:j + 1], h[:, j % 2, :], AX.X, ALU.max, apply_absolute_value=True), c)
                link(V.tensor_scalar(sm[:, 14, j:j + 1], sm[:, 13, j:j + 1], TINY, 1.0 / 127.0, ALU.max, ALU.mult), c)
                link(V.reciprocal(sm[:, 15, j:j + 1], sm[:, 14, j:j + 1]), c)
                need(dve, "ssq", c, j + 1)
                V.tensor_scalar(h[:, j % 2, :], h[:, j % 2, :], sm[:, 15, j:j + 1], ROUND, ALU.mult, ALU.add).then_inc(sem("hr"), 1)

            def y_out(c, j):
                need(dve, "y", c, j + 1)
                V.tensor_copy(y2[:, j, :], Y[:, 0, 0:D]).then_inc(sem("y2"), 1)

            def first_factors(c):
                need(dve, "norm2", c, 1)
                small(4, c, V.tensor_scalar, sm[:, 9, :], 1e-12, None, ALU.max)
                small(5, c, V.reciprocal, sm[:, 4, :])
                small(4, c, V.tensor_tensor, sm[:, 13, :], sm[:, 5, :], ALU.mult)
                small(4, c, V.tensor_scalar, sm[:, 4, :], float(F1) ** 0.5, EPS, ALU.mult, ALU.max)
                small(4, c, V.tensor_scalar, sm[:, 4, :], 1.0 / 127.0, None, ALU.mult)
                small(4, c, V.tensor_scalar, sm[:, 4, :], t["mean2"][:, :], t["tanh"][:, 2:3], ALU.mult, ALU.mult)

            def add_first(c):
                need(dve, "y2", c, 4)
                for j in range(CT):
                    last = V.scalar_tensor_tensor(out=xrow(c, j), in0=y2[:, j, :], scalar=sm[:, 4, j:j + 1],
                                                  in1=xrow(c, j), op0=ALU.mult, op1=ALU.add)
                link(last, c, apart=True)
                stats(lambda j: xrow(c, j), c, "mv2")

            def minus_mean(c):
                for j in range(CT):
                    last = V.tensor_scalar(y4[:, j, :], xrow(c, j), mv[:, j, 0:1], None, ALU.subtract)
                last.then_inc(sem("xm"), 1)

            def plus_summary(c):
                need(dve, "rstd2", c, 1)
                need(dve, "xm", c, 1)
                need(dve, "summ_in", c, 16 * CT)
                for j in range(CT):
                    last = V.scalar_tensor_tensor(out=y4[:, j, :], in0=y4[:, j, :], scalar=sm[:, 0, j:j + 1],
                                                  in1=summ[:, j, :], op0=ALU.mult, op1=ALU.add)
                last.then_inc(sem("ys"), 1)
                need(dve, "ys", c, 1, apart=True)
                stats(lambda j: y4[:, j, :], c, "mv3")

            def add_block(c):
                for j in range(CT):
                    last = V.scalar_tensor_tensor(out=y4[:, j, :], in0=y4[:, j, :], scalar=mv[:, j, 0:1],
                                                  in1=t["gamma"][:, :], op0=ALU.subtract, op1=ALU.mult)
                link(last, c)
                need(dve, "rstd3", c, 1)
                need(dve, "xb", c, 1)
                for j in range(CT):
                    last = V.scalar_tensor_tensor(out=xrow(c, j), in0=y4[:, j, :], scalar=sm[:, 0, j:j + 1],
                                                  in1=xrow(c, j), op0=ALU.mult, op1=ALU.add)
                last.then_inc(sem("x3"), 1)
                need(dve, "x3", c, 1, apart=True)
                stats(lambda j: xrow(c, j), c, "mv4")

            def last_norm(c):
                need(dve, "rstd4", c, 1)
                normed(lambda j: xrow(c, j), lambda j: y4[:, j, :], c, "z")

            def x_low(c):
                need(dve, "x_hi", c, 1)
                V.tensor_tensor(flat(xT_lo[:, :, :]), flat(xTf[:, :, :]), flat(xT_hi[:, :, :]), ALU.subtract
                                ).then_inc(sem("x_lo"), 1)

            def top_two(c):
                need(dve, "logits_ps", c, 1)
                V.tensor_copy(flat(logits[:, :, :]), Y[:, 0, 0:CT * E]).then_inc(sem("logits"), 1)
                need(dve, "logits", c, 1, apart=True)
                for j in range(CT):
                    last = V.max(top[:, j, :], logits[:, j, :])
                link(last, c, apart=True)
                for j in range(CT):
                    last = V.max_index(top_i[:, j, :], top[:, j, :], logits[:, j, :])
                link(last, c)
                need(dve, "exp_gap", c, 0)
                V.tensor_tensor(sm[:, 11, :], top[:, :, 1], top[:, :, 0], ALU.subtract).then_inc(sem("gap"), 1)
                link(V.tensor_copy(top_f[:, :, :], top_i[:, :, 0:2]), c)
                need(dve, "gT_ps", c, 0)
                link(V.tensor_tensor(gpack[:, :, 0:8], experts[:, :, :], top_f[:, :, 0:1].to_broadcast([P, CT, E]),
                                     ALU.is_equal), c)
                link(V.tensor_tensor(onehot[:, :, :], experts[:, :, :], top_f[:, :, 1:2].to_broadcast([P, CT, E]),
                                     ALU.is_equal), c)
                link(V.tensor_tensor(gpack[:, :, 8:16], onehot[:, :, :], gpack[:, :, 0:8], ALU.subtract), c)
                need(dve, "exp_gap", c, 1)
                small(4, c, V.tensor_scalar, sm[:, 12, :], 1.0, None, ALU.add)
                link(V.reciprocal(rw[:, :, 0], sm[:, 4, :]), c)
                link(V.tensor_tensor(rw[:, :, 1], sm[:, 12, :], rw[:, :, 0], ALU.mult), c)
                part = gpack[:, :, 16:22].rearrange("p a (s i) -> p i a s", i=3)
                link(V.tensor_copy(part[:, 0], rw[:, :, :]), c)
                link(V.tensor_tensor(rw_rest[:, :, :], rw[:, :, :], part[:, 0], ALU.subtract), c)
                link(V.tensor_copy(part[:, 1], rw_rest[:, :, :]), c)
                V.tensor_tensor(part[:, 2], rw_rest[:, :, :], part[:, 1], ALU.subtract).then_inc(sem("routing"), 1)

            def routing_turned(c):
                need(dve, "gT_ps", c, 1)
                V.tensor_copy(gT[:, :], Y0b[0:32, 0:N]).then_inc(sem("gT"), 1)

            def begin(c):
                centered(c)
                rounded(c)

            def step(c, e, g):
                if c is not None:
                    masked(c)
                    gate(c, 0)
                for s in range(1, FT):
                    if e is not None and s <= 4:
                        hidden_scaled(e, s - 1)
                    if e is not None and s == FT - 1:
                        y_out(e, CT - 1)
                        first_factors(e)
                        add_first(e)
                    if c is not None:
                        gate(c, 2 * s - 1)
                    if e is not None and 3 <= s <= 5:
                        y_out(e, s - 3)
                    if e is not None and s == FT - 1:
                        minus_mean(e)
                    if c is not None:
                        gate(c, 2 * s)
                        if 2 <= s < FT - 1:
                            low(c, s - 2)
                if e is not None:
                    plus_summary(e)
                if c is not None:
                    gate(c, 2 * FT - 1)
                    low(c, FT - 3)
                    low(c, FT - 2)
                    low(c, FT - 1)
                if e is not None:
                    add_block(e)
                if c is not None:
                    back_masked(c, 0)
                if e is not None:
                    last_norm(e)
                if c is not None:
                    back_parts(c, 0)
                if e is not None:
                    x_low(e)
                    top_two(e)
                if c is not None:
                    back_masked(c, 1)
                    back_parts(c, 1)
                if e is not None:
                    routing_turned(e)
                if g is not None:
                    centered(g)
                if c is not None:
                    for j in range(CT):
                        store(c, j)
                if g is not None:
                    rounded(g)

            run(dve, step, begin)
            assert all(links[n] == PER[n] for n in links), links

        @block.tensor
        def _(pe):
            pe.wait_ge(sem("consts"), 10)
            mm = nc.tensor.matmul
            PARTS = ((0, 0), (1, 0), (0, 1))

            def products(out, pairs, start, stop):
                n = len(pairs) * 3
                for i, (lhs, rhs) in enumerate(pairs):
                    for k, (a, b) in enumerate(PARTS):
                        last = mm(out, lhs[a], rhs[b], start=start and i == k == 0, stop=stop and 3 * i + k == n - 1,
                                  skip_group_check=True)
                return last

            def lora(w, k, f, slot, out, stop):
                q = 2 * w + k
                wt = ("B1", "B3")[w]
                fs = slice(f * P, (f + 1) * P)
                return products(out, [((t[wt + "_hi"][:, k, fs], t[wt + "_lo"][:, k, fs]),
                                       (am[:, q, slot, 0, :], am[:, q, slot, 1, :]))], False, stop)

            def first(c, f):
                if f < 2:
                    need(pe, "a_lo", c, 2 * f + 2)
                    need(pe, "p_read", c, 0)
                else:
                    need(pe, "gated", c, AT[f - 2, 1] + 1)
                for w, wt in enumerate(("W1", "W3")):
                    out = X[:, 2 * (f % 2) + w, :]
                    fs = slice(f * P, (f + 1) * P)
                    products(out, [((t[wt + "_hi"][:, k, fs], t[wt + "_lo"][:, k, fs]),
                                    (xT_hi[:, k, :], xT_lo[:, k, :])) for k in range(2)], True, False)
                for w in range(2):
                    out = X[:, 2 * (f % 2) + w, :]
                    for k in range(2):
                        if f == 0:
                            need(pe, "a_masked", c, 2 * w + k + 1)
                        last = lora(w, k, f, 0, out, k == 1)
                last.then_inc(sem("f0"), 1)

            def second(c, f):
                if f == 0:
                    need(pe, "a_masked", c, 8)
                need(pe, "gated", c, AT[f, 0] + 1)
                for w in range(2):
                    for k in range(2):
                        last = lora(w, k, f, 1, X[:, 2 * (f % 2) + w, :], k == 1)
                last.then_inc(sem("fd"), 1)

            def down(c, j):
                need(pe, "p_read", c, j + 1)
                js = slice(j * P, (j + 1) * P)
                products(X[:, BANKS[j], 0:D], [((gc_hi[:, f, js], gc_lo[:, f, js]),
                                                (t["W2_hi"][:, f, :], t["W2_lo"][:, f, :])) for f in range(FT)],
                         True, False)

            def down_lora(c, j):
                need(pe, "m_lo", c, 2)
                js = slice(j * P, (j + 1) * P)
                products(X[:, BANKS[j], 0:D], [((m_hi[:, k, js], m_lo[:, k, js]),
                                                (t["B2_hi"][:, k, :], t["B2_lo"][:, k, :])) for k in range(2)],
                         False, True).then_inc(sem("down"), 1)

            def a_products(c):
                need(pe, "x_lo", c, 1)
                need(pe, "x_hi", c, 1)
                for q in range(4):
                    need(pe, "out_sb", c, -1 if q == 0 else 0)
                    wt, es = ("A1", "A3")[q // 2], slice(q % 2 * P, (q % 2 + 1) * P)
                    products(X[:, q, :], [((t[wt + "_hi"][:, k, es], t[wt + "_lo"][:, k, es]),
                                           (xT_hi[:, k, :], xT_lo[:, k, :])) for k in range(2)], True, True
                             ).then_inc(sem("a_ps"), 1)

            def back(c, q, fs):
                if q < 2:
                    need(pe, "gated", c, AT[FT - 2, 1] + 1)
                else:
                    need(pe, "gated", c, 2 * FT)
                es = slice(q // 2 * P, (q // 2 + 1) * P)
                hi, lo = (g1_hi, g1_lo) if q % 2 else (gc_hi, gc_lo)
                for f in fs:
                    if q < 2:
                        need(pe, "g1_lo" if q % 2 else "gc_lo", c, f + 1)
                    last = products(X[:, BANKS[q], :], [((t["A2_hi"][:, f, es], t["A2_lo"][:, f, es]),
                                                         (hi[:, f, :], lo[:, f, :]))], f == 0, f == FT - 1)
                if f == FT - 1:
                    last.then_inc(sem("p_ps"), 1)

            def up(c, j):
                if j == 0:
                    need(pe, "xqT", c, 1)
                    need(pe, "xTf", c, 0)
                    need(pe, "spread", c, 0)
                need(pe, "gelu", c, j)
                for n in range(2):
                    for k in range(2):
                        last = mm(Y[:, 1 + n, :], xqT[:, k, j * P:(j + 1) * P], t["w1T"][:, k, n * 512:(n + 1) * 512],
                                  start=(k == 0), stop=(k == 1))
                last.then_inc(sem("hp"), 1)

            def turn_hidden(c, j):
                need(pe, "hq", c, j + 1)
                need(pe, "hqT", c, j)
                if j == 0:
                    need(pe, "spread", c, 0)
                for n in range(8):
                    last = nc.tensor.transpose(Y3b[:, n * P:(n + 1) * P], hq[:, j % 2, n * P:(n + 1) * P], identb[:, :])
                last.then_inc(sem("hqT_ps"), 1)

            def second_product(c, j):
                need(pe, "hqT", c, j + 1)
                need(pe, "xqT" if j == 0 else "y2", c, max(j, 1))
                for n in range(8):
                    last = mm(Y[:, 0, 0:D], hqT[:, n, :], t["w2T"][:, n, :], start=(n == 0), stop=(n == 7))
                last.then_inc(sem("y"), 1)

            def turn_xq(c):
                need(pe, "xq", c, 1)
                need(pe, "gT", c, 0)
                for k in range(2):
                    for j in range(CT):
                        last = nc.tensor.transpose(Y0b[:, (k * CT + j) * P:(k * CT + j + 1) * P],
                                                   xq[:, j, k * P:(k + 1) * P], identb[:, :])
                last.then_inc(sem("xqT_ps"), 1)

            def turn_z(c):
                need(pe, "z", c, 1)
                need(pe, "gelu", c, 4)
                for k in range(2):
                    for j in range(CT):
                        last = nc.tensor.transpose(Y[:, 1 + k, j * P:(j + 1) * P], y4[:, j, k * P:(k + 1) * P], ident[:, :])
                last.then_inc(sem("zT"), 1)

            def route(c):
                need(pe, "xTf", c, 1)
                need(pe, "y2", c, 4)
                for j in range(CT):
                    for k in range(2):
                        last = mm(Y[:, 0, j * E:(j + 1) * E], xTf[:, k, j * P:(j + 1) * P], t["WgT"][:, k, :],
                                  start=(k == 0), stop=(k == 1), skip_group_check=True)
                last.then_inc(sem("logits_ps"), 1)

            def turn_routing(c):
                need(pe, "routing", c, 1)
                need(pe, "logits", c, 1)
                for j in range(CT):
                    last = nc.tensor.transpose(Y0b[0:32, j * P:(j + 1) * P], gpack[:, j, :], identb[:, :])
                last.then_inc(sem("gT_ps"), 1)

            def spread(c, vs):
                need(pe, "gT", c, 1)
                need(pe, "hqT", c, 4)
                need(pe, "xTf", c, 1)
                for v in vs:
                    if v >= 2:
                        need(pe, "spread", c, v - 1)
                    mm(Y[:, 2 + v % 2, :], sel[:, v, :], gT[:, :], start=True, stop=True).then_inc(sem("spread_ps"), 1)

            def step(c, e, g):
                if c is not None:
                    a_products(c)
                if e is not None:
                    turn_xq(e)
                if c is not None:
                    first(c, 0)
                if e is not None:
                    up(e, 0)
                for s in range(1, FT):
                    if c is not None:
                        first(c, s)
                    if e is not None and 2 <= s <= 5:
                        turn_hidden(e, s - 2)
                    if c is not None:
                        second(c, s - 1)
                    if e is not None and s <= 3:
                        up(e, s)
                    if e is not None and 2 <= s <= 5:
                        second_product(e, s - 2)
                if c is not None:
                    second(c, FT - 1)
                    back(c, 0, range(FT - 1))
                    back(c, 1, range(FT - 1))
                    back(c, 0, (FT - 1,))
                    back(c, 1, (FT - 1,))
                    back(c, 2, range(FT))
                    back(c, 3, range(4))
                if e is not None:
                    turn_z(e)
                if c is not None:
                    back(c, 3, range(4, FT))
                if e is not None:
                    route(e)
                if c is not None:
                    for j in range(3):
                        down(c, j)
                if e is not None:
                    turn_routing(e)
                if c is not None:
                    down(c, 3)
                for k in range(3):
                    if e is not None:
                        spread(e, (2 * k, 2 * k + 1))
                    if c is not None:
                        for j in ((0, 1), (2,), (3,))[k]:
                            down_lora(c, j)

            run(pe, step)


def program(nc, a, out):
    with ExitStack() as ctx:
        def sb(name, shape, dt=F32):
            return ctx.enter_context(nc.sbuf_tensor(name, shape, dt))

        t = {"passed": ctx.enter_context(nc.semaphore("passed"))}
        t |= {"x": sb("x", [P, TILES, D]), "ident": sb("ident", [P, P]), "identb": sb("identb", [P, P], BF16)}
        t |= {"g": sb("g", [P, 8]), "tanh": sb("tanh", [P, 4]), "gain0": sb("gain0", [P, 1]), "expd": sb("expd", [P, 1])}
        t |= {"mean1": sb("mean1", [P, 1]), "mean2": sb("mean2", [P, 1])}
        t |= {"gamma": sb("gamma", [P, D]), "beta": sb("beta", [P, D]), "WgT": sb("WgT", [P, 2, E])}
        shapes = [(n + part, dims) for n, dims in (
            ("W1", (2, F)), ("W3", (2, F)), ("B1", (2, F)), ("B3", (2, F)), ("A1", (2, ER)), ("A3", (2, ER)),
            ("B2", (2, D)), ("W2", (FT, D)), ("A2", (FT, ER))) for part in ("_hi", "_lo")]
        shapes += [("w1T", (2, F1)), ("w2T", (F1 // P, D))]
        t["area"] = sb("area", [P, sum(a * b for _, (a, b) in shapes)], BF16)
        start = 0
        for n, (a_, b_) in shapes:
            t[n] = t["area"][:, start:start + a_ * b_].rearrange("p (a b) -> p a b", b=b_)
            start += a_ * b_

        def tiles_of(ap):
            return ap.rearrange("(n b) s d -> (b s) n d", b=2)

        def rows(ap):
            return ap.rearrange("(n p) d -> p n d", p=P)

        def column(ap, n):
            return ap.unsqueeze(0).to_broadcast([P, n])

        t["x_dram"], t["ctx_dram"], t["out_dram"] = tiles_of(a["x"]), tiles_of(a["ctx_2048"]), tiles_of(out)
        t["g_xattn_dram"], t["g_ffn_dram"] = column(a["g_xattn"], 2), column(a["g_ffn"], 2)
        t["gamma0_dram"] = column(a["L0_xattn_gamma"], 1)
        t["decay_dram"] = column(a["L1_xattn_decay"], 1)
        t["w1_dram"], t["w2_dram"] = rows(a["L0_ffn_w1"]), rows(a["L0_ffn_w2"])
        for n in ("W1", "W3", "W2"):
            t[n + "_dram"] = rows(a["L1_ffn_" + n])
        for n in ("A1", "A3", "A2"):
            t[n + "_dram"] = a["L1_ffn_" + n].rearrange("e r h -> (e r) h").rearrange("(n p) h -> p n h", p=P)
        for n in ("B1", "B3", "B2"):
            b = a["L1_ffn_" + n].rearrange("e (n p) r -> n p e r", p=P)
            t[n + "_dram"] = [b[i] for i in range(2 if n == "B2" else FT)]
        t["Win_dram"], t["Wout_dram"] = rows(a["L1_xattn_W_in"]), rows(a["L1_xattn_W_out"])
        t["b_in_dram"] = a["L1_xattn_b_in"].rearrange("(n p) -> p n", p=P)
        t["b_out_dram"] = a["L1_xattn_b_out"].unsqueeze(0)
        t["Wg_dram"] = a["L1_ffn_Wg"]
        t["gamma_dram"], t["beta_dram"] = column(a["L1_xattn_gamma"], D), column(a["L1_xattn_beta"], D)
        t["summ_dram"] = nc.dram_tensor("summaries", (NB, D), F32, kind="Internal").ap()
        t["q_parts_dram"] = nc.dram_tensor("q_parts_scratch", (2, 3, DH, 2 * HEADS, D), BF16, kind="Internal").ap()
        t["k_parts_dram"] = nc.dram_tensor("k_parts_scratch", (2, 5, DH, 2 * HEADS, D), BF16, kind="Internal").ap()
        t["pv_dram"] = nc.dram_tensor("pv_scratch", (2, 2, 2, P, D), F32, kind="Internal").ap()

        def k_windows(u, h):
            rows = t["k_parts_dram"][u, :, :, h * 8:h * 8 + 8, :].rearrange("a d h l -> (a d) (h l)")
            return bass.AP(rows.tensor, rows.offset, [[8 * 2 * HEADS * D, 3], [2 * HEADS * D, 24], [1, HEADS * D]])

        t["k_windows"] = k_windows
        with ExitStack() as early:
            t["ctx"] = early.enter_context(nc.sbuf_tensor("ctx", [P, TILES, D], F32))
            nat_shapes = {n: [P, FT, D] for n in ("W1", "W3", "B1", "B3")} | {n: [P, 2, D] for n in ("A1", "A3", "B2")}
            nat_shapes |= {"W2": [P, 2, F], "A2": [P, 2, F], "w1": [P, F1 // P, D], "w2": [P, 2, F1]}
            t["nat"] = {n: early.enter_context(nc.sbuf_tensor(f"nat_{n}", shape, F32)) for n, shape in nat_shapes.items()}
            attention(nc, t)
            turned = {n: early.enter_context(nc.sbuf_tensor(n + "T", [P, 2, D], F32)) for n in ("Win", "Wout")}
            prepare(nc, t, turned)
        tokens(nc, t)


_INS = ["x", "ctx_2048", "g_xattn", "g_ffn", "L0_xattn_gamma", "L0_ffn_w1", "L0_ffn_w2", "L1_xattn_decay",
        "L1_xattn_W_in", "L1_xattn_b_in", "L1_xattn_W_out", "L1_xattn_b_out", "L1_xattn_gamma", "L1_xattn_beta",
        "L1_ffn_Wg", "L1_ffn_W1", "L1_ffn_W2", "L1_ffn_W3", "L1_ffn_A1", "L1_ffn_B1", "L1_ffn_A2", "L1_ffn_B2",
        "L1_ffn_A3", "L1_ffn_B3"]


def kernel(**inputs):
    import numpy as _np
    import concourse.bacc as _bacc
    from concourse import mybir as _mybir
    from concourse.bass_utils import run_bass_kernel_spmd as _run

    nc = _bacc.Bacc("TRN2", target_bir_lowering=False, num_devices=1)
    arrays, args = {}, {}
    for name in _INS:
        a = _np.ascontiguousarray(inputs[name])
        if a.ndim == 0:
            a = a.reshape(1)
        arrays[f"in_{name}_dram"] = a
        args[name] = nc.dram_tensor(f"in_{name}_dram", a.shape, _mybir.dt.from_np(a.dtype), kind="ExternalInput").ap()
    out = nc.dram_tensor("out_dram", (NB, S, D), F32, kind="ExternalOutput").ap()
    program(nc, args, out)
    r = _run(nc, [arrays], core_ids=[0])
    return r.results[0]["out_dram"]
```
